# Optimizing a Trainium2 kernel written in Bass

```python
import numpy as np
import jax
import jax.numpy as jnp

def _softmax(x, axis=-1):
    return jax.nn.softmax(x, axis=axis)
def _gelu(x):
    return jax.nn.gelu(x, approximate=True)
def _silu(x):
    return jax.nn.silu(x)
def _sigmoid(x):
    return jax.nn.sigmoid(x)
def _layernorm(x, axis=-1, eps=1e-5):
    m = jnp.mean(x, axis=axis, keepdims=True)
    v = jnp.var(x, axis=axis, keepdims=True)
    return (x - m) / jnp.sqrt(v + eps)
def _scatter_add(tgt, idx, src, axis=0):
    return tgt.at[idx].add(src)
def _segment_sum(src, seg, n):
    return jax.ops.segment_sum(src, seg, n)

kernel_name = 'mk_conv_preact_d2_conv_nchw128_19a682'

def setup_inputs(seed: int = 0):
    np.random.seed(seed)
    _w = jnp.asarray
    def _rec_inputs():
        import jax
        import jax.numpy as jnp
        _gk = jax.random.key(seed)
        x = -0.0002928 + 1 * jax.random.normal(jax.random.fold_in(_gk, 1), (8, 128, 64, 64), jnp.float32)
        return x
    x = _rec_inputs()
    def _L0_conv_setup():
        import jax, jax.numpy as jnp
        import numpy as np
        K = 3
        STRIDE = 1
        DIL = 2
        PAD = 2
        DG = 2

        def _grouped_conv(x, w, b, groups):
            out = jax.lax.conv_general_dilated(x, w, window_strides=(STRIDE, STRIDE), padding=[(PAD, PAD), (PAD, PAD)], rhs_dilation=(DIL, DIL), feature_group_count=groups, dimension_numbers=('NCHW', 'OIHW', 'NCHW'))
            return out + b[None, :, None, None]

        def _bilinear_gather(xg, py, px):
            B, G, Cg, H, W = xg.shape
            y0 = jnp.floor(py)
            x0 = jnp.floor(px)
            wy = py - y0
            wx = px - x0
            y0i = y0.astype(jnp.int32)
            x0i = x0.astype(jnp.int32)
            xf = xg.reshape(B, G, Cg, H * W)

            def corner(yi, xi, wgt):
                valid = (yi >= 0) & (yi < H) & (xi >= 0) & (xi < W)
                yc = jnp.clip(yi, 0, H - 1)
                xc = jnp.clip(xi, 0, W - 1)
                idx = (yc * W + xc).reshape(B, G, -1)
                g = jax.vmap(jax.vmap(lambda f, i: f[:, i]))(xf, idx)
                g = g.reshape(B, G, Cg, *py.shape[2:])
                return g * (wgt * valid)[:, :, None]
            return corner(y0i, x0i, (1 - wy) * (1 - wx)) + corner(y0i, x0i + 1, (1 - wy) * wx) + corner(y0i + 1, x0i, wy * (1 - wx)) + corner(y0i + 1, x0i + 1, wy * wx)
        key = jax.random.key(seed)
        k1, k2, k3, k4 = jax.random.split(key, 4)
        B, C, H, W, Co = (8, 128, 64, 64, 128)
        KK = K * K
        x = jax.random.normal(k1, (B, C, H, W), jnp.float32)
        offset_w = jax.random.normal(k2, (DG * 3 * KK, C // DG, K, K), jnp.float32) * 0.01
        offset_b = jax.random.normal(k3, (DG * 3 * KK,), jnp.float32) * 0.01
        weight = jax.random.normal(k4, (Co, C, K, K), jnp.float32) / np.sqrt(C * KK).astype(np.float32)
        return {'x': x, 'offset_w': offset_w, 'offset_b': offset_b, 'weight': weight}
    _L0_conv_all = _L0_conv_setup()
    _L0_conv_in = {k: v for k, v in _L0_conv_all.items() if k in ('offset_w', 'offset_b', 'weight', )}
    del _L0_conv_all

    def _L1_conv_setup():
        import jax, jax.numpy as jnp
        import numpy as np
        B, CIN, COUT, H, W = (8, 128, 128, 256, 256)
        HM0, HM1 = (32, 32)
        W_SCALE = 1.0 / (CIN * COUT)
        key = jax.random.key(seed)
        kx, k1r, k1i, k2r, k2i = jax.random.split(key, 5)
        x = jax.random.normal(kx, (B, CIN, H, W), dtype=jnp.float32)
        w1_real = jax.random.normal(k1r, (CIN, COUT, HM0, HM1), dtype=jnp.float32) * W_SCALE
        w1_imag = jax.random.normal(k1i, (CIN, COUT, HM0, HM1), dtype=jnp.float32) * W_SCALE
        w2_real = jax.random.normal(k2r, (CIN, COUT, HM0, HM1), dtype=jnp.float32) * W_SCALE
        w2_imag = jax.random.normal(k2i, (CIN, COUT, HM0, HM1), dtype=jnp.float32) * W_SCALE
        return {'x': x, 'w1_real': w1_real, 'w1_imag': w1_imag, 'w2_real': w2_real, 'w2_imag': w2_imag}
    _L1_conv_all = _L1_conv_setup()
    _L1_conv_in = {k: v for k, v in _L1_conv_all.items() if k in ('w1_real', 'w1_imag', 'w2_real', 'w2_imag', )}
    del _L1_conv_all

    return {
        "x": x,
        "L0_conv_offset_w": _L0_conv_in["offset_w"],
        "L0_conv_offset_b": _L0_conv_in["offset_b"],
        "L0_conv_weight": _L0_conv_in["weight"],
        "L1_conv_w1_real": _L1_conv_in["w1_real"],
        "L1_conv_w1_imag": _L1_conv_in["w1_imag"],
        "L1_conv_w2_real": _L1_conv_in["w2_real"],
        "L1_conv_w2_imag": _L1_conv_in["w2_imag"],
    }

def reference(x, L0_conv_offset_w, L0_conv_offset_b, L0_conv_weight, L1_conv_w1_real, L1_conv_w1_imag, L1_conv_w2_real, L1_conv_w2_imag):
    import jax
    import jax.numpy as jnp
    def _L0_conv_ref(x, offset_w, offset_b, weight):
        import jax, jax.numpy as jnp
        import numpy as np
        K = 3
        STRIDE = 1
        DIL = 2
        PAD = 2
        DG = 2

        def _grouped_conv(x, w, b, groups):
            out = jax.lax.conv_general_dilated(x, w, window_strides=(STRIDE, STRIDE), padding=[(PAD, PAD), (PAD, PAD)], rhs_dilation=(DIL, DIL), feature_group_count=groups, dimension_numbers=('NCHW', 'OIHW', 'NCHW'))
            return out + b[None, :, None, None]

        def _bilinear_gather(xg, py, px):
            B, G, Cg, H, W = xg.shape
            y0 = jnp.floor(py)
            x0 = jnp.floor(px)
            wy = py - y0
            wx = px - x0
            y0i = y0.astype(jnp.int32)
            x0i = x0.astype(jnp.int32)
            xf = xg.reshape(B, G, Cg, H * W)

            def corner(yi, xi, wgt):
                valid = (yi >= 0) & (yi < H) & (xi >= 0) & (xi < W)
                yc = jnp.clip(yi, 0, H - 1)
                xc = jnp.clip(xi, 0, W - 1)
                idx = (yc * W + xc).reshape(B, G, -1)
                g = jax.vmap(jax.vmap(lambda f, i: f[:, i]))(xf, idx)
                g = g.reshape(B, G, Cg, *py.shape[2:])
                return g * (wgt * valid)[:, :, None]
            return corner(y0i, x0i, (1 - wy) * (1 - wx)) + corner(y0i, x0i + 1, (1 - wy) * wx) + corner(y0i + 1, x0i, wy * (1 - wx)) + corner(y0i + 1, x0i + 1, wy * wx)
        B, C, H, W = x.shape
        Co = weight.shape[0]
        KK = K * K
        om = _grouped_conv(x, offset_w, offset_b, DG)
        Ho, Wo = (om.shape[2], om.shape[3])
        off = om[:, :DG * 2 * KK].reshape(B, DG, KK, 2, Ho, Wo)
        mask = jax.nn.sigmoid(om[:, DG * 2 * KK:]).reshape(B, DG, KK, Ho, Wo) * 2.0
        ky, kx = jnp.meshgrid(jnp.arange(K), jnp.arange(K), indexing='ij')
        grid_y = (jnp.arange(Ho) * STRIDE - PAD).astype(x.dtype)
        grid_x = (jnp.arange(Wo) * STRIDE - PAD).astype(x.dtype)
        py = off[:, :, :, 0] + (ky.reshape(KK, 1, 1) * DIL + grid_y[None, :, None])
        px = off[:, :, :, 1] + (kx.reshape(KK, 1, 1) * DIL + grid_x[None, None, :])
        Cg = C // DG
        xg = x.reshape(B, DG, Cg, H, W)
        val = _bilinear_gather(xg, py, px) * mask[:, :, None]
        w = weight.reshape(Co, DG, Cg, KK)
        out = jnp.einsum('bgckhw,ogck->bohw', val, w)
        return out

    def _L1_conv_ref(x, w1_real, w1_imag, w2_real, w2_imag):
        import jax, jax.numpy as jnp
        import numpy as np
        B, CIN, COUT, H, W = (8, 128, 128, 256, 256)
        HM0, HM1 = (32, 32)
        W_SCALE = 1.0 / (CIN * COUT)
        """2D FactorizedSpectralConv forward (dense weights, separable=False, no bias).

            rfft2 (norm='forward') -> contract two low-frequency corners with complex
            weights via einsum 'bixy,ioxy->boxy' -> zero-fill remaining modes -> irfft2.
            """
        b, cin, h, w = x.shape
        cout = w1_real.shape[1]
        hm0, hm1 = (w1_real.shape[2], w1_real.shape[3])
        xf = jnp.fft.rfft2(x, norm='forward')
        w1 = jax.lax.complex(w1_real, w1_imag)
        w2 = jax.lax.complex(w2_real, w2_imag)
        top = jnp.einsum('bixy,ioxy->boxy', xf[:, :, :hm0, :hm1], w1)
        bot = jnp.einsum('bixy,ioxy->boxy', xf[:, :, -hm0:, :hm1], w2)
        out_fft = jnp.zeros((b, cout, h, w // 2 + 1), dtype=xf.dtype)
        out_fft = out_fft.at[:, :, :hm0, :hm1].set(top)
        out_fft = out_fft.at[:, :, -hm0:, :hm1].set(bot)
        return jnp.fft.irfft2(out_fft, s=(h, w), norm='forward')

    def _gn(v, G=32, eps=1e-5):
        B_, C_, H_, W_ = v.shape
        g = v.reshape(B_, G, C_ // G, H_, W_)
        m = jnp.mean(g, axis=(2, 3, 4), keepdims=True)
        s = jnp.var(g, axis=(2, 3, 4), keepdims=True)
        return ((g - m) / jnp.sqrt(s + eps)).reshape(v.shape)

    def _ln_c(v, eps=1e-6):
        m = jnp.mean(v, axis=1, keepdims=True)
        s = jnp.var(v, axis=1, keepdims=True)
        return (v - m) / jnp.sqrt(s + eps)

    def _ln_t(v, eps=1e-5):
        m = jnp.mean(v, axis=-1, keepdims=True)
        s = jnp.var(v, axis=-1, keepdims=True)
        return (v - m) / jnp.sqrt(s + eps)

    def _to_tokens(v):
        B_, C_, H_, W_ = v.shape
        return v.reshape(B_, C_, H_ * W_).transpose(0, 2, 1)
    def _from_tokens(t, like):
        B_, C_, H_, W_ = like.shape
        return t.transpose(0, 2, 1).reshape(B_, C_, H_, W_)

    x = x + _L0_conv_ref(_gn(x), L0_conv_offset_w, L0_conv_offset_b, L0_conv_weight)
    x = x + _L1_conv_ref(_gn(x), L1_conv_w1_real, L1_conv_w1_imag, L1_conv_w2_real, L1_conv_w2_imag)
    return x


_drawn_inputs = setup_inputs


def setup_inputs(seed=0):
    import zlib

    import numpy as np

    out = dict(_drawn_inputs(seed))
    spreads = {}
    factors = {'L0_conv_offset_b': 4.642,
     'L1_conv_w1_real': 64.0,
     'L1_conv_w1_imag': 64.0,
     'L1_conv_w2_real': 64.0,
     'L1_conv_w2_imag': 64.0}
    for name, (base, spread) in spreads.items():
        noise = np.random.default_rng([zlib.crc32(name.encode()), seed]).standard_normal(out[name].shape)
        drawn = base * np.exp(spread * noise) if base else spread * noise
        out[name] = jnp.asarray(drawn.astype(out[name].dtype))
    for name, factor in factors.items():
        out[name] = (out[name] * factor).astype(out[name].dtype)
    return out
```

```python
import concourse.bass as bass
from concourse import mybir
import numpy as np
from contextlib import ExitStack

F32, F16, I32 = mybir.dt.float32, mybir.dt.float16, mybir.dt.int32
ALU = mybir.AluOpType
ACT = mybir.ActivationFunctionType
AX = mybir.AxisListType

C, H, W = 128, 64, 64
PIX = H * W
TAPS = 9
DG = 2
CG = C // DG
OMC = DG * 3 * TAPS
NMASK = DG * TAPS
REACH = 2.0
TR = 4
TILES = (H + 4) // TR
BANDS = H // TR
PR = TR + 4
PC = 16
SW = W + 4
TW = TR * W
COLTILES = [(0, 16, 0), (16, 12, 12), (28, 12, 24), (40, 12, 36), (52, 16, 48)]
OMR = H + 8
LO = 64
PATT = OMC
XR, XCOLS = H + 8, W + 4
PIECES = [(0, 0, 5), (0, 5, 9), (1, 0, 9), (2, 0, 9), (3, 0, 9), (4, 0, 5), (4, 5, 9)]
NP_ = len(PIECES)
PRIME = 1
NCH = PIX // 512


def col_base(pcol):
    return next(px for at, n, px in COLTILES if at <= pcol + 2 < at + n)


def constants_l0():
    sel = np.zeros((128, 2 * DG * TAPS + TAPS, 128), np.float16)
    r, c = np.arange(128) // PC, np.arange(128) % PC
    for g in range(DG):
        for k in range(TAPS):
            dy, dx = 2 * (k // 3) - 2, 2 * (k % 3) - 2
            u = g * TAPS + k
            for yx in range(2):
                row = NMASK + (g * TAPS + k) * 2 + yx
                sel[row, 2 * u + yx] = sel[LO + row, 2 * u + yx] = 1
            sel[PATT + (1 if dy == 0 else 0), 2 * u] = 1
            sel[PATT + 5, 2 * u] = 2 - r
            sel[PATT + 2 + dx // 2 + 1, 2 * u + 1] = 1
            sel[PATT + 5, 2 * u + 1] = -c
            half = slice(g * CG, (g + 1) * CG)
            sel[u, 2 * DG * TAPS + k, half] = sel[LO + u, 2 * DG * TAPS + k, half] = 2
    patt = np.zeros((6, OMR, W), np.float16)
    pr, pc = np.arange(OMR)[:, None], np.arange(W)
    patt[0], patt[1] = pr % TR, (pr + 2) % TR
    for n, dx in enumerate((-2, 0, 2)):
        patt[2 + n] = [p + dx - col_base(p + dx) for p in pc]
    patt[5] = 1
    same = (np.arange(C)[:, None] // 4 == np.arange(C) // 4)
    return {"c_sel": sel, "c_patt": patt.reshape(6, OMR * W),
            "c_group": (same / 4).astype(np.float32), "c_ident": np.eye(128, dtype=np.float32)}


def build_l0(nc, x, woff, boff, wconv, c_sel, c_patt, c_group, c_ident, x1, fint, B):
    with ExitStack() as ctx:
        def sb(name, shape, dt=F32):
            return ctx.enter_context(nc.sbuf_tensor(name, shape, dt))

        def ps(name):
            return ctx.enter_context(nc.psum_tensor(name, [128, 512], F32))

        def sem(name):
            return ctx.enter_context(nc.semaphore(name))

        xraw = sb("xraw", [128, PIX])
        xpad = sb("xpad", [128, XR, XCOLS])
        om = sb("om", [128, OMR * W], F16)
        sel = sb("sel", [128, 2 * DG * TAPS + TAPS, 128], F16)
        wof = sb("wof", [128, TAPS, OMC])
        bof = sb("bof", [OMC, 1])
        wcv = sb("wcv", [128, TAPS, 128])
        group = sb("group", [128, 128])
        ident = sb("ident", [128, 128])
        strip = [sb(f"strip{i}", [128, 5, PR, PC]) for i in range(2)]
        patch = [sb(f"patch{i}", [128, 5, 128]) for i in range(2)]
        dist = [sb(f"dist{i}", [128, 512]) for i in range(3)]
        hat = [sb(f"hat{i}", [128, 512]) for i in range(2)]
        samp = [[sb(f"samp{i}{g}", [128, TAPS * TR, SW]) for g in range(DG)] for i in range(2)]
        val = [sb(f"val{i}", [128, TAPS * TR, SW]) for i in range(2)]
        mask = [sb(f"mask{i}", [128, TAPS * TR, SW]) for i in range(2)]
        om32 = [sb(f"om32{i}", [OMC, 512]) for i in range(2)]
        stats = sb("stats", [128, NCH, 6])
        mv = sb("mv", [128, 2])
        gs = sb("gs", [128, 8])
        fmax = sb("fmax", [OMC, B * NCH])
        fcol = sb("fcol", [OMC, 1])
        fone = sb("fone", [1, 2])

        dist_ps = [ps(f"dist_ps{i}") for i in range(2)]
        val_ps = [ps(f"val_ps{i}") for i in range(2)]
        mask_ps, conv_ps, patch_ps, off_ps = ps("mask_ps"), ps("conv_ps"), ps("patch_ps"), ps("off_ps")

        s_const, s_zero, s_om0, s_patt = sem("const_loaded"), sem("buffers_zeroed"), sem("maps_zeroed"), sem("patterns_loaded")
        s_x, s_st, s_xpad = sem("x_loaded"), sem("x1_stored"), sem("x_normalized")
        s_v = sem("stat_step_vector")
        s_pg = sem("group_mean_ready")
        s_rt = sem("root_ready")
        s_offp, s_om32, s_sig, s_hi, s_lo = sem("offset_conv_done"), sem("maps_biased"), sem("masks_ready"), sem("maps_high"), sem("maps_low")
        s_cl, s_fx, s_fm = sem("maps_clamped"), sem("stat_step_small"), sem("offset_bound")
        s_strip, s_pt, s_patch = sem("strip_ready"), sem("patch_transposed"), sem("patch_ready")
        s_bc, s_dist, s_hat, s_samp = sem("positions_spread"), sem("distances_ready"), sem("hats_ready"), sem("sampling_ready")
        s_mp, s_mask = sem("mask_spread"), sem("mask_ready")
        s_smm, s_val = sem("values_sampled"), sem("values_ready")
        s_conv, s_band = sem("conv_done"), sem("band_ready")
        s_fl, s_flp = sem("flag_step"), sem("flag_turned")
        s_pass_v, s_pass_p = sem("passed_vector"), sem("passed_pool")

        NCONST = 6
        U = DG * TAPS

        block = ctx.enter_context(nc.Block())

        @block.sync
        def _(sp):
            for s in (s_st, s_bc, s_mp, s_pt, s_hat, s_val, s_smm, s_lo, s_samp, s_conv, s_band, s_patch, s_dist, s_mask, s_om32, s_strip, s_xpad):
                sp.sem_inc(s, PRIME)
            sp.dma_start(sel[:], c_sel).then_inc(s_const, 16)
            sp.dma_start(group[:], c_group).then_inc(s_const, 16)
            sp.dma_start(ident[:], c_ident).then_inc(s_const, 16)
            sp.dma_start(wcv[:], wconv).then_inc(s_const, 16)
            sp.dma_start(bof[0:NMASK, :], boff[2 * NMASK:OMC, :]).then_inc(s_const, 16)
            sp.dma_start(bof[NMASK:OMC, :], boff[0:2 * NMASK, :]).then_inc(s_const, 16)
            sp.wait_ge(s_om0, 1)
            sp.dma_start(om[PATT:PATT + 6, :], c_patt).then_inc(s_patt, 16)
            sp.wait_ge(s_zero, 1)
            sp.dma_start(wof[0:CG, :, NMASK:NMASK + 27], woff[:, :, 0:27]).then_inc(s_patt, 16)
            sp.dma_start(wof[CG:C, :, NMASK + 27:OMC], woff[:, :, 27:36]).then_inc(s_patt, 16)
            sp.dma_start(wof[CG:C, :, 0:NMASK], woff[:, :, 36:54]).then_inc(s_patt, 16)
            with sp.Fori(0, B) as b:
                sp.wait_ge(s_st, PRIME + 16 * b)
                sp.dma_start(xraw[:], x[bass.ds(b, 1), :, :].rearrange("a c p -> c (a p)")).then_inc(s_x, 16)
                sp.wait_ge(s_band, PRIME + BANDS * (b + 1))
                sp.dma_start(x1[bass.ds(b, 1), :, :].rearrange("a c p -> c (a p)"), xraw[:]).then_inc(s_st, 16)
            sp.wait_ge(s_st, PRIME + 16 * B)

        @block.gpsimd
        def _(pool):
            pool.memset(om[:], 0.0).then_inc(s_om0, 1)
            pool.memset(wof[:], 0.0).then_inc(s_zero, 1)
            pool.memset(xpad[:], 0.0).then_inc(s_zero, 1)
            for i in range(2):
                for g in range(DG):
                    pool.memset(samp[i][g][:], 0.0).then_inc(s_zero, 1)
                pool.memset(mask[i][:], 0.0).then_inc(s_zero, 1)

            with pool.Fori(0, B) as b:
                pool.wait_ge(s_xpad, PRIME + NCH * (b + 1))
                pool.wait_ge(s_zero, 8)
                pool.wait_ge(s_pt, PRIME + 5 * TILES * b)
                pool.sem_inc(s_pass_p, 1)
                for j, (_, _, px) in enumerate(COLTILES):
                    pool.tensor_copy(strip[0][:, j], xpad[:, 0:PR, 2 + px:2 + px + PC]).then_inc(s_strip, 1)
                with pool.Fori(0, TILES // 2) as h:
                    for d in (1, 2):
                        t = TILES * b + 2 * h + d
                        pool.wait_ge(s_pt, PRIME + 5 * (t - 1))
                        pool.wait_ge(s_zero, 8)
                        for j, (_, _, px) in enumerate(COLTILES):
                            pool.tensor_copy(strip[d % 2][:, j], xpad[:, bass.ds(TR * (2 * h + d), PR), 2 + px:2 + px + PC]).then_inc(s_strip, 1)

        @block.scalar
        def _(act):
            def tile(b, i, s, first):
                t = TILES * b + i
                for u in range(U):
                    g, k = divmod(u, TAPS)
                    n = U * t + u
                    act.wait_ge(s_bc, PRIME + n + 1)
                    if u >= 3:
                        act.wait_ge(s_hat, PRIME + n - 2)
                    else:
                        act.wait_ge(s_hat, PRIME + U * t)
                    act.activation(dist[u % 3][:], dist_ps[u % 2][:], ACT.Abs).then_inc(s_dist, 1)
                    if u < TAPS:
                        dx = 2 * (k % 3) - 2
                        act.wait_ge(s_mp, PRIME + TAPS * t + k + 1)
                        if k == 0 and not first:
                            act.wait_ge(s_val, PRIME + NP_ * (t - 1))
                        if k == 0 and first:
                            act.wait_ge(s_val, PRIME + NP_ * t)
                        act.activation(mask[s][:, k * TR:(k + 1) * TR, 2 + dx:2 + dx + W],
                                       mask_ps[:, (k % 2) * TW:(k % 2 + 1) * TW].rearrange("p (r c) -> p r c", c=W),
                                       ACT.Identity).then_inc(s_mask, 1)
                    if u == 3:
                        act.wait_ge(s_pt, PRIME + 5 * t + 4)
                        if first:
                            act.wait_ge(s_smm, PRIME + NP_ * t)
                        else:
                            act.wait_ge(s_smm, PRIME + NP_ * (t - 1))
                        act.activation(patch[s][:, 0:4, :], patch_ps[:].rearrange("p (j c) -> p j c", c=128), ACT.Identity).then_inc(s_patch, 1)
                        act.wait_ge(s_pt, PRIME + 5 * t + 5)
                        act.activation(patch[s][:, 4, :], off_ps[:, 0:128], ACT.Identity).then_inc(s_patch, 1)

            act.wait_ge(s_const, 16 * NCONST)
            act.wait_ge(s_zero, 8)
            with act.Fori(0, B) as b:
                act.wait_ge(s_v, 6 * b + 5)
                act.activation(gs[:, 4:5], gs[:, 3:4], ACT.Sqrt).then_inc(s_rt, 1)
                act.wait_ge(s_v, 6 * b + 6)
                act.wait_ge(s_strip, PRIME + 5 * TILES * b)
                for q in range(NCH):
                    act.activation(xpad[:, 4 + 8 * q:12 + 8 * q, 2:2 + W],
                                   xraw[:, 512 * q:512 * (q + 1)].rearrange("p (r c) -> p r c", c=W),
                                   ACT.Identity, bias=gs[:, 6:7], scale=gs[:, 5:6]).then_inc(s_xpad, 1)
                for q in range(NCH):
                    n = NCH * b + q
                    act.wait_ge(s_offp, n + 1)
                    if q >= 2:
                        act.wait_ge(s_lo, PRIME + n - 1)
                    else:
                        act.wait_ge(s_lo, PRIME + NCH * b)
                    act.activation(om32[q % 2][:], off_ps[0:OMC, :], ACT.Identity, bias=bof[:, 0:1]).then_inc(s_om32, 1)
                    act.wait_ge(s_om32, PRIME + n + 1)
                    act.activation(om32[q % 2][0:NMASK, :], om32[q % 2][0:NMASK, :], ACT.Sigmoid).then_inc(s_sig, 1)
                    act.wait_ge(s_cl, n + 1)
                    if q == 0:
                        act.wait_ge(s_bc, PRIME + U * TILES * b)
                        act.wait_ge(s_mp, PRIME + TAPS * TILES * b)
                    act.activation(om[0:OMC, (4 + 8 * q) * W:(12 + 8 * q) * W], om32[q % 2][:], ACT.Identity).then_inc(s_hi, 1)
                tile(b, 0, 0, True)
                with act.Fori(0, TILES // 2) as h:
                    for d in (1, 2):
                        tile(b, 2 * h + d, d % 2, False)

        @block.vector
        def _(dve):
            def evacuate(tp, s, m, i):
                j, k0, k1 = PIECES[m]
                at, n, _ = COLTILES[j]
                dve.wait_ge(s_smm, PRIME + NP_ * tp + m + 1)
                dve.wait_ge(s_mask, PRIME + TAPS * (tp + 1))
                rows = slice(k0 * TR, k1 * TR)
                dve.tensor_tensor(val[s][:, rows, at:at + n],
                                  val_ps[m % 2][:, 0:(k1 - k0) * TR * n].rearrange("p (r c) -> p r c", c=n),
                                  mask[s][:, rows, at:at + n], ALU.mult).then_inc(s_val, 1)

            def add_band(b, r, n):
                dve.wait_ge(s_conv, PRIME + n + 1)
                dst = xraw[:, bass.ds(TW * r, TW)] if not isinstance(r, int) else xraw[:, TW * r:TW * (r + 1)]
                half = n_half(r)
                dve.tensor_tensor(dst, conv_ps[:, half * TW:(half + 1) * TW], dst, ALU.add).then_inc(s_band, 1)

            def tile(b, i, s, prev, band):
                t = TILES * b + i
                for u in range(U):
                    g, k = divmod(u, TAPS)
                    n = U * t + u
                    dx = 2 * (k % 3) - 2
                    dve.wait_ge(s_dist, PRIME + n + 1)
                    if u >= 2:
                        dve.wait_ge(s_samp, PRIME + n - 1)
                    else:
                        dve.wait_ge(s_samp, PRIME + U * t)
                    dve.tensor_scalar(hat[u % 2][:], dist[u % 3][:], 1.0, -1.0, ALU.min, ALU.add).then_inc(s_hat, 1)
                    if u == 0:
                        if prev:
                            dve.wait_ge(s_smm, PRIME + NP_ * (t - 1))
                        else:
                            dve.wait_ge(s_smm, PRIME + NP_ * t)
                    dve.wait_ge(s_hat, PRIME + n + 1)
                    dve.tensor_tensor(samp[s][g][:, k * TR:(k + 1) * TR, 2 + dx:2 + dx + W],
                                      hat[u % 2][:, 0:TW].rearrange("p (r c) -> p r c", c=W),
                                      hat[u % 2][:, TW:2 * TW].rearrange("p (r c) -> p r c", c=W),
                                      ALU.mult).then_inc(s_samp, 1)
                    if prev and 2 <= u < 2 + NP_:
                        if u == 2:
                            dve.wait_ge(s_conv, PRIME + (BANDS * b + i - 2 if band else BANDS * b))
                        evacuate(t - 1, 1 - s, u - 2, i - 1)
                if band:
                    add_band_at(b, i - 2, s)

            def add_band_at(b, r, s):
                n = BANDS * b + r
                dve.wait_ge(s_conv, PRIME + n + 1)
                at = TW * r
                dst = xraw[:, bass.ds(at, TW)]
                dve.tensor_tensor(dst, conv_ps[:, s * TW:(s + 1) * TW], dst, ALU.add).then_inc(s_band, 1)

            dve.wait_ge(s_const, 16 * NCONST)
            dve.wait_ge(s_zero, 8)
            with dve.Fori(0, B) as b:
                v = 6 * b
                dve.wait_ge(s_x, 16 * (b + 1))
                for q in range(NCH):
                    ins = dve.bn_stats(stats[:, q, :], xraw[:, 512 * q:512 * (q + 1)])
                ins.then_inc(s_v, 1)
                dve.wait_ge(s_v, v + 1)
                dve.sem_inc(s_pass_v, 1)
                dve.bn_aggr(mv[:], stats[:].rearrange("p a b -> p (a b)")).then_inc(s_v, 1)
                dve.wait_ge(s_pg, 2 * b + 1)
                dve.tensor_copy(gs[:, 0:1], off_ps[:, 0:1]).then_inc(s_v, 1)
                dve.wait_ge(s_v, v + 3)
                dve.tensor_tensor(gs[:, 1:2], mv[:, 0:1], gs[:, 0:1], ALU.subtract).then_inc(s_fx, 1)
                dve.wait_ge(s_fx, 4 * b + 1)
                dve.tensor_tensor(gs[:, 1:2], gs[:, 1:2], gs[:, 1:2], ALU.mult).then_inc(s_fx, 1)
                dve.wait_ge(s_fx, 4 * b + 2)
                dve.tensor_tensor(gs[:, 2:3], gs[:, 1:2], mv[:, 1:2], ALU.add).then_inc(s_v, 1)
                dve.wait_ge(s_pg, 2 * b + 2)
                dve.tensor_scalar(gs[:, 3:4], off_ps[:, 1:2], 1e-5, None, ALU.add).then_inc(s_v, 1)
                dve.wait_ge(s_rt, b + 1)
                dve.wait_ge(s_xpad, PRIME + NCH * b)
                dve.reciprocal(gs[:, 5:6], gs[:, 4:5]).then_inc(s_fx, 1)
                dve.wait_ge(s_fx, 4 * b + 3)
                dve.tensor_scalar(gs[:, 7:8], gs[:, 0:1], -1.0, None, ALU.mult).then_inc(s_fx, 1)
                dve.wait_ge(s_fx, 4 * b + 4)
                dve.tensor_tensor(gs[:, 6:7], gs[:, 7:8], gs[:, 5:6], ALU.mult).then_inc(s_v, 1)
                for q in range(NCH):
                    n = NCH * b + q
                    dve.wait_ge(s_sig, n + 1)
                    dve.tensor_reduce(fmax[:, bass.ds(n, 1)], om32[q % 2][:], AX.X, ALU.max, apply_absolute_value=True).then_inc(s_fm, 1)
                    dve.wait_ge(s_fm, n + 1)
                    dve.tensor_scalar(om32[q % 2][:], om32[q % 2][:], 256.0, -256.0, ALU.min, ALU.max).then_inc(s_cl, 1)
                    dve.wait_ge(s_hi, n + 1)
                    dve.tensor_tensor(om[LO:LO + OMC, (4 + 8 * q) * W:(12 + 8 * q) * W], om32[q % 2][:],
                                      om[0:OMC, (4 + 8 * q) * W:(12 + 8 * q) * W], ALU.subtract).then_inc(s_lo, 1)
                tile(b, 0, 0, False, False)
                tile(b, 1, 1, True, False)
                with dve.Fori(0, (TILES - 3) // 2) as h:
                    for d in (2, 3):
                        tile(b, 2 * h + d, d % 2, True, True)
                tile(b, 16, 0, True, True)
                t = TILES * (b + 1)
                for m in range(NP_):
                    if m == 0:
                        dve.wait_ge(s_conv, PRIME + BANDS * b + 15)
                    evacuate(t - 1, 0, m, 16)
                add_band_at(b, 15, 1)
            dve.wait_ge(s_fm, NCH * B)
            dve.tensor_reduce(fcol[:], fmax[:], AX.X, ALU.max).then_inc(s_fl, 1)
            dve.wait_ge(s_flp, 1)
            dve.tensor_reduce(fone[:, 0:1], off_ps[0:1, 0:OMC], AX.X, ALU.max).then_inc(s_fl, 1)
            dve.wait_ge(s_fl, 2)
            dve.tensor_scalar(fone[:, 1:2], fone[:, 0:1], REACH, None, ALU.is_ge).then_inc(s_fl, 1)
            dve.wait_ge(s_fl, 3)
            dve.tensor_copy(fint[:], fone[:, 1:2]).then_inc(s_fl, 1)
            dve.wait_ge(s_fl, 4)

        @block.tensor
        def _(pe):
            def sample(tp, s, m):
                j, k0, k1 = PIECES[m]
                at, n, _ = COLTILES[j]
                e = NP_ * tp + m
                if m == 0:
                    pe.wait_ge(s_samp, PRIME + U * (tp + 1))
                    pe.wait_ge(s_patch, PRIME + 2 * (tp + 1))
                    pe.wait_ge(s_val, PRIME + e)
                else:
                    pe.wait_ge(s_val, PRIME + e - 1)
                for g in range(DG):
                    ins = pe.matmul(val_ps[m % 2][g * CG:(g + 1) * CG, 0:(k1 - k0) * TR * n],
                                    patch[s][:, j, g * CG:(g + 1) * CG],
                                    samp[s][g][:, k0 * TR:k1 * TR, at:at + n], start=True, stop=True)
                ins.then_inc(s_smm, 1)

            def conv(n, r, tlast, part):
                s = r
                k = part
                dx = 2 * (k % 3) - 2
                out = conv_ps[:, s * TW:(s + 1) * TW].rearrange("p (r c) -> p r c", c=W)
                cols = slice(2 + dx, 2 + dx + W)
                if k == 0:
                    pe.wait_ge(s_val, PRIME + NP_ * (tlast + 1))
                    pe.wait_ge(s_band, PRIME + n)
                if k < 3:
                    ins = pe.matmul(out, wcv[:, k, :], val[s][:, k * TR:(k + 1) * TR, cols], start=(k == 0), stop=False)
                elif k < 6:
                    pe.matmul(out[:, 0:2, :], wcv[:, k, :], val[s][:, k * TR + 2:(k + 1) * TR, cols], start=False, stop=False)
                    ins = pe.matmul(out[:, 2:4, :], wcv[:, k, :], val[1 - s][:, k * TR:k * TR + 2, cols], start=False, stop=False)
                else:
                    ins = pe.matmul(out, wcv[:, k, :], val[1 - s][:, k * TR:(k + 1) * TR, cols], start=False, stop=(k == 8))
                if k == 8:
                    ins.then_inc(s_conv, 1)

            def tile(b, i, s, prev, band):
                t = TILES * b + i
                pe.wait_ge(s_strip, PRIME + 5 * (t + 1))
                pe.wait_ge(s_patch, PRIME + 2 * t)
                for j, (_, _, px) in enumerate(COLTILES):
                    dst = patch_ps[:, j * 128:(j + 1) * 128] if j < 4 else off_ps[:, 0:128]
                    pe.transpose(dst, strip[s][:, j].rearrange("p r c -> p (r c)"), ident[:]).then_inc(s_pt, 1)
                for u in range(U):
                    g, k = divmod(u, TAPS)
                    dy = 2 * (k // 3) - 2
                    n = U * t + u
                    at = W * (TR * i + 2 - dy)
                    if u >= 2:
                        pe.wait_ge(s_dist, PRIME + n - 1)
                    else:
                        pe.wait_ge(s_dist, PRIME + U * t)
                    src = om[:, bass.ds(at, TW)]
                    pe.matmul(dist_ps[u % 2][:, 0:TW], sel[:, 2 * u, :], src, start=True, stop=True)
                    pe.matmul(dist_ps[u % 2][:, TW:2 * TW], sel[:, 2 * u + 1, :], src, start=True, stop=True).then_inc(s_bc, 1)
                    if u < TAPS:
                        pe.wait_ge(s_mask, PRIME + TAPS * t + k)
                        pe.matmul(mask_ps[:, (k % 2) * TW:(k % 2 + 1) * TW], sel[:, 2 * U + k, :], src,
                                  start=True, stop=True).then_inc(s_mp, 1)
                    if prev and 1 <= u < 1 + NP_:
                        sample(t - 1, 1 - s, u - 1)
                    if band and u >= TAPS:
                        conv(BANDS * b + i - 2, s, t - 1, u - TAPS)

            pe.wait_ge(s_const, 16 * NCONST)
            pe.wait_ge(s_patt, 16 * 4)
            with pe.Fori(0, B) as b:
                pe.wait_ge(s_v, 6 * b + 2)
                pe.wait_ge(s_patch, PRIME + 2 * TILES * b)
                pe.matmul(off_ps[:, 0:1], group[:], mv[:, 0:1], start=True, stop=True).then_inc(s_pg, 1)
                pe.wait_ge(s_v, 6 * b + 4)
                pe.matmul(off_ps[:, 1:2], group[:], gs[:, 2:3], start=True, stop=True).then_inc(s_pg, 1)
                pe.wait_ge(s_xpad, PRIME + NCH * (b + 1))
                pe.wait_ge(s_v, 6 * b + 5)
                for q in range(NCH):
                    pe.wait_ge(s_om32, PRIME + NCH * b + q)
                    for k in range(TAPS):
                        dy, dx = 2 * (k // 3) - 2, 2 * (k % 3) - 2
                        ins = pe.matmul(off_ps[0:OMC, :], wof[:, k, :],
                                        xpad[:, 8 * q + dy + 4:8 * q + dy + 12, 2 + dx:2 + dx + W],
                                        start=(k == 0), stop=(k == TAPS - 1))
                    ins.then_inc(s_offp, 1)
                pe.wait_ge(s_lo, PRIME + NCH * (b + 1))
                tile(b, 0, 0, False, False)
                tile(b, 1, 1, True, False)
                with pe.Fori(0, (TILES - 3) // 2) as h:
                    for d in (2, 3):
                        tile(b, 2 * h + d, d % 2, True, True)
                tile(b, 16, 0, True, True)
                t = TILES * (b + 1)
                for m in range(NP_):
                    sample(t - 1, 0, m)
                for k in range(TAPS):
                    conv(BANDS * b + 15, 1, t - 1, k)
            pe.wait_ge(s_fl, 1)
            pe.transpose(off_ps[0:1, 0:OMC], fcol[:], ident[0:OMC, 0:OMC]).then_inc(s_flp, 1)

GK = 128


def constants_general():
    sel = np.zeros((GK, TAPS, 2 * DG + 1, 128), np.float32)
    col = np.arange(128) % W
    for k in range(TAPS):
        dy, dx = 2 * (k // 3) - 2, 2 * (k % 3) - 2
        for g in range(DG):
            row = NMASK + (g * TAPS + k) * 2
            sel[row, k, 2 * g] = sel[PATT, k, 2 * g] = 1
            sel[PATT + 2, k, 2 * g] = dy
            sel[row + 1, k, 2 * g + 1] = sel[PATT + 1, k, 2 * g + 1] = 1
            sel[PATT + 2, k, 2 * g + 1] = dx - col
            sel[g * TAPS + k, k, 2 * DG, g * CG:(g + 1) * CG] = 2
    pos = np.zeros((3, H, W), np.float32)
    pos[0], pos[1], pos[2] = np.arange(H)[:, None], np.arange(W), 1
    rows = -(2 * np.arange(H // 2) + (np.arange(128) // W)[:, None]).astype(np.float32)
    return {"c_gsel": sel, "c_gpos": pos.reshape(3, PIX), "c_grow": rows}


def build_general(nc, fint, x, woff, boff, wconv, c_gsel, c_gpos, c_grow, c_group, c_ident, x1, B):
    PAIRS = H // 2
    with ExitStack() as ctx:
        sb = lambda n, s, d=F32: ctx.enter_context(nc.sbuf_tensor(n, s, d))
        ps = lambda n: ctx.enter_context(nc.psum_tensor(n, [128, 512], F32))
        sem = lambda n: ctx.enter_context(nc.semaphore(n))
        xraw, xn, xt = sb("g_xraw", [128, PIX]), sb("g_xn", [128, PIX]), sb("g_xt", [128, PAIRS, C])
        xpad = sb("g_xpad", [128, XR, XCOLS])
        om = sb("g_om", [GK, PIX])
        sel, selk = sb("g_sel", [GK, TAPS, 2 * DG + 1, 128]), sb("g_selk", [GK, 2 * DG + 1, 128])
        wof, bof = sb("g_wof", [128, TAPS, OMC]), sb("g_bof", [OMC, 1])
        wcv, wck = sb("g_wcv", [128, TAPS, 128]), sb("g_wck", [128, 128])
        group, ident, rows = sb("g_group", [128, 128]), sb("g_ident", [128, 128]), sb("g_rows", [128, PAIRS])
        stats, mv, gs = sb("g_stats", [128, NCH, 6]), sb("g_mv", [128, 2]), sb("g_gs", [128, 8])
        ypos, xdist, xhat = sb("g_ypos", [128, 512]), sb("g_xdist", [128, 512]), sb("g_xhat", [128, 512])
        ydist, yhat, samp = ([sb(f"g_{n}{i}", [128, 512]) for i in range(2)] for n in ("ydist", "yhat", "samp"))
        mask, val = sb("g_mask", [128, 512]), sb("g_val", [128, 512])
        y_ps, x_ps, m_ps, v_ps, c_ps, t_ps = (ps(f"g_{n}_ps") for n in "yxmvct")

        s_const, s_zero, s_patt = sem("g_const_loaded"), sem("g_zeroed"), sem("g_patterns_loaded")
        s_x, s_st, s_pass_v = sem("g_x_loaded"), sem("g_x1_stored"), sem("g_passed_vector")
        s_v, s_pg, s_rt, s_xpad, s_xn = sem("g_stat_step"), sem("g_group_ready"), sem("g_root_ready"), sem("g_padded"), sem("g_normalized")
        s_tp, s_xt = sem("g_turned"), sem("g_turned_copied")
        s_off, s_om, s_sig, s_cl = sem("g_offset_conv_done"), sem("g_maps_biased"), sem("g_masks_ready"), sem("g_maps_clamped")
        s_tap, s_pos, s_yp, s_xd, s_xh = sem("g_tap_operands"), sem("g_positions_spread"), sem("g_rows_copied"), sem("g_column_distance"), sem("g_column_hat")
        s_yd, s_yh, s_s, s_mm = sem("g_row_distance"), sem("g_row_hat"), sem("g_sampling_ready"), sem("g_sampled")
        s_mp, s_mask, s_val, s_conv, s_acc = sem("g_mask_spread"), sem("g_mask_ready"), sem("g_values_ready"), sem("g_conv_done"), sem("g_added")
        block = ctx.enter_context(nc.Block())

        @block.sync
        def _(sp):
            flag = sp.value_load(fint[0:1, 0:1], min_val=0, max_val=1)
            with sp.If(flag == 1):
                for s in (s_st, s_conv, s_val, s_yd, s_xh, s_yh, s_s, s_mm, s_pos, s_mp, s_acc, s_xn, s_xt, s_om, s_mask, s_yp, s_xd):
                    sp.sem_inc(s, PRIME)
                for dst, src in ((sel, c_gsel), (group, c_group), (ident, c_ident), (rows, c_grow), (wcv, wconv)):
                    sp.dma_start(dst[:], src).then_inc(s_const, 16)
                sp.dma_start(bof[0:NMASK, :], boff[2 * NMASK:OMC, :]).then_inc(s_const, 16)
                sp.dma_start(bof[NMASK:OMC, :], boff[0:2 * NMASK, :]).then_inc(s_const, 16)
                sp.wait_ge(s_zero, 3)
                sp.dma_start(om[PATT:PATT + 3, :], c_gpos).then_inc(s_patt, 16)
                sp.dma_start(wof[0:CG, :, NMASK:NMASK + 27], woff[:, :, 0:27]).then_inc(s_patt, 16)
                sp.dma_start(wof[CG:C, :, NMASK + 27:OMC], woff[:, :, 27:36]).then_inc(s_patt, 16)
                sp.dma_start(wof[CG:C, :, 0:NMASK], woff[:, :, 36:54]).then_inc(s_patt, 16)
                with sp.Fori(0, B) as b:
                    sp.wait_ge(s_st, PRIME + 16 * b)
                    sp.dma_start(xraw[:], x[bass.ds(b, 1), :, :].rearrange("a c p -> c (a p)")).then_inc(s_x, 16)
                    sp.wait_ge(s_acc, PRIME + NCH * TAPS * (b + 1))
                    sp.dma_start(x1[bass.ds(b, 1), :, :].rearrange("a c p -> c (a p)"), xraw[:]).then_inc(s_st, 16)
                sp.wait_ge(s_st, PRIME + 16 * B)

        @block.gpsimd
        def _(pool):
            flag = pool.value_load(fint[0:1, 0:1], min_val=0, max_val=1)
            with pool.If(flag == 1):
                pool.memset(wof[:], 0.0).then_inc(s_zero, 1)
                pool.memset(om[:], 0.0).then_inc(s_zero, 1)
                pool.memset(xpad[:], 0.0).then_inc(s_zero, 1)

        @block.scalar
        def _(act):
            flag = act.value_load(fint[0:1, 0:1], min_val=0, max_val=1)
            with act.If(flag == 1):
                act.wait_ge(s_const, 16 * 7)
                act.wait_ge(s_zero, 3)
                with act.Fori(0, B) as b:
                    act.wait_ge(s_v, 9 * b + 6)
                    act.activation(gs[:, 4:5], gs[:, 3:4], ACT.Sqrt).then_inc(s_rt, 1)
                    act.wait_ge(s_v, 9 * b + 9)
                    act.wait_ge(s_conv, PRIME + NCH * TAPS * b)
                    for q in range(NCH):
                        act.activation(xpad[:, 4 + 8 * q:12 + 8 * q, 2:2 + W],
                                       xraw[:, 512 * q:512 * (q + 1)].rearrange("p (r c) -> p r c", c=W),
                                       ACT.Identity, bias=gs[:, 6:7], scale=gs[:, 5:6]).then_inc(s_xpad, 1)
                        act.activation(xn[:, 512 * q:512 * (q + 1)], xraw[:, 512 * q:512 * (q + 1)],
                                       ACT.Identity, bias=gs[:, 6:7], scale=gs[:, 5:6]).then_inc(s_xn, 1)
                    for q in range(NCH):
                        act.wait_ge(s_tp, NCH * b + q + 1)
                        act.activation(xt[:, 4 * q:4 * q + 4, :], t_ps[:].rearrange("p (m c) -> p m c", c=C), ACT.Identity).then_inc(s_xt, 1)
                    for q in range(NCH):
                        n = NCH * b + q
                        act.wait_ge(s_off, n + 1)
                        part = om[0:OMC, 512 * q:512 * (q + 1)]
                        act.activation(part, t_ps[0:OMC, :], ACT.Identity, bias=bof[:, 0:1]).then_inc(s_om, 1)
                        act.wait_ge(s_om, PRIME + n + 1)
                        part = om[0:NMASK, 512 * q:512 * (q + 1)]
                        act.activation(part, part, ACT.Sigmoid).then_inc(s_sig, 1)
                    with act.Fori(0, NCH) as q:
                        with act.Fori(0, TAPS) as k:
                            e = (NCH * b + q) * TAPS + k
                            act.wait_ge(s_mp, PRIME + e + 1)
                            act.wait_ge(s_val, PRIME + e)
                            act.activation(mask[:], m_ps[:], ACT.Identity).then_inc(s_mask, 1)
                            for g in range(DG):
                                act.wait_ge(s_pos, PRIME + DG * e + g + 1)
                                act.wait_ge(s_yd, PRIME + PAIRS * (DG * e + g))
                                act.wait_ge(s_xh, PRIME + DG * e + g)
                                act.activation(ypos[:], y_ps[:], ACT.Identity).then_inc(s_yp, 1)
                                act.activation(xdist[:], x_ps[:], ACT.Abs).then_inc(s_xd, 1)
                                act.wait_ge(s_yp, PRIME + DG * e + g + 1)
                                for n in range(PAIRS):
                                    m = PAIRS * (DG * e + g) + n
                                    act.wait_ge(s_yh, PRIME + (m - 1 if n >= 2 else PAIRS * (DG * e + g)))
                                    act.activation(ydist[n % 2][:], ypos[:], ACT.Abs, bias=rows[:, n:n + 1]).then_inc(s_yd, 1)

        @block.vector
        def _(dve):
            flag = dve.value_load(fint[0:1, 0:1], min_val=0, max_val=1)
            with dve.If(flag == 1):
                dve.wait_ge(s_const, 16 * 7)
                dve.wait_ge(s_zero, 3)
                with dve.Fori(0, B) as b:
                    v = 9 * b
                    dve.wait_ge(s_x, 16 * (b + 1))
                    for q in range(NCH):
                        ins = dve.bn_stats(stats[:, q, :], xraw[:, 512 * q:512 * (q + 1)])
                    ins.then_inc(s_v, 1)
                    dve.wait_ge(s_v, v + 1)
                    dve.sem_inc(s_pass_v, 1)
                    dve.bn_aggr(mv[:], stats[:].rearrange("p a b -> p (a b)")).then_inc(s_v, 1)
                    dve.wait_ge(s_pg, 2 * b + 1)
                    dve.tensor_copy(gs[:, 0:1], t_ps[:, 0:1]).then_inc(s_v, 1)
                    dve.wait_ge(s_v, v + 3)
                    dve.tensor_tensor(gs[:, 1:2], mv[:, 0:1], gs[:, 0:1], ALU.subtract).then_inc(s_v, 1)
                    dve.wait_ge(s_v, v + 4)
                    dve.scalar_tensor_tensor(gs[:, 2:3], gs[:, 1:2], gs[:, 1:2], mv[:, 1:2], ALU.mult, ALU.add).then_inc(s_v, 1)
                    dve.wait_ge(s_pg, 2 * b + 2)
                    dve.tensor_scalar(gs[:, 3:4], t_ps[:, 1:2], 1e-5, None, ALU.add).then_inc(s_v, 1)
                    dve.wait_ge(s_rt, b + 1)
                    dve.wait_ge(s_xn, PRIME + NCH * b)
                    dve.reciprocal(gs[:, 5:6], gs[:, 4:5]).then_inc(s_v, 1)
                    dve.tensor_scalar(gs[:, 7:8], gs[:, 0:1], -1.0, None, ALU.mult).then_inc(s_v, 1)
                    dve.wait_ge(s_v, v + 8)
                    dve.tensor_tensor(gs[:, 6:7], gs[:, 7:8], gs[:, 5:6], ALU.mult).then_inc(s_v, 1)
                    for q in range(NCH):
                        n = NCH * b + q
                        dve.wait_ge(s_sig, n + 1)
                        part = om[0:OMC, 512 * q:512 * (q + 1)]
                        dve.tensor_scalar(part, part, 256.0, -256.0, ALU.min, ALU.max).then_inc(s_cl, 1)
                    with dve.Fori(0, NCH) as q:
                        with dve.Fori(0, TAPS) as k:
                            e = (NCH * b + q) * TAPS + k
                            dve.wait_ge(s_conv, PRIME + e)
                            dve.wait_ge(s_pos, PRIME + DG * e)
                            dve.wait_ge(s_mp, PRIME + e)
                            dve.tensor_copy(selk[:], sel[:, bass.ds(k, 1), :, :].rearrange("p a s q -> p (a s) q")).then_inc(s_tap, 1)
                            dve.tensor_copy(wck[:], wcv[:, bass.ds(k, 1), :].rearrange("p a o -> p (a o)")).then_inc(s_tap, 1)
                            for g in range(DG):
                                dve.wait_ge(s_xd, PRIME + DG * e + g + 1)
                                dve.wait_ge(s_s, PRIME + PAIRS * (DG * e + g))
                                dve.tensor_scalar(xhat[:], xdist[:], 1.0, -1.0, ALU.min, ALU.add).then_inc(s_xh, 1)
                                dve.wait_ge(s_xh, PRIME + DG * e + g + 1)
                                for n in range(PAIRS):
                                    m = PAIRS * (DG * e + g) + n
                                    dve.wait_ge(s_yd, PRIME + m + 1)
                                    dve.wait_ge(s_s, PRIME + (m - 1 if n >= 2 else PAIRS * (DG * e + g)))
                                    dve.tensor_scalar(yhat[n % 2][:], ydist[n % 2][:], 1.0, -1.0, ALU.min, ALU.add).then_inc(s_yh, 1)
                                    dve.wait_ge(s_yh, PRIME + m + 1)
                                    dve.wait_ge(s_mm, PRIME + (m - 1 if n >= 2 else PAIRS * (DG * e + g)))
                                    dve.tensor_tensor(samp[n % 2][:], xhat[:], yhat[n % 2][:], ALU.mult).then_inc(s_s, 1)
                            dve.wait_ge(s_mm, PRIME + PAIRS * DG * (e + 1))
                            dve.wait_ge(s_mask, PRIME + e + 1)
                            dve.tensor_tensor(val[:], v_ps[:], mask[:], ALU.mult).then_inc(s_val, 1)
                            dve.wait_ge(s_conv, PRIME + e + 1)
                            dve.wait_ge(s_acc, PRIME + e)
                            dst = xraw[:, bass.ds(512 * q, 512)]
                            dve.tensor_tensor(dst, c_ps[:], dst, ALU.add).then_inc(s_acc, 1)

        @block.tensor
        def _(pe):
            flag = pe.value_load(fint[0:1, 0:1], min_val=0, max_val=1)
            with pe.If(flag == 1):
                pe.wait_ge(s_const, 16 * 7)
                pe.wait_ge(s_patt, 16 * 4)
                with pe.Fori(0, B) as b:
                    pe.wait_ge(s_v, 9 * b + 2)
                    pe.matmul(t_ps[:, 0:1], group[:], mv[:, 0:1], start=True, stop=True).then_inc(s_pg, 1)
                    pe.wait_ge(s_v, 9 * b + 5)
                    pe.matmul(t_ps[:, 1:2], group[:], gs[:, 2:3], start=True, stop=True).then_inc(s_pg, 1)
                    pe.wait_ge(s_v, 9 * b + 6)
                    for q in range(NCH):
                        pe.wait_ge(s_xn, PRIME + NCH * b + q + 1)
                        pe.wait_ge(s_xt, PRIME + NCH * b + q)
                        for m in range(4):
                            ins = pe.transpose(t_ps[:, 128 * m:128 * m + 128], xn[:, 512 * q + 128 * m:512 * q + 128 * m + 128], ident[:])
                        ins.then_inc(s_tp, 1)
                    pe.wait_ge(s_xpad, NCH * (b + 1))
                    pe.wait_ge(s_xt, PRIME + NCH * (b + 1))
                    for q in range(NCH):
                        pe.wait_ge(s_om, PRIME + NCH * b + q)
                        for k in range(TAPS):
                            dy, dx = 2 * (k // 3) - 2, 2 * (k % 3) - 2
                            ins = pe.matmul(t_ps[0:OMC, :], wof[:, k, :],
                                            xpad[:, 8 * q + dy + 4:8 * q + dy + 12, 2 + dx:2 + dx + W],
                                            start=(k == 0), stop=(k == TAPS - 1))
                        ins.then_inc(s_off, 1)
                    with pe.Fori(0, NCH) as q:
                        with pe.Fori(0, TAPS) as k:
                            pe.wait_ge(s_cl, NCH * (b + 1))
                            e = (NCH * b + q) * TAPS + k
                            src = om[:, bass.ds(512 * q, 512)]
                            pe.wait_ge(s_tap, 2 * (e + 1))
                            pe.wait_ge(s_mask, PRIME + e)
                            pe.matmul(m_ps[:], selk[:, 2 * DG, :], src, start=True, stop=True).then_inc(s_mp, 1)
                            for g in range(DG):
                                pe.wait_ge(s_yp, PRIME + DG * e + g)
                                pe.wait_ge(s_xd, PRIME + DG * e + g)
                                pe.matmul(y_ps[:], selk[:, 2 * g, :], src, start=True, stop=True)
                                pe.matmul(x_ps[:], selk[:, 2 * g + 1, :], src, start=True, stop=True).then_inc(s_pos, 1)
                                pe.wait_ge(s_val, PRIME + e)
                                for n in range(PAIRS):
                                    m = PAIRS * (DG * e + g) + n
                                    pe.wait_ge(s_s, PRIME + m + 1)
                                    pe.matmul(v_ps[g * CG:(g + 1) * CG, :], xt[:, n, g * CG:(g + 1) * CG], samp[n % 2][:],
                                              start=(n == 0), stop=(n == PAIRS - 1)).then_inc(s_mm, 1)
                            pe.wait_ge(s_val, PRIME + e + 1)
                            pe.wait_ge(s_acc, PRIME + e)
                            pe.matmul(c_ps[:], wck[:], val[:], start=True, stop=True).then_inc(s_conv, 1)

KX, KY = H, W // 2
ROWS2 = H // 2
CT = 4
KQ = KY // CT


def constants_l1():
    w, ky, h, kx = np.arange(W), np.arange(KY), np.arange(H), np.arange(KX)
    a = 2 * np.pi * np.outer(w, ky) / W
    fw = np.zeros((2, W, 2, 2, KY))
    for i in range(2):
        fw[i, :, i, 0], fw[i, :, i, 1] = np.cos(a), -np.sin(a)
    b = 2 * np.pi * np.outer(h, kx) / H
    fh = np.zeros((H, 2, 2, KX))
    fh[:, 0, 0], fh[:, 1, 0], fh[:, 0, 1], fh[:, 1, 1] = np.cos(b), np.sin(b), -np.sin(b), np.cos(b)
    fh /= PIX
    c = b.T
    ih = np.zeros((KX, 2, H, 2))
    ih[:, 0, :, 0], ih[:, 1, :, 0], ih[:, 0, :, 1], ih[:, 1, :, 1] = np.cos(c), -np.sin(c), np.sin(c), np.cos(c)
    iw = np.zeros((2, 2, KY, 2, W))
    for n in range(KY):
        k = CT * (n % KQ) + n // KQ
        d = 2 * np.pi * k * w / W
        for i in range(2):
            iw[i, 0, n, i] = np.cos(d) * (1 if k == 0 else 2)
            iw[i, 1, n, i] = -np.sin(d) * (0 if k == 0 else 2)
    f = lambda m: np.ascontiguousarray(m.reshape(128, 128).astype(np.float32))
    same = (np.arange(C)[:, None] // 4 == np.arange(C) // 4)
    return {"c_fw": f(fw), "c_fh": f(fh), "c_ih": f(ih), "c_iw": f(iw)}


def build_l1(nc, x1, wspec, c_fw, c_fh, c_ih, c_iw, c_group, c_ident, out, B=8):
    f1 = nc.dram_tensor("f1_scratch", [B, H, 2, KY, C], F32, kind="Internal").ap()
    ysp = nc.dram_tensor("y_scratch", [B, KX, 2, KY, C], F32, kind="Internal").ap()
    gsp = nc.dram_tensor("g_scratch", [B, H, 2, KY, C], F32, kind="Internal").ap()
    with ExitStack() as keep:
        norm = keep.enter_context(nc.sbuf_tensor("norm", [128, 2, B], F32))
        forward_columns(nc, x1, f1, c_fw, c_group, c_ident, norm, B)
        with nc.sbuf_tensor("spec", [128, KX, KY, 2, B], F32) as spec:
            forward_rows(nc, f1, c_fh, norm, spec, B)
            mix_modes(nc, spec, wspec, ysp, B)
    inverse_rows(nc, ysp, gsp, c_ih, B)
    inverse_columns(nc, gsp, x1, out, c_iw, B)


def forward_columns(nc, x1, f1, c_fw, c_group, c_ident, norm, B):
    with ExitStack() as ctx:
        sb = lambda n, s: ctx.enter_context(nc.sbuf_tensor(n, s, F32))
        ps = lambda n: ctx.enter_context(nc.psum_tensor(n, [128, 512], F32))
        sem = lambda n: ctx.enter_context(nc.semaphore(n))
        fw, group, ident = sb("fw", [128, 128]), sb("group1", [128, 128]), sb("ident1", [128, 128])
        xin = [sb(f"xin{i}", [128, PIX]) for i in range(2)]
        xt = [sb(f"xt{i}", [128, 512]) for i in range(2)]
        fo = [sb(f"fo{i}", [128, ROWS2, C]) for i in range(2)]
        stats, mv, gs = sb("stats1", [128, NCH, 6]), sb("mv1", [128, 2]), sb("gs1", [128, 6])
        t_ps = [ps(f"t_ps{i}") for i in range(2)]
        f_ps = [ps(f"f_ps{i}") for i in range(2)]
        g_ps = ps("g_ps")
        s_const, s_x, s_st = sem("fc_const"), [sem(f"fc_x{i}") for i in range(2)], [sem(f"fc_stored{i}") for i in range(2)]
        s_v, s_pg, s_rt, s_nm = sem("fc_stat_step"), sem("fc_group"), sem("fc_root"), sem("fc_norm")
        s_fx = sem("fc_stat_small")
        s_pass_v, s_pass_s = sem("fc_passed_vector"), sem("fc_passed_sync")
        s_tp, s_xt, s_f, s_fo = sem("fc_turned"), sem("fc_turned_copied"), sem("fc_transformed"), sem("fc_copied")
        block = ctx.enter_context(nc.Block())

        @block.sync
        def _(sp):
            for s in (s_fo, s_f, *s_st, s_xt):
                sp.sem_inc(s, PRIME)
            sp.dma_start(fw[:], c_fw).then_inc(s_const, 16)
            sp.dma_start(group[:], c_group).then_inc(s_const, 16)
            sp.dma_start(ident[:], c_ident).then_inc(s_const, 16)
            with sp.Fori(0, B // 2) as h:
                for i in range(2):
                    b = 2 * h + i
                    sp.wait_ge(s_fo, PRIME + NCH * (b + 1))
                    sp.dma_start(f1[bass.ds(b, 1), :, :, :, :].rearrange("a (m t) r k c -> (t r k) (a m) c", t=2),
                                   fo[i][:]).then_inc(s_st[i], 16)
            for i in range(2):
                sp.wait_ge(s_st[i], PRIME + 16 * (B // 2))

        @block.gpsimd
        def _(pool):
            with pool.Fori(0, B // 2) as h:
                for i in range(2):
                    b = 2 * h + i
                    pool.wait_ge(s_fo, PRIME + 2 * NCH * h)
                    pool.sem_inc(s_pass_s, 1)
                    pool.dma_start(xin[i][:], x1[bass.ds(b, 1), :, :].rearrange("a c p -> c (a p)")).then_inc(s_x[i], 16)

        @block.scalar
        def _(act):
            with act.Fori(0, B // 2) as h:
                for i in range(2):
                    b = 2 * h + i
                    for q in range(NCH):
                        n = NCH * b + q
                        act.wait_ge(s_tp, n + 1)
                        if q >= 2:
                            act.wait_ge(s_f, PRIME + n - 1)
                        else:
                            act.wait_ge(s_f, PRIME + NCH * b)
                        act.activation(xt[q % 2][:], t_ps[q % 2][:], ACT.Identity).then_inc(s_xt, 1)
                    act.wait_ge(s_v, 5 * b + 5)
                    act.activation(gs[:, 4:5], gs[:, 3:4], ACT.Sqrt).then_inc(s_rt, 1)

        @block.vector
        def _(dve):
            def copy_out(i, h, b, q):
                n = NCH * b + q
                dve.wait_ge(s_f, PRIME + n + 1)
                if q == 0:
                    dve.wait_ge(s_st[i], PRIME + 16 * h)
                dve.tensor_copy(fo[i][:, 4 * q:4 * q + 4, :], f_ps[q % 2][:].rearrange("p (m c) -> p m c", c=C)).then_inc(s_fo, 1)

            with dve.Fori(0, B // 2) as h:
                for i in range(2):
                    b = 2 * h + i
                    v = 5 * b
                    dve.wait_ge(s_x[i], 16 * (h + 1))
                    for q in range(NCH):
                        ins = dve.bn_stats(stats[:, q, :], xin[i][:, 512 * q:512 * (q + 1)])
                    ins.then_inc(s_v, 1)
                    dve.wait_ge(s_v, v + 1)
                    dve.sem_inc(s_pass_v, 1)
                    dve.bn_aggr(mv[:], stats[:].rearrange("p a b -> p (a b)")).then_inc(s_v, 1)
                    dve.wait_ge(s_pg, 2 * b + 1)
                    dve.tensor_copy(gs[:, 0:1], g_ps[:, 0:1]).then_inc(s_v, 1)
                    dve.wait_ge(s_v, v + 3)
                    dve.tensor_tensor(gs[:, 1:2], mv[:, 0:1], gs[:, 0:1], ALU.subtract).then_inc(s_fx, 1)
                    dve.wait_ge(s_fx, 3 * b + 1)
                    dve.tensor_tensor(gs[:, 1:2], gs[:, 1:2], gs[:, 1:2], ALU.mult).then_inc(s_fx, 1)
                    dve.wait_ge(s_fx, 3 * b + 2)
                    dve.tensor_tensor(gs[:, 2:3], gs[:, 1:2], mv[:, 1:2], ALU.add).then_inc(s_v, 1)
                    dve.wait_ge(s_pg, 2 * b + 2)
                    dve.tensor_scalar(gs[:, 3:4], g_ps[:, 1:2], 1e-5, None, ALU.add).then_inc(s_v, 1)
                    dve.tensor_copy(norm[:, 1, bass.ds(b, 1)], gs[:, 0:1]).then_inc(s_fx, 1)
                    for q in range(NCH):
                        copy_out(i, h, b, q)
                    dve.wait_ge(s_rt, b + 1)
                    dve.wait_ge(s_fx, 3 * b + 3)
                    dve.reciprocal(norm[:, 0, bass.ds(b, 1)], gs[:, 4:5]).then_inc(s_nm, 1)


        @block.tensor
        def _(pe):
            def turn(i, b, q):
                if q >= 2:
                    pe.wait_ge(s_xt, PRIME + NCH * b + q - 1)
                for m in range(4):
                    ins = pe.transpose(t_ps[q % 2][:, m * 128:(m + 1) * 128],
                                       xin[i][:, (4 * q + m) * 128:(4 * q + m + 1) * 128], ident[:])
                ins.then_inc(s_tp, 1)

            pe.wait_ge(s_const, 48)
            with pe.Fori(0, B // 2) as h:
                for i in range(2):
                    b = 2 * h + i
                    pe.wait_ge(s_x[i], 16 * (h + 1))
                    pe.wait_ge(s_xt, PRIME + NCH * b)
                    turn(i, b, 0)
                    pe.wait_ge(s_v, 5 * b + 2)
                    pe.matmul(g_ps[:, 0:1], group[:], mv[:, 0:1], start=True, stop=True).then_inc(s_pg, 1)
                    turn(i, b, 1)
                    pe.wait_ge(s_v, 5 * b + 4)
                    pe.matmul(g_ps[:, 1:2], group[:], gs[:, 2:3], start=True, stop=True).then_inc(s_pg, 1)
                    for q in range(NCH):
                        n = NCH * b + q
                        pe.wait_ge(s_xt, PRIME + n + 1)
                        if q >= 2:
                            pe.wait_ge(s_fo, PRIME + n - 1)
                        else:
                            pe.wait_ge(s_fo, PRIME + NCH * b)
                        pe.matmul(f_ps[q % 2][:], fw[:], xt[q % 2][:], start=True, stop=True).then_inc(s_f, 1)
                        if q + 2 < NCH:
                            turn(i, b, q + 2)


def forward_rows(nc, f1, c_fh, norm, spec, B):
    G = KY // 4
    with ExitStack() as ctx:
        sb = lambda n, s: ctx.enter_context(nc.sbuf_tensor(n, s, F32))
        sem = lambda n: ctx.enter_context(nc.semaphore(n))
        fh = sb("fh", [128, 128])
        fin = [sb(f"fin{i}", [128, KY, C]) for i in range(2)]
        ps = [ctx.enter_context(nc.psum_tensor(f"r_ps{i}", [128, 512], F32)) for i in range(4)]
        s_const, s_f = sem("fr_const"), [sem(f"fr_in{i}") for i in range(2)]
        s_r, s_a, s_d, s_dc = sem("fr_transformed"), sem("fr_by_scalar"), sem("fr_by_vector"), sem("fr_dc")
        block = ctx.enter_context(nc.Block())

        def place(b, g):
            return spec[:, :, 4 * g:4 * g + 4, :, bass.ds(b, 1)].rearrange("p x y r a -> p y r (x a)")

        @block.sync
        def _(sp):
            for s in (s_r, s_a, s_d):
                sp.sem_inc(s, PRIME)
            sp.dma_start(fh[:], c_fh).then_inc(s_const, 16)
            with sp.Fori(0, B // 2) as h:
                for i in range(2):
                    sp.wait_ge(s_r, PRIME + 2 * G * h)
                    sp.dma_start(fin[i][:], f1[bass.ds(2 * h + i, 1), :, :, :, :].rearrange("a h r k c -> (a h r) k c")).then_inc(s_f[i], 16)

        @block.tensor
        def _(pe):
            pe.wait_ge(s_const, 16)
            with pe.Fori(0, B // 2) as h:
                for i in range(2):
                    b = 2 * h + i
                    pe.wait_ge(s_f[i], 16 * (h + 1))
                    for g in range(G):
                        done, n = (s_a, G // 2 * b + g // 2) if g % 2 == 0 else (s_d, G // 2 * b + g // 2)
                        if g >= 4:
                            pe.wait_ge(done, PRIME + n - 1)
                        else:
                            pe.wait_ge(done, PRIME + G // 2 * b)
                        for y in range(4):
                            ins = pe.matmul(ps[g % 4][:, 128 * y:128 * y + 128], fin[i][:, 4 * g + y, :], fh[:], start=True, stop=True)
                        ins.then_inc(s_r, 1)

        @block.scalar
        def _(act):
            with act.Fori(0, B // 2) as h:
                for i in range(2):
                    b = 2 * h + i
                    for g in range(0, G, 2):
                        act.wait_ge(s_r, PRIME + G * b + g + 1)
                        act.activation(place(b, g), ps[g % 4][:].rearrange("p (y r x) -> p y r x", y=4, r=2), ACT.Identity,
                                       scale=norm[:, 0, bass.ds(b, 1)]).then_inc(s_a, 1)

        @block.vector
        def _(dve):
            with dve.Fori(0, B // 2) as h:
                for i in range(2):
                    b = 2 * h + i
                    for g in range(1, G, 2):
                        dve.wait_ge(s_r, PRIME + G * b + g + 1)
                        dve.tensor_scalar(place(b, g), ps[g % 4][:].rearrange("p (y r x) -> p y r x", y=4, r=2),
                                          norm[:, 0, bass.ds(b, 1)], None, ALU.mult).then_inc(s_d, 1)
            dve.tensor_tensor(norm[:, 1, :], norm[:, 1, :], norm[:, 0, :], ALU.mult).then_inc(s_dc, 1)
            dve.wait_ge(s_dc, 1)
            dve.wait_ge(s_a, PRIME + G // 2 * B)
            dve.tensor_tensor(spec[:, 0, 0, 0, :], spec[:, 0, 0, 0, :], norm[:, 1, :], ALU.subtract).then_inc(s_dc, 1)


def mix_modes(nc, spec, wspec, ysp, B):
    P2 = 2 * B
    with ExitStack() as ctx:
        sb = lambda n, s: ctx.enter_context(nc.sbuf_tensor(n, s, F32))
        sem = lambda n: ctx.enter_context(nc.semaphore(n))
        wt = [sb(f"wt{i}", [128, 2, KY, C]) for i in range(2)]
        xs = [sb(f"xs{i}", [128, KY, 3 * B]) for i in range(2)]
        ys = [sb(f"ys{i}", [128, KQ, C]) for i in range(2)]
        ps = [ctx.enter_context(nc.psum_tensor(f"m_ps{i}", [128, 512], F32)) for i in range(4)]
        s_w = [[sem(f"mm_weights{i}{r}") for r in range(2)] for i in range(2)]
        s_zero, s_xs, s_mm, s_y = sem("mm_zeroed"), sem("mm_operand"), sem("mm_mixed"), sem("mm_copied")
        s_st = [sem(f"mm_stored{i}") for i in range(2)]
        block = ctx.enter_context(nc.Block())

        @block.sync
        def _(sp):
            for s in (s_mm, *s_st, s_y):
                sp.sem_inc(s, PRIME)
            with sp.Fori(0, KX // 2) as h:
                for i in range(2):
                    k = 2 * h + i
                    sp.wait_ge(s_mm, PRIME + 4 * h)
                    for r in range(2):
                        sp.dma_start(wt[i][:, r, :, :], wspec[bass.ds(k, 1), r, :, :, :].rearrange("a i y o -> i (a y) o")).then_inc(s_w[i][r], 16)

        @block.scalar
        def _(act):
            with act.Fori(0, KX // 2) as h:
                for i in range(2):
                    k = 2 * h + i
                    act.wait_ge(s_y, PRIME + 2 * (k + 1))
                    for j in range(CT):
                        act.dma_start(ysp[:, bass.ds(k, 1), :, KQ * j:KQ * (j + 1), :].rearrange("b a r q o -> (a r) b (q o)"),
                                      ys[i][32 * j:32 * j + P2, :, :].rearrange("p q o -> p (q o)")).then_inc(s_st[i], 16)
            for i in range(2):
                act.wait_ge(s_st[i], PRIME + 16 * CT * (KX // 2))

        @block.vector
        def _(dve):
            for p in ps:
                ins = dve.memset(p[:], 0.0)
            ins.then_inc(s_zero, 1)
            dve.wait_ge(s_zero, 1)

            def operand(i, h):
                k = 2 * h + i
                src = spec[:, bass.ds(k, 1), :, :, :].rearrange("p a y r b -> p (a y) (r b)")
                dve.wait_ge(s_mm, PRIME + 4 * h)
                dve.tensor_copy(xs[i][:, :, B:3 * B], src).then_inc(s_xs, 1)
                dve.tensor_scalar(xs[i][:, :, 0:B], src[:, :, B:2 * B], -1.0, None, ALU.mult).then_inc(s_xs, 1)

            with dve.Fori(0, KX // 2) as h:
                for i in range(2):
                    operand(i, h)
                for i in range(2):
                    k = 2 * h + i
                    for f in range(2):
                        dve.wait_ge(s_mm, PRIME + 2 * k + f + 1)
                        if f == 0:
                            dve.wait_ge(s_st[i], PRIME + 16 * CT * h)
                        dve.tensor_copy(ys[i][:, 4 * f:4 * f + 4, :], ps[2 * i + f][:].rearrange("p (q o) -> p q o", o=C)).then_inc(s_y, 1)

        @block.tensor
        def _(pe):
            pe.wait_ge(s_zero, 1)
            with pe.Fori(0, KX // 2) as h:
                for i in range(2):
                    k = 2 * h + i
                    pe.wait_ge(s_xs, 2 * (k + 1))
                    for r in range(2):
                        pe.wait_ge(s_w[i][r], 16 * (h + 1))
                    pe.wait_ge(s_y, PRIME + 4 * h)
                    for f in range(2):
                        for q in range(4 * f, 4 * f + 4):
                            for j in range(CT):
                                y = CT * q + j
                                o = ps[2 * i + f][32 * j:32 * j + P2, (q % 4) * C:(q % 4 + 1) * C]
                                pe.matmul(o, xs[i][:, y, B:3 * B], wt[i][:, 0, y, :], start=True, stop=False)
                                ins = pe.matmul(o, xs[i][:, y, 0:2 * B], wt[i][:, 1, y, :], start=False, stop=True)
                        ins.then_inc(s_mm, 1)


def inverse_rows(nc, ysp, gsp, c_ih, B):
    with ExitStack() as ctx:
        sb = lambda n, s: ctx.enter_context(nc.sbuf_tensor(n, s, F32))
        sem = lambda n: ctx.enter_context(nc.semaphore(n))
        ih = sb("ih", [128, 128])
        yin = [sb(f"yin{i}", [128, KY * C]) for i in range(2)]
        go = [sb(f"go{i}", [128, KY * C]) for i in range(2)]
        ps = [ctx.enter_context(nc.psum_tensor(f"i_ps{i}", [128, 512], F32)) for i in range(4)]
        s_const, s_in, s_st = sem("ir_const"), [sem(f"ir_in{i}") for i in range(2)], [sem(f"ir_stored{i}") for i in range(2)]
        s_mm, s_a, s_d = sem("ir_transformed"), sem("ir_by_scalar"), sem("ir_by_vector")
        block = ctx.enter_context(nc.Block())

        @block.sync
        def _(sp):
            for s in (s_mm, *s_st, s_a, s_d):
                sp.sem_inc(s, PRIME)
            sp.dma_start(ih[:], c_ih).then_inc(s_const, 16)
            with sp.Fori(0, B // 2) as h:
                for i in range(2):
                    b = 2 * h + i
                    sp.wait_ge(s_a, PRIME + NCH // 2 * (b + 1))
                    sp.wait_ge(s_d, PRIME + NCH // 2 * (b + 1))
                    sp.dma_start(gsp[bass.ds(b, 1), :, :, :, :].rearrange("a h r k c -> (a h r) (k c)"), go[i][:]).then_inc(s_st[i], 16)
            for i in range(2):
                sp.wait_ge(s_st[i], PRIME + 16 * (B // 2))

        def copier(eng, odd, done, copy):
            with eng.Fori(0, B // 2) as h:
                for i in range(2):
                    eng.wait_ge(s_st[i], PRIME + 16 * h)
                    for q in range(odd, NCH, 2):
                        eng.wait_ge(s_mm, PRIME + NCH * (2 * h + i) + q + 1)
                        copy(go[i][:, 512 * q:512 * (q + 1)], ps[q % 4][:]).then_inc(done, 1)

        @block.gpsimd
        def _(pool):
            with pool.Fori(0, B // 2) as h:
                for i in range(2):
                    pool.wait_ge(s_mm, PRIME + 2 * NCH * h)
                    pool.dma_start(yin[i][:], ysp[bass.ds(2 * h + i, 1), :, :, :, :].rearrange("a x r k c -> (a x r) (k c)")).then_inc(s_in[i], 16)

        @block.scalar
        def _(act):
            copier(act, 0, s_a, lambda o, p: act.activation(o, p, ACT.Identity))

        @block.vector
        def _(dve):
            copier(dve, 1, s_d, lambda o, p: dve.tensor_copy(o, p))

        @block.tensor
        def _(pe):
            pe.wait_ge(s_const, 16)
            with pe.Fori(0, B // 2) as h:
                for i in range(2):
                    b = 2 * h + i
                    pe.wait_ge(s_in[i], 16 * (h + 1))
                    for q in range(NCH):
                        done = (s_a, s_d)[q % 2]
                        n = NCH // 2 * b + q // 2
                        pe.wait_ge(done, PRIME + (n - 1 if q >= 4 else NCH // 2 * b))
                        pe.matmul(ps[q % 4][:], ih[:], yin[i][:, 512 * q:512 * (q + 1)], start=True, stop=True).then_inc(s_mm, 1)


def inverse_columns(nc, gsp, x1, out, c_iw, B):
    with ExitStack() as ctx:
        sb = lambda n, s: ctx.enter_context(nc.sbuf_tensor(n, s, F32))
        sem = lambda n: ctx.enter_context(nc.semaphore(n))
        iw = sb("iw", [128, 128])
        gin = [sb(f"gin{i}", [128, ROWS2, C]) for i in range(2)]
        xr = [sb(f"xr{i}", [128, PIX]) for i in range(2)]
        ps = [ctx.enter_context(nc.psum_tensor(f"o_ps{i}", [128, 512], F32)) for i in range(4)]
        s_const, s_in, s_x, s_st = sem("ic_const"), [sem(f"ic_in{i}") for i in range(2)], [sem(f"ic_x{i}") for i in range(2)], [sem(f"ic_stored{i}") for i in range(2)]
        s_mm, s_o = sem("ic_transformed"), sem("ic_added")
        block = ctx.enter_context(nc.Block())

        @block.sync
        def _(sp):
            for s in (s_mm, *s_st, s_o):
                sp.sem_inc(s, PRIME)
            sp.dma_start(iw[:], c_iw).then_inc(s_const, 16)
            with sp.Fori(0, B // 2) as h:
                for i in range(2):
                    b = 2 * h + i
                    sp.wait_ge(s_o, PRIME + NCH * (b + 1))
                    sp.dma_start(out[bass.ds(b, 1), :, :].rearrange("a c p -> c (a p)"), xr[i][:]).then_inc(s_st[i], 16)
            for i in range(2):
                sp.wait_ge(s_st[i], PRIME + 16 * (B // 2))

        @block.scalar
        def _(act):
            with act.Fori(0, B // 2) as h:
                for i in range(2):
                    b = 2 * h + i
                    act.wait_ge(s_mm, PRIME + 2 * NCH * h)
                    for t in range(2):
                        act.dma_start(gin[i][64 * t:64 * t + 64], gsp[bass.ds(b, 1), :, :, :, :].rearrange("a (m t) r k c -> t (r k) (a m) c", t=2)[t]).then_inc(s_in[i], 16)
                    act.wait_ge(s_st[i], PRIME + 16 * h)
                    act.dma_start(xr[i][:], x1[bass.ds(b, 1), :, :].rearrange("a c p -> c (a p)")).then_inc(s_x[i], 16)

        @block.vector
        def _(dve):
            with dve.Fori(0, B // 2) as h:
                for i in range(2):
                    b = 2 * h + i
                    dve.wait_ge(s_x[i], 16 * (h + 1))
                    for q in range(NCH):
                        dve.wait_ge(s_mm, PRIME + NCH * b + q + 1)
                        dve.tensor_tensor(xr[i][:, 512 * q:512 * (q + 1)], ps[q % 4][:], xr[i][:, 512 * q:512 * (q + 1)], ALU.add).then_inc(s_o, 1)

        @block.tensor
        def _(pe):
            pe.wait_ge(s_const, 16)
            with pe.Fori(0, B // 2) as h:
                for i in range(2):
                    b = 2 * h + i
                    pe.wait_ge(s_in[i], 32 * (h + 1))
                    for q in range(NCH):
                        pe.wait_ge(s_o, PRIME + (NCH * b + q - 3 if q >= 4 else NCH * b))
                        for m in range(4):
                            ins = pe.matmul(ps[q % 4][:, 128 * m:128 * m + 128], gin[i][:, 4 * q + m, :], iw[:], start=True, stop=True)
                        ins.then_inc(s_mm, 1)


def build(nc, B, x, woff, boff, wconv, wspec, c_sel, c_patt, c_gsel, c_gpos, c_grow, c_group, c_ident,
          c_fw, c_fh, c_ih, c_iw, out):
    x1 = nc.dram_tensor("x1_scratch", [B, C, PIX], F32, kind="Internal").ap()
    with nc.sbuf_tensor("fint", [1, 1], I32) as fint:
        build_l0(nc, x, woff, boff, wconv, c_sel, c_patt, c_group, c_ident, x1, fint, B)
        build_general(nc, fint, x, woff, boff, wconv, c_gsel, c_gpos, c_grow, c_group, c_ident, x1, B)
    build_l1(nc, x1, wspec, c_fw, c_fh, c_ih, c_iw, c_group, c_ident, out, B)


def kernel(x, L0_conv_offset_w, L0_conv_offset_b, L0_conv_weight,
           L1_conv_w1_real, L1_conv_w1_imag, L1_conv_w2_real, L1_conv_w2_imag):
    import concourse.bacc as bacc
    from concourse.bass_utils import run_bass_kernel_spmd

    B = x.shape[0]
    wspec = np.empty((KX, 2, C, KY, C), np.float32)
    for half, parts in enumerate(((L1_conv_w1_real, L1_conv_w1_imag), (L1_conv_w2_real, L1_conv_w2_imag))):
        for r, w in enumerate(parts):
            wspec[half * KX // 2:(half + 1) * KX // 2, r] = np.asarray(w).transpose(2, 0, 3, 1)
    arrays = {
        "x": np.ascontiguousarray(np.asarray(x).reshape(B, C, PIX)),
        "woff": np.ascontiguousarray(np.asarray(L0_conv_offset_w).transpose(1, 2, 3, 0).reshape(CG, TAPS, OMC)),
        "boff": np.ascontiguousarray(np.asarray(L0_conv_offset_b).reshape(OMC, 1)),
        "wconv": np.ascontiguousarray(np.asarray(L0_conv_weight).transpose(1, 2, 3, 0).reshape(C, TAPS, C)),
        "wspec": wspec,
        **constants_l0(), **constants_general(), **constants_l1(),
    }
    nc = bacc.Bacc("TRN2", target_bir_lowering=False, num_devices=1)
    aps = {n: nc.dram_tensor(n, a.shape, mybir.dt.from_np(a.dtype), kind="ExternalInput").ap() for n, a in arrays.items()}
    out = nc.dram_tensor("out", (B, C, PIX), F32, kind="ExternalOutput").ap()
    build(nc, B=B, out=out, **aps)
    r = run_bass_kernel_spmd(nc, [arrays], core_ids=[0])
    return r.results[0]["out"].reshape(B, C, H, W)
```

```python
import concourse.bass as bass
from concourse import mybir
import numpy as np
from contextlib import ExitStack

F32, F16, I32 = mybir.dt.float32, mybir.dt.float16, mybir.dt.int32
ALU = mybir.AluOpType
ACT = mybir.ActivationFunctionType
AX = mybir.AxisListType

C, H, W = 128, 64, 64
PIX = H * W
TAPS = 9
DG = 2
CG = C // DG
OMC = DG * 3 * TAPS
NMASK = DG * TAPS
REACH = 2.0
TR = 4
TILES = (H + 4) // TR
BANDS = H // TR
PR = TR + 4
PC = 16
SW = W + 4
TW = TR * W
COLTILES = [(0, 16, 0), (16, 12, 12), (28, 12, 24), (40, 12, 36), (52, 16, 48)]
OMR = H + 8
LO = 64
PATT = OMC
XR, XCOLS = H + 8, W + 4
PIECES = [(0, 0, 5), (0, 5, 9), (1, 0, 9), (2, 0, 9), (3, 0, 9), (4, 0, 5), (4, 5, 9)]
NP_ = len(PIECES)
PRIME = 64
NCH = PIX // 512


def col_base(pcol):
    return next(px for at, n, px in COLTILES if at <= pcol + 2 < at + n)


def constants_l0():
    sel = np.zeros((128, 2 * DG * TAPS + TAPS, 128), np.float16)
    r, c = np.arange(128) // PC, np.arange(128) % PC
    for g in range(DG):
        for k in range(TAPS):
            dy, dx = 2 * (k // 3) - 2, 2 * (k % 3) - 2
            u = g * TAPS + k
            for yx in range(2):
                row = NMASK + (g * TAPS + k) * 2 + yx
                sel[row, 2 * u + yx] = sel[LO + row, 2 * u + yx] = 1
            sel[PATT + (1 if dy == 0 else 0), 2 * u] = 1
            sel[PATT + 5, 2 * u] = 2 - r
            sel[PATT + 2 + dx // 2 + 1, 2 * u + 1] = 1
            sel[PATT + 5, 2 * u + 1] = -c
            half = slice(g * CG, (g + 1) * CG)
            sel[u, 2 * DG * TAPS + k, half] = sel[LO + u, 2 * DG * TAPS + k, half] = 2
    patt = np.zeros((6, OMR, W), np.float16)
    pr, pc = np.arange(OMR)[:, None], np.arange(W)
    patt[0], patt[1] = pr % TR, (pr + 2) % TR
    for n, dx in enumerate((-2, 0, 2)):
        patt[2 + n] = [p + dx - col_base(p + dx) for p in pc]
    patt[5] = 1
    same = (np.arange(C)[:, None] // 4 == np.arange(C) // 4)
    return {"c_sel": sel, "c_patt": patt.reshape(6, OMR * W),
            "c_group": (same / 4).astype(np.float32), "c_ident": np.eye(128, dtype=np.float32)}


def build_l0(nc, x, woff, boff, wconv, c_sel, c_patt, c_group, c_ident, x1, fint, B):
    with ExitStack() as ctx:
        def sb(name, shape, dt=F32):
            return ctx.enter_context(nc.sbuf_tensor(name, shape, dt))

        def ps(name):
            return ctx.enter_context(nc.psum_tensor(name, [128, 512], F32))

        def sem(name):
            return ctx.enter_context(nc.semaphore(name))

        xraw = sb("xraw", [128, PIX])
        xpad = [sb(f"xpad{i}", [128, XR, XCOLS]) for i in range(2)]
        om = [sb(f"om{i}", [128, OMR * W], F16) for i in range(2)]
        sel = sb("sel", [128, 2 * DG * TAPS + TAPS, 128], F16)
        wof, bof = sb("wof", [128, TAPS, OMC]), sb("bof", [OMC, 1])
        wcv = sb("wcv", [128, TAPS, 128])
        group, ident = sb("group", [128, 128]), sb("ident", [128, 128])
        strip = [sb(f"strip{i}", [128, 5, PR, PC]) for i in range(2)]
        patch = [sb(f"patch{i}", [128, 5, 128]) for i in range(2)]
        dist = [sb(f"dist{i}", [128, 512]) for i in range(3)]
        hat = [sb(f"hat{i}", [128, 512]) for i in range(2)]
        samp = [[sb(f"samp{i}{g}", [128, TAPS * TR, SW]) for g in range(DG)] for i in range(2)]
        val = [sb(f"val{i}", [128, TAPS * TR, SW]) for i in range(2)]
        mask = [sb(f"mask{i}", [128, TAPS * TR, SW]) for i in range(2)]
        om32 = sb("om32", [OMC, 512])
        band = [sb(f"band{i}", [128, TW]) for i in range(2)]
        stats, mv, gs, power = sb("stats", [128, NCH, 6]), sb("mv", [128, 2]), sb("gs", [128, 8]), sb("power", [128, 1])
        fmax, fcol, fone = sb("fmax", [OMC, (B + 1) * NCH]), sb("fcol", [OMC, 1]), sb("fone", [1, 2])

        dist_ps = [ps(f"dist_ps{i}") for i in range(2)]
        val_ps = [ps(f"val_ps{i}") for i in range(2)]
        mask_ps, conv_ps, patch_ps, off_ps = ps("mask_ps"), ps("conv_ps"), ps("patch_ps"), ps("off_ps")

        s_const, s_zero, s_om0, s_patt = sem("const_loaded"), sem("buffers_zeroed"), sem("maps_zeroed"), sem("patterns_loaded")
        s_x, s_norm = sem("x_loaded"), sem("x_normalized")
        s_v, s_fx = sem("stat_step"), sem("stat_small_step")
        s_pg, s_rt, s_pow = sem("group_mean_ready"), sem("root_ready"), sem("power_set")
        s_off, s_om, s_sig, s_cl = sem("offset_conv_done"), sem("maps_biased"), sem("masks_ready"), sem("maps_clamped")
        s_fm, s_hi, s_lo = sem("offset_bound"), sem("maps_high"), sem("maps_low")
        s_strip, s_pt, s_patch = sem("strip_ready"), sem("patch_turned"), sem("patch_ready")
        s_bc, s_dist, s_hat, s_samp = sem("positions_spread"), sem("distances_ready"), sem("hats_ready"), sem("sampling_ready")
        s_mp, s_mask = sem("mask_spread"), sem("mask_ready")
        s_smm, s_val = sem("values_sampled"), sem("values_ready")
        s_conv, s_band = sem("conv_done"), sem("band_ready")
        s_bx, s_st = [sem(f"band_loaded{i}") for i in range(2)], [sem(f"band_stored{i}") for i in range(2)]
        s_fl, s_flp = sem("flag_step"), sem("flag_turned")
        s_pass_v, s_pass_p = sem("passed_vector"), sem("passed_pool")

        NCONST = 6
        NZERO = 9
        U = DG * TAPS
        PAIRS = (TILES - 3) // 2

        CONVOLVES = {"start": 0, "second": 0, "two": 0, "odd": 1, "even": 1, "zero": 1, "one": 1}
        SAMPLES_AT = {5 + 2 * m: m for m in range(NP_)}
        VALUES_AT = {7 + 2 * m: m for m in range(NP_ - 1)} | {0: NP_ - 1}

        def bands_before(b, i, kind):
            return BANDS * b + {"zero": -2, "one": -1, "two": 0}.get(kind, i - 3)

        def image_tiles(eng, b, q, tile):
            tile(b, 2, q, q, "two")
            with eng.Fori(0, PAIRS) as h:
                tile(b, 2 * h + 3, q, 1 - q, "odd", h)
                tile(b, 2 * h + 4, q, q, "even", h)
            tile(b + 1, 0, 1 - q, 1 - q, "zero")
            tile(b + 1, 1, 1 - q, q, "one")

        block = ctx.enter_context(nc.Block())

        @block.sync
        def _(sp):
            for s in (s_norm, s_om, s_hi, s_lo, s_cl, s_pt, s_patch, s_bc, s_dist, s_hat, s_samp, s_mp, s_mask,
                      s_smm, s_val, s_conv, s_band, s_strip, s_off, *s_st):
                sp.sem_inc(s, PRIME)
            sp.dma_start(xraw[:], x[0, :, :]).then_inc(s_x, 16)
            sp.dma_start(sel[:], c_sel).then_inc(s_const, 16)
            sp.dma_start(group[:], c_group).then_inc(s_const, 16)
            sp.dma_start(ident[:], c_ident).then_inc(s_const, 16)
            sp.dma_start(wcv[:], wconv).then_inc(s_const, 16)
            sp.dma_start(bof[0:NMASK, :], boff[2 * NMASK:OMC, :]).then_inc(s_const, 16)
            sp.dma_start(bof[NMASK:OMC, :], boff[0:2 * NMASK, :]).then_inc(s_const, 16)
            sp.wait_ge(s_om0, 3)
            for i in range(2):
                sp.dma_start(om[i][PATT:PATT + 6, :], c_patt).then_inc(s_patt, 16)
            sp.dma_start(wof[0:CG, :, NMASK:NMASK + 27], woff[:, :, 0:27]).then_inc(s_patt, 16)
            sp.dma_start(wof[CG:C, :, NMASK + 27:OMC], woff[:, :, 27:36]).then_inc(s_patt, 16)
            sp.dma_start(wof[CG:C, :, 0:NMASK], woff[:, :, 36:54]).then_inc(s_patt, 16)

            def load_band(b, r, i, use):
                sp.wait_ge(s_st[i], PRIME + 16 * use)
                sp.dma_start(band[i][:], x[bass.ds(b, 1), :, bass.ds(TW * r, TW)].rearrange("a c p -> c (a p)")).then_inc(s_bx[i], 16)

            def store_band(b, r, i):
                sp.wait_ge(s_band, PRIME + BANDS * b + r + 1)
                sp.dma_start(x1[bass.ds(b, 1), :, bass.ds(TW * r, TW)].rearrange("a c p -> c (a p)"), band[i][:]).then_inc(s_st[i], 16)

            with sp.Fori(0, B) as b:
                sp.wait_ge(s_norm, PRIME + NCH * (b + 1))
                sp.dma_start(xraw[:], x[bass.ds((b + 1) % B, 1), :, :].rearrange("a c p -> c (a p)")).then_inc(s_x, 16)
                load_band(b, 0, 0, BANDS // 2 * b)
                with sp.Fori(0, BANDS // 2 - 1) as h:
                    load_band(b, 2 * h + 1, 1, BANDS // 2 * b + h)
                    store_band(b, 2 * h, 0)
                    load_band(b, 2 * h + 2, 0, BANDS // 2 * b + h + 1)
                    store_band(b, 2 * h + 1, 1)
                load_band(b, 15, 1, BANDS // 2 * b + 7)
                store_band(b, 14, 0)
                store_band(b, 15, 1)
            for i in range(2):
                sp.wait_ge(s_st[i], PRIME + 16 * B * BANDS // 2)

        @block.gpsimd
        def _(pool):
            for i in range(2):
                pool.memset(om[i][:], 0.0).then_inc(s_om0, 1)
            pool.memset(wof[:], 0.0).then_inc(s_om0, 1)
            for i in range(2):
                pool.memset(xpad[i][:], 0.0).then_inc(s_zero, 1)
                for g in range(DG):
                    pool.memset(samp[i][g][:], 0.0).then_inc(s_zero, 1)
                pool.memset(mask[i][:], 0.0).then_inc(s_zero, 1)
            pool.memset(fmax[:], 0.0).then_inc(s_zero, 1)

            def tile(b, i, q, s, kind, h=None):
                t = TILES * b + i
                if kind in ("start", "zero"):
                    pool.wait_ge(s_norm, PRIME + NCH * (b + 1))
                pool.wait_ge(s_pt, PRIME + 2 * (t - 1))
                if kind != "start":
                    pool.sem_inc(s_pass_p, 1)
                for j, (_, _, px) in enumerate(COLTILES):
                    src = xpad[q][:, 0:PR, 2 + px:2 + px + PC] if kind in ("start", "zero") \
                        else xpad[q][:, bass.ds(TR * i, PR), 2 + px:2 + px + PC]
                    ins = pool.tensor_copy(strip[s][:, j], src)
                ins.then_inc(s_strip, 1)
                if kind == "two":
                    root(b + 1)

            def root(b):
                pool.wait_ge(s_pow, 1)
                pool.wait_ge(s_v, 6 * b + 5)
                pool.tensor_tensor(gs[:, 5:6], gs[:, 3:4], power[:], ALU.pow).then_inc(s_rt, 1)

            pool.wait_ge(s_zero, NZERO)
            pool.memset(power[:], -0.5).then_inc(s_pow, 1)
            root(0)
            tile(0, 0, 0, 0, "start")
            tile(0, 1, 0, 1, "second")
            with pool.Fori(0, B // 2) as p:
                for q in range(2):
                    image_tiles(pool, 2 * p + q, q, tile)

        @block.scalar
        def _(act):
            def normalize(b, q, c):
                rows = slice(4 + 8 * c, 12 + 8 * c) if isinstance(c, int) else bass.ds(4 + 8 * c, 8)
                cols = slice(512 * c, 512 * (c + 1)) if isinstance(c, int) else bass.ds(512 * c, 512)
                act.activation(xpad[q][:, rows, 2:2 + W], xraw[:, cols].rearrange("p (r c) -> p r c", c=W),
                               ACT.Identity, bias=gs[:, 6:7], scale=gs[:, 5:6]).then_inc(s_norm, 1)

            def maps_bias(n):
                act.wait_ge(s_off, PRIME + n + 1)
                act.wait_ge(s_lo, PRIME + n)
                act.activation(om32[:], off_ps[0:OMC, :], ACT.Identity, bias=bof[:, 0:1]).then_inc(s_om, 1)

            def maps_mask(n):
                act.wait_ge(s_om, PRIME + n + 1)
                act.activation(om32[0:NMASK, :], om32[0:NMASK, :], ACT.Sigmoid).then_inc(s_sig, 1)

            def maps_high(b, q, c):
                act.wait_ge(s_cl, PRIME + NCH * b + c + 1)
                at = (4 + 8 * c) * W
                dst = om[q][0:OMC, at:at + 512] if isinstance(c, int) else om[q][0:OMC, bass.ds(at, 512)]
                act.activation(dst, om32[:], ACT.Identity).then_inc(s_hi, 1)

            def tile(b, i, q, s, kind, h=None):
                t = TILES * b + i
                for u in range(U):
                    n = U * t + u
                    act.wait_ge(s_bc, PRIME + n + 1)
                    act.wait_ge(s_hat, PRIME + n - 2)
                    act.activation(dist[u % 3][:], dist_ps[u % 2][:], ACT.Abs).then_inc(s_dist, 1)
                    k = u - 3
                    if 0 <= k < TAPS:
                        dx = 2 * (k % 3) - 2
                        act.wait_ge(s_mp, PRIME + TAPS * t + k + 1)
                        if k == 0:
                            act.wait_ge(s_val, PRIME + NP_ * (t - 1))
                        act.activation(mask[s][:, k * TR:(k + 1) * TR, 2 + dx:2 + dx + W],
                                       mask_ps[:, 0:TW].rearrange("p (r c) -> p r c", c=W), ACT.Identity).then_inc(s_mask, 1)
                    if u == 3:
                        act.wait_ge(s_pt, PRIME + 2 * t + 1)
                        act.wait_ge(s_smm, PRIME + NP_ * (t - 1))
                        act.activation(patch[s][:, 0:4, :], patch_ps[:].rearrange("p (j c) -> p j c", c=128), ACT.Identity).then_inc(s_patch, 1)
                    if u == 8:
                        act.wait_ge(s_pt, PRIME + 2 * t + 2)
                        act.activation(patch[s][:, 4, :], patch_ps[:, 0:128], ACT.Identity).then_inc(s_patch, 1)
                    if kind == "two" and u == 17:
                        act.wait_ge(s_v, 6 * (b + 1) + 6)
                        normalize(b + 1, 1 - q, 0)
                    if kind == "odd" and u == 2:
                        normalize(b + 1, 1 - q, h + 1)
                    if kind == "even":
                        if u == 14:
                            maps_bias(NCH * (b + 1) + h)
                        if u == 15:
                            maps_mask(NCH * (b + 1) + h)
                        if u == 17:
                            maps_high(b + 1, 1 - q, h)
                    if kind == "zero":
                        if u == 14:
                            maps_bias(NCH * b + NCH - 1)
                        if u == 15:
                            maps_mask(NCH * b + NCH - 1)
                        if u == 17:
                            maps_high(b, q, NCH - 1)

            act.wait_ge(s_const, 16 * NCONST)
            act.wait_ge(s_patt, 16 * 5)
            act.wait_ge(s_zero, NZERO)
            act.wait_ge(s_v, 6)
            for c in range(NCH):
                normalize(0, 0, c)
            for c in range(NCH):
                maps_bias(c)
                maps_mask(c)
                maps_high(0, 0, c)
            tile(0, 0, 0, 0, "start")
            tile(0, 1, 0, 1, "second")
            with act.Fori(0, B // 2) as p:
                for q in range(2):
                    image_tiles(act, 2 * p + q, q, tile)

        @block.vector
        def _(dve):
            def statistics(b, step):
                v = 6 * b
                if step == 0:
                    dve.wait_ge(s_x, 16 * (b + 1))
                if step < NCH:
                    ins = dve.bn_stats(stats[:, step, :], xraw[:, 512 * step:512 * (step + 1)])
                    if step == NCH - 1:
                        ins.then_inc(s_v, 1)
                if step == 8:
                    dve.wait_ge(s_v, v + 1)
                    dve.sem_inc(s_pass_v, 1)
                    dve.bn_aggr(mv[:], stats[:].rearrange("p a b -> p (a b)")).then_inc(s_v, 1)
                if step == 9:
                    dve.wait_ge(s_pg, 2 * b + 1)
                    dve.tensor_copy(gs[:, 0:1], off_ps[:, 0:1]).then_inc(s_v, 1)
                    dve.wait_ge(s_v, v + 3)
                    dve.tensor_tensor(gs[:, 1:2], mv[:, 0:1], gs[:, 0:1], ALU.subtract).then_inc(s_fx, 1)
                    dve.wait_ge(s_fx, 3 * b + 1)
                    dve.tensor_tensor(gs[:, 1:2], gs[:, 1:2], gs[:, 1:2], ALU.mult).then_inc(s_fx, 1)
                    dve.wait_ge(s_fx, 3 * b + 2)
                    dve.tensor_tensor(gs[:, 2:3], gs[:, 1:2], mv[:, 1:2], ALU.add).then_inc(s_v, 1)
                if step == 10:
                    dve.wait_ge(s_pg, 2 * b + 2)
                    dve.tensor_scalar(gs[:, 3:4], off_ps[:, 1:2], 1e-5, None, ALU.add).then_inc(s_v, 1)
                    dve.tensor_scalar(gs[:, 7:8], gs[:, 0:1], -1.0, None, ALU.mult).then_inc(s_fx, 1)
                if step == 11:
                    dve.wait_ge(s_rt, b + 1)
                    dve.wait_ge(s_fx, 3 * b + 3)
                    dve.tensor_tensor(gs[:, 6:7], gs[:, 7:8], gs[:, 5:6], ALU.mult).then_inc(s_v, 1)

            def maps_clamp(n):
                dve.wait_ge(s_sig, n + 1)
                dve.tensor_reduce(fmax[:, bass.ds(n, 1)], om32[:], AX.X, ALU.max, apply_absolute_value=True).then_inc(s_fm, 1)
                dve.wait_ge(s_fm, n + 1)
                dve.tensor_scalar(om32[:], om32[:], 256.0, -256.0, ALU.min, ALU.max).then_inc(s_cl, 1)

            def maps_low(b, q, c):
                at = (4 + 8 * c) * W
                rows = slice(at, at + 512) if isinstance(c, int) else bass.ds(at, 512)
                dve.wait_ge(s_hi, PRIME + NCH * b + c + 1)
                dve.tensor_tensor(om[q][LO:LO + OMC, rows], om32[:], om[q][0:OMC, rows], ALU.subtract).then_inc(s_lo, 1)

            def sampling(n, u, s):
                g, k = divmod(u, TAPS)
                dx = 2 * (k % 3) - 2
                dve.wait_ge(s_hat, PRIME + n + 1)
                dve.tensor_tensor(samp[s][g][:, k * TR:(k + 1) * TR, 2 + dx:2 + dx + W],
                                  hat[u % 2][:, 0:TW].rearrange("p (r c) -> p r c", c=W),
                                  hat[u % 2][:, TW:2 * TW].rearrange("p (r c) -> p r c", c=W),
                                  ALU.mult).then_inc(s_samp, 1)

            def values(t, s, m):
                j, k0, k1 = PIECES[m]
                at, n, _ = COLTILES[j]
                rows = slice(k0 * TR, k1 * TR)
                dve.wait_ge(s_mask, PRIME + TAPS * (t + 1))
                dve.wait_ge(s_smm, PRIME + NP_ * t + m + 1)
                dve.tensor_tensor(val[s][:, rows, at:at + n],
                                  val_ps[(m + s) % 2][:, 0:(k1 - k0) * TR * n].rearrange("p (r c) -> p r c", c=n),
                                  mask[s][:, rows, at:at + n], ALU.mult).then_inc(s_val, 1)

            def tile(b, i, q, s, kind, h=None):
                t = TILES * b + i
                for u in range(U):
                    n = U * t + u
                    dve.wait_ge(s_dist, PRIME + n + 1)
                    dve.wait_ge(s_samp, PRIME + n - 1)
                    dve.tensor_scalar(hat[u % 2][:], dist[u % 3][:], 1.0, -1.0, ALU.min, ALU.add).then_inc(s_hat, 1)
                    if u == 0 and kind != "start":
                        sampling(n - 1, U - 1, 1 - s)
                    if u == 0:
                        dve.wait_ge(s_smm, PRIME + NP_ * (t - 1))
                    if u > 0:
                        sampling(n - 1, u - 1, s)
                    m = VALUES_AT.get(u)
                    if m == NP_ - 1 and kind not in ("start", "second"):
                        values(t - 2, s, m)
                    elif m is not None and m < NP_ - 1 and kind != "start":
                        if m == 0:
                            dve.wait_ge(s_conv, PRIME + bands_before(b, i, kind) + CONVOLVES[kind])
                        values(t - 1, 1 - s, m)
                    if CONVOLVES[kind] and u == 9:
                        i2 = {"even": 1, "one": 1}.get(kind, 0)
                        use = BANDS // 2 * b + {"odd": h, "even": h, "zero": -1, "one": -1}[kind]
                        dve.wait_ge(s_conv, PRIME + bands_before(b, i, kind) + 1)
                        dve.wait_ge(s_bx[i2], 16 * (use + 1))
                        dve.tensor_tensor(band[i2][:], conv_ps[:, 0:TW], band[i2][:], ALU.add).then_inc(s_band, 1)
                    if kind == "two" and u < 12:
                        statistics(b + 1, u)
                    if kind == "even" and u == 16:
                        maps_clamp(NCH * (b + 1) + h)
                    if kind == "even" and u == 17:
                        maps_low(b + 1, 1 - q, h)
                    if kind == "zero" and u == 16:
                        maps_clamp(NCH * b + NCH - 1)
                    if kind == "zero" and u == 17:
                        maps_low(b, q, NCH - 1)

            dve.wait_ge(s_const, 16 * NCONST)
            dve.wait_ge(s_zero, NZERO)
            for step in range(12):
                statistics(0, step)
            for c in range(NCH):
                maps_clamp(c)
                maps_low(0, 0, c)
            tile(0, 0, 0, 0, "start")
            tile(0, 1, 0, 1, "second")
            with dve.Fori(0, B // 2) as p:
                for q in range(2):
                    image_tiles(dve, 2 * p + q, q, tile)
            dve.wait_ge(s_fm, NCH * (B + 1))
            dve.tensor_reduce(fcol[:], fmax[:], AX.X, ALU.max).then_inc(s_fl, 1)
            dve.wait_ge(s_flp, 1)
            dve.tensor_reduce(fone[:, 0:1], off_ps[0:1, 0:OMC], AX.X, ALU.max).then_inc(s_fl, 1)
            dve.wait_ge(s_fl, 2)
            dve.tensor_scalar(fone[:, 1:2], fone[:, 0:1], REACH, None, ALU.is_ge).then_inc(s_fl, 1)
            dve.wait_ge(s_fl, 3)
            dve.tensor_copy(fint[:], fone[:, 1:2]).then_inc(s_fl, 1)
            dve.wait_ge(s_fl, 4)

        @block.tensor
        def _(pe):
            def sample(t, s, m):
                j, k0, k1 = PIECES[m]
                at, n, _ = COLTILES[j]
                if m == 0:
                    pe.wait_ge(s_samp, PRIME + U * (t + 1))
                    pe.wait_ge(s_patch, PRIME + 2 * (t + 1))
                pe.wait_ge(s_val, PRIME + NP_ * t + m - 1)
                for g in range(DG):
                    ins = pe.matmul(val_ps[(m + s) % 2][g * CG:(g + 1) * CG, 0:(k1 - k0) * TR * n],
                                    patch[s][:, j, g * CG:(g + 1) * CG],
                                    samp[s][g][:, k0 * TR:k1 * TR, at:at + n], start=True, stop=True)
                ins.then_inc(s_smm, 1)

            def conv(t, s, n, k):
                dx = 2 * (k % 3) - 2
                out = conv_ps[:, 0:TW].rearrange("p (r c) -> p r c", c=W)
                cols = slice(2 + dx, 2 + dx + W)
                if k == 0:
                    pe.wait_ge(s_val, PRIME + NP_ * (t + 1))
                    pe.wait_ge(s_band, PRIME + n)
                if k < 3:
                    ins = pe.matmul(out, wcv[:, k, :], val[s][:, k * TR:(k + 1) * TR, cols], start=(k == 0), stop=False)
                elif k < 6:
                    pe.matmul(out[:, 0:2, :], wcv[:, k, :], val[s][:, k * TR + 2:(k + 1) * TR, cols], start=False, stop=False)
                    ins = pe.matmul(out[:, 2:4, :], wcv[:, k, :], val[1 - s][:, k * TR:k * TR + 2, cols], start=False, stop=False)
                else:
                    ins = pe.matmul(out, wcv[:, k, :], val[1 - s][:, k * TR:(k + 1) * TR, cols], start=False, stop=(k == 8))
                if k == 8:
                    ins.then_inc(s_conv, 1)

            def offsets(b, q, c, k):
                dy, dx = 2 * (k // 3) - 2, 2 * (k % 3) - 2
                if k == 0:
                    pe.wait_ge(s_om, PRIME + NCH * b + c)
                    if isinstance(c, int) and c == NCH - 1:
                        pe.wait_ge(s_norm, PRIME + NCH * (b + 1))
                    else:
                        pe.wait_ge(s_norm, PRIME + NCH * b + c + 2)
                at = 8 * c + dy + 4
                rows = slice(at, at + 8) if isinstance(c, int) else bass.ds(at, 8)
                ins = pe.matmul(off_ps[0:OMC, :], wof[:, k, :], xpad[q][:, rows, 2 + dx:2 + dx + W],
                                start=(k == 0), stop=(k == TAPS - 1))
                if k == TAPS - 1:
                    ins.then_inc(s_off, 1)

            def group_mean(b):
                pe.wait_ge(s_v, 6 * b + 2)
                pe.matmul(off_ps[:, 0:1], group[:], mv[:, 0:1], start=True, stop=True).then_inc(s_pg, 1)

            def group_variance(b):
                pe.wait_ge(s_v, 6 * b + 4)
                pe.matmul(off_ps[:, 1:2], group[:], gs[:, 2:3], start=True, stop=True).then_inc(s_pg, 1)

            def turn(s, j):
                dst = patch_ps[:, (j % 4) * 128:(j % 4 + 1) * 128]
                return pe.transpose(dst, strip[s][:, j].rearrange("p r c -> p (r c)"), ident[:])

            def tile(b, i, q, s, kind, h=None):
                t = TILES * b + i
                if kind in ("start", "second", "zero"):
                    pe.wait_ge(s_lo, PRIME + NCH * (b + 1) - 1)
                if kind == "two":
                    pe.wait_ge(s_lo, PRIME + NCH * (b + 1))
                for u in range(U):
                    g, k = divmod(u, TAPS)
                    dy = 2 * (k // 3) - 2
                    n = U * t + u
                    at = W * (TR * i + 2 - dy)
                    src = om[q][:, bass.ds(at, TW)]
                    pe.wait_ge(s_dist, PRIME + n - 1)
                    pe.matmul(dist_ps[u % 2][:, 0:TW], sel[:, 2 * u, :], src, start=True, stop=True)
                    pe.matmul(dist_ps[u % 2][:, TW:2 * TW], sel[:, 2 * u + 1, :], src, start=True, stop=True).then_inc(s_bc, 1)
                    k = u - 3
                    if 0 <= k < TAPS:
                        dy = 2 * (k // 3) - 2
                        pe.wait_ge(s_mask, PRIME + TAPS * t + k)
                        pe.matmul(mask_ps[:, 0:TW], sel[:, 2 * U + k, :], om[q][:, bass.ds(W * (TR * i + 2 - dy), TW)],
                                  start=True, stop=True).then_inc(s_mp, 1)
                    if u == 1:
                        pe.wait_ge(s_patch, PRIME + 2 * t)
                        pe.wait_ge(s_strip, PRIME + t + 1)
                        for j in range(4):
                            ins = turn(s, j)
                        ins.then_inc(s_pt, 1)
                    if u == 6:
                        pe.wait_ge(s_patch, PRIME + 2 * t + 1)
                        turn(s, 4).then_inc(s_pt, 1)
                    if CONVOLVES[kind] and 3 <= u < 8:
                        for k in range(2 * (u - 3), min(2 * (u - 3) + 2, TAPS)):
                            conv(t - 2, 1 - s, bands_before(b, i, kind), k)
                    if kind != "start" and u in SAMPLES_AT:
                        sample(t - 1, 1 - s, SAMPLES_AT[u])
                    if kind == "two" and u == 10:
                        group_mean(b + 1)
                    if kind == "two" and u == 12:
                        group_variance(b + 1)
                    if kind == "odd" and u in (8, 10, 12, 14, 16):
                        offsets(b + 1, 1 - q, h, (u - 8) // 2)
                    if kind == "even" and u in (8, 9, 10, 12):
                        offsets(b + 1, 1 - q, h, {8: 5, 9: 6, 10: 7, 12: 8}[u])
                    if kind == "zero" and 4 <= u < 13:
                        offsets(b, q, NCH - 1, u - 4)

            pe.wait_ge(s_const, 16 * NCONST)
            pe.wait_ge(s_patt, 16 * 5)
            group_mean(0)
            group_variance(0)
            pe.wait_ge(s_v, 5)
            for c in range(NCH):
                for k in range(TAPS):
                    offsets(0, 0, c, k)
            tile(0, 0, 0, 0, "start")
            tile(0, 1, 0, 1, "second")
            with pe.Fori(0, B // 2) as p:
                for q in range(2):
                    image_tiles(pe, 2 * p + q, q, tile)
            pe.wait_ge(s_fl, 1)
            pe.transpose(off_ps[0:1, 0:OMC], fcol[:], ident[0:OMC, 0:OMC]).then_inc(s_flp, 1)

GK = 128


def constants_general():
    sel = np.zeros((GK, TAPS, 2 * DG + 1, 128), np.float32)
    col = np.arange(128) % W
    for k in range(TAPS):
        dy, dx = 2 * (k // 3) - 2, 2 * (k % 3) - 2
        for g in range(DG):
            row = NMASK + (g * TAPS + k) * 2
            sel[row, k, 2 * g] = sel[PATT, k, 2 * g] = 1
            sel[PATT + 2, k, 2 * g] = dy
            sel[row + 1, k, 2 * g + 1] = sel[PATT + 1, k, 2 * g + 1] = 1
            sel[PATT + 2, k, 2 * g + 1] = dx - col
            sel[g * TAPS + k, k, 2 * DG, g * CG:(g + 1) * CG] = 2
    pos = np.zeros((3, H, W), np.float32)
    pos[0], pos[1], pos[2] = np.arange(H)[:, None], np.arange(W), 1
    rows = -(2 * np.arange(H // 2) + (np.arange(128) // W)[:, None]).astype(np.float32)
    return {"c_gsel": sel, "c_gpos": pos.reshape(3, PIX), "c_grow": rows}


def build_general(nc, fint, x, woff, boff, wconv, c_gsel, c_gpos, c_grow, c_group, c_ident, x1, B):
    PAIRS = H // 2
    with ExitStack() as ctx:
        sb = lambda n, s, d=F32: ctx.enter_context(nc.sbuf_tensor(n, s, d))
        ps = lambda n: ctx.enter_context(nc.psum_tensor(n, [128, 512], F32))
        sem = lambda n: ctx.enter_context(nc.semaphore(n))
        xraw, xn, xt = sb("g_xraw", [128, PIX]), sb("g_xn", [128, PIX]), sb("g_xt", [128, PAIRS, C])
        xpad = sb("g_xpad", [128, XR, XCOLS])
        om = sb("g_om", [GK, PIX])
        sel, selk = sb("g_sel", [GK, TAPS, 2 * DG + 1, 128]), sb("g_selk", [GK, 2 * DG + 1, 128])
        wof, bof = sb("g_wof", [128, TAPS, OMC]), sb("g_bof", [OMC, 1])
        wcv, wck = sb("g_wcv", [128, TAPS, 128]), sb("g_wck", [128, 128])
        group, ident, rows = sb("g_group", [128, 128]), sb("g_ident", [128, 128]), sb("g_rows", [128, PAIRS])
        stats, mv, gs = sb("g_stats", [128, NCH, 6]), sb("g_mv", [128, 2]), sb("g_gs", [128, 8])
        ypos, xdist, xhat = sb("g_ypos", [128, 512]), sb("g_xdist", [128, 512]), sb("g_xhat", [128, 512])
        ydist, yhat, samp = ([sb(f"g_{n}{i}", [128, 512]) for i in range(2)] for n in ("ydist", "yhat", "samp"))
        mask, val = sb("g_mask", [128, 512]), sb("g_val", [128, 512])
        y_ps, x_ps, m_ps, v_ps, c_ps, t_ps = (ps(f"g_{n}_ps") for n in "yxmvct")

        s_const, s_zero, s_patt = sem("g_const_loaded"), sem("g_zeroed"), sem("g_patterns_loaded")
        s_x, s_st, s_pass_v = sem("g_x_loaded"), sem("g_x1_stored"), sem("g_passed_vector")
        s_v, s_pg, s_rt, s_xpad, s_xn = sem("g_stat_step"), sem("g_group_ready"), sem("g_root_ready"), sem("g_padded"), sem("g_normalized")
        s_tp, s_xt = sem("g_turned"), sem("g_turned_copied")
        s_off, s_om, s_sig, s_cl = sem("g_offset_conv_done"), sem("g_maps_biased"), sem("g_masks_ready"), sem("g_maps_clamped")
        s_tap, s_pos, s_yp, s_xd, s_xh = sem("g_tap_operands"), sem("g_positions_spread"), sem("g_rows_copied"), sem("g_column_distance"), sem("g_column_hat")
        s_yd, s_yh, s_s, s_mm = sem("g_row_distance"), sem("g_row_hat"), sem("g_sampling_ready"), sem("g_sampled")
        s_mp, s_mask, s_val, s_conv, s_acc = sem("g_mask_spread"), sem("g_mask_ready"), sem("g_values_ready"), sem("g_conv_done"), sem("g_added")
        block = ctx.enter_context(nc.Block())

        @block.sync
        def _(sp):
            flag = sp.value_load(fint[0:1, 0:1], min_val=0, max_val=1)
            with sp.If(flag == 1):
                for s in (s_st, s_conv, s_val, s_yd, s_xh, s_yh, s_s, s_mm, s_pos, s_mp, s_acc, s_xn, s_xt, s_om, s_mask, s_yp, s_xd):
                    sp.sem_inc(s, PRIME)
                for dst, src in ((sel, c_gsel), (group, c_group), (ident, c_ident), (rows, c_grow), (wcv, wconv)):
                    sp.dma_start(dst[:], src).then_inc(s_const, 16)
                sp.dma_start(bof[0:NMASK, :], boff[2 * NMASK:OMC, :]).then_inc(s_const, 16)
                sp.dma_start(bof[NMASK:OMC, :], boff[0:2 * NMASK, :]).then_inc(s_const, 16)
                sp.wait_ge(s_zero, 3)
                sp.dma_start(om[PATT:PATT + 3, :], c_gpos).then_inc(s_patt, 16)
                sp.dma_start(wof[0:CG, :, NMASK:NMASK + 27], woff[:, :, 0:27]).then_inc(s_patt, 16)
                sp.dma_start(wof[CG:C, :, NMASK + 27:OMC], woff[:, :, 27:36]).then_inc(s_patt, 16)
                sp.dma_start(wof[CG:C, :, 0:NMASK], woff[:, :, 36:54]).then_inc(s_patt, 16)
                with sp.Fori(0, B) as b:
                    sp.wait_ge(s_st, PRIME + 16 * b)
                    sp.dma_start(xraw[:], x[bass.ds(b, 1), :, :].rearrange("a c p -> c (a p)")).then_inc(s_x, 16)
                    sp.wait_ge(s_acc, PRIME + NCH * TAPS * (b + 1))
                    sp.dma_start(x1[bass.ds(b, 1), :, :].rearrange("a c p -> c (a p)"), xraw[:]).then_inc(s_st, 16)
                sp.wait_ge(s_st, PRIME + 16 * B)

        @block.gpsimd
        def _(pool):
            flag = pool.value_load(fint[0:1, 0:1], min_val=0, max_val=1)
            with pool.If(flag == 1):
                pool.memset(wof[:], 0.0).then_inc(s_zero, 1)
                pool.memset(om[:], 0.0).then_inc(s_zero, 1)
                pool.memset(xpad[:], 0.0).then_inc(s_zero, 1)

        @block.scalar
        def _(act):
            flag = act.value_load(fint[0:1, 0:1], min_val=0, max_val=1)
            with act.If(flag == 1):
                act.wait_ge(s_const, 16 * 7)
                act.wait_ge(s_zero, 3)
                with act.Fori(0, B) as b:
                    act.wait_ge(s_v, 9 * b + 6)
                    act.activation(gs[:, 4:5], gs[:, 3:4], ACT.Sqrt).then_inc(s_rt, 1)
                    act.wait_ge(s_v, 9 * b + 9)
                    act.wait_ge(s_conv, PRIME + NCH * TAPS * b)
                    for q in range(NCH):
                        act.activation(xpad[:, 4 + 8 * q:12 + 8 * q, 2:2 + W],
                                       xraw[:, 512 * q:512 * (q + 1)].rearrange("p (r c) -> p r c", c=W),
                                       ACT.Identity, bias=gs[:, 6:7], scale=gs[:, 5:6]).then_inc(s_xpad, 1)
                        act.activation(xn[:, 512 * q:512 * (q + 1)], xraw[:, 512 * q:512 * (q + 1)],
                                       ACT.Identity, bias=gs[:, 6:7], scale=gs[:, 5:6]).then_inc(s_xn, 1)
                    for q in range(NCH):
                        act.wait_ge(s_tp, NCH * b + q + 1)
                        act.activation(xt[:, 4 * q:4 * q + 4, :], t_ps[:].rearrange("p (m c) -> p m c", c=C), ACT.Identity).then_inc(s_xt, 1)
                    for q in range(NCH):
                        n = NCH * b + q
                        act.wait_ge(s_off, n + 1)
                        part = om[0:OMC, 512 * q:512 * (q + 1)]
                        act.activation(part, t_ps[0:OMC, :], ACT.Identity, bias=bof[:, 0:1]).then_inc(s_om, 1)
                        act.wait_ge(s_om, PRIME + n + 1)
                        part = om[0:NMASK, 512 * q:512 * (q + 1)]
                        act.activation(part, part, ACT.Sigmoid).then_inc(s_sig, 1)
                    with act.Fori(0, NCH) as q:
                        with act.Fori(0, TAPS) as k:
                            e = (NCH * b + q) * TAPS + k
                            act.wait_ge(s_mp, PRIME + e + 1)
                            act.wait_ge(s_val, PRIME + e)
                            act.activation(mask[:], m_ps[:], ACT.Identity).then_inc(s_mask, 1)
                            for g in range(DG):
                                act.wait_ge(s_pos, PRIME + DG * e + g + 1)
                                act.wait_ge(s_yd, PRIME + PAIRS * (DG * e + g))
                                act.wait_ge(s_xh, PRIME + DG * e + g)
                                act.activation(ypos[:], y_ps[:], ACT.Identity).then_inc(s_yp, 1)
                                act.activation(xdist[:], x_ps[:], ACT.Abs).then_inc(s_xd, 1)
                                act.wait_ge(s_yp, PRIME + DG * e + g + 1)
                                for n in range(PAIRS):
                                    m = PAIRS * (DG * e + g) + n
                                    act.wait_ge(s_yh, PRIME + (m - 1 if n >= 2 else PAIRS * (DG * e + g)))
                                    act.activation(ydist[n % 2][:], ypos[:], ACT.Abs, bias=rows[:, n:n + 1]).then_inc(s_yd, 1)

        @block.vector
        def _(dve):
            flag = dve.value_load(fint[0:1, 0:1], min_val=0, max_val=1)
            with dve.If(flag == 1):
                dve.wait_ge(s_const, 16 * 7)
                dve.wait_ge(s_zero, 3)
                with dve.Fori(0, B) as b:
                    v = 9 * b
                    dve.wait_ge(s_x, 16 * (b + 1))
                    for q in range(NCH):
                        ins = dve.bn_stats(stats[:, q, :], xraw[:, 512 * q:512 * (q + 1)])
                    ins.then_inc(s_v, 1)
                    dve.wait_ge(s_v, v + 1)
                    dve.sem_inc(s_pass_v, 1)
                    dve.bn_aggr(mv[:], stats[:].rearrange("p a b -> p (a b)")).then_inc(s_v, 1)
                    dve.wait_ge(s_pg, 2 * b + 1)
                    dve.tensor_copy(gs[:, 0:1], t_ps[:, 0:1]).then_inc(s_v, 1)
                    dve.wait_ge(s_v, v + 3)
                    dve.tensor_tensor(gs[:, 1:2], mv[:, 0:1], gs[:, 0:1], ALU.subtract).then_inc(s_v, 1)
                    dve.wait_ge(s_v, v + 4)
                    dve.scalar_tensor_tensor(gs[:, 2:3], gs[:, 1:2], gs[:, 1:2], mv[:, 1:2], ALU.mult, ALU.add).then_inc(s_v, 1)
                    dve.wait_ge(s_pg, 2 * b + 2)
                    dve.tensor_scalar(gs[:, 3:4], t_ps[:, 1:2], 1e-5, None, ALU.add).then_inc(s_v, 1)
                    dve.wait_ge(s_rt, b + 1)
                    dve.wait_ge(s_xn, PRIME + NCH * b)
                    dve.reciprocal(gs[:, 5:6], gs[:, 4:5]).then_inc(s_v, 1)
                    dve.tensor_scalar(gs[:, 7:8], gs[:, 0:1], -1.0, None, ALU.mult).then_inc(s_v, 1)
                    dve.wait_ge(s_v, v + 8)
                    dve.tensor_tensor(gs[:, 6:7], gs[:, 7:8], gs[:, 5:6], ALU.mult).then_inc(s_v, 1)
                    for q in range(NCH):
                        n = NCH * b + q
                        dve.wait_ge(s_sig, n + 1)
                        part = om[0:OMC, 512 * q:512 * (q + 1)]
                        dve.tensor_scalar(part, part, 256.0, -256.0, ALU.min, ALU.max).then_inc(s_cl, 1)
                    with dve.Fori(0, NCH) as q:
                        with dve.Fori(0, TAPS) as k:
                            e = (NCH * b + q) * TAPS + k
                            dve.wait_ge(s_conv, PRIME + e)
                            dve.wait_ge(s_pos, PRIME + DG * e)
                            dve.wait_ge(s_mp, PRIME + e)
                            dve.tensor_copy(selk[:], sel[:, bass.ds(k, 1), :, :].rearrange("p a s q -> p (a s) q")).then_inc(s_tap, 1)
                            dve.tensor_copy(wck[:], wcv[:, bass.ds(k, 1), :].rearrange("p a o -> p (a o)")).then_inc(s_tap, 1)
                            for g in range(DG):
                                dve.wait_ge(s_xd, PRIME + DG * e + g + 1)
                                dve.wait_ge(s_s, PRIME + PAIRS * (DG * e + g))
                                dve.tensor_scalar(xhat[:], xdist[:], 1.0, -1.0, ALU.min, ALU.add).then_inc(s_xh, 1)
                                dve.wait_ge(s_xh, PRIME + DG * e + g + 1)
                                for n in range(PAIRS):
                                    m = PAIRS * (DG * e + g) + n
                                    dve.wait_ge(s_yd, PRIME + m + 1)
                                    dve.wait_ge(s_s, PRIME + (m - 1 if n >= 2 else PAIRS * (DG * e + g)))
                                    dve.tensor_scalar(yhat[n % 2][:], ydist[n % 2][:], 1.0, -1.0, ALU.min, ALU.add).then_inc(s_yh, 1)
                                    dve.wait_ge(s_yh, PRIME + m + 1)
                                    dve.wait_ge(s_mm, PRIME + (m - 1 if n >= 2 else PAIRS * (DG * e + g)))
                                    dve.tensor_tensor(samp[n % 2][:], xhat[:], yhat[n % 2][:], ALU.mult).then_inc(s_s, 1)
                            dve.wait_ge(s_mm, PRIME + PAIRS * DG * (e + 1))
                            dve.wait_ge(s_mask, PRIME + e + 1)
                            dve.tensor_tensor(val[:], v_ps[:], mask[:], ALU.mult).then_inc(s_val, 1)
                            dve.wait_ge(s_conv, PRIME + e + 1)
                            dve.wait_ge(s_acc, PRIME + e)
                            dst = xraw[:, bass.ds(512 * q, 512)]
                            dve.tensor_tensor(dst, c_ps[:], dst, ALU.add).then_inc(s_acc, 1)

        @block.tensor
        def _(pe):
            flag = pe.value_load(fint[0:1, 0:1], min_val=0, max_val=1)
            with pe.If(flag == 1):
                pe.wait_ge(s_const, 16 * 7)
                pe.wait_ge(s_patt, 16 * 4)
                with pe.Fori(0, B) as b:
                    pe.wait_ge(s_v, 9 * b + 2)
                    pe.matmul(t_ps[:, 0:1], group[:], mv[:, 0:1], start=True, stop=True).then_inc(s_pg, 1)
                    pe.wait_ge(s_v, 9 * b + 5)
                    pe.matmul(t_ps[:, 1:2], group[:], gs[:, 2:3], start=True, stop=True).then_inc(s_pg, 1)
                    pe.wait_ge(s_v, 9 * b + 6)
                    for q in range(NCH):
                        pe.wait_ge(s_xn, PRIME + NCH * b + q + 1)
                        pe.wait_ge(s_xt, PRIME + NCH * b + q)
                        for m in range(4):
                            ins = pe.transpose(t_ps[:, 128 * m:128 * m + 128], xn[:, 512 * q + 128 * m:512 * q + 128 * m + 128], ident[:])
                        ins.then_inc(s_tp, 1)
                    pe.wait_ge(s_xpad, NCH * (b + 1))
                    pe.wait_ge(s_xt, PRIME + NCH * (b + 1))
                    for q in range(NCH):
                        pe.wait_ge(s_om, PRIME + NCH * b + q)
                        for k in range(TAPS):
                            dy, dx = 2 * (k // 3) - 2, 2 * (k % 3) - 2
                            ins = pe.matmul(t_ps[0:OMC, :], wof[:, k, :],
                                            xpad[:, 8 * q + dy + 4:8 * q + dy + 12, 2 + dx:2 + dx + W],
                                            start=(k == 0), stop=(k == TAPS - 1))
                        ins.then_inc(s_off, 1)
                    with pe.Fori(0, NCH) as q:
                        with pe.Fori(0, TAPS) as k:
                            pe.wait_ge(s_cl, NCH * (b + 1))
                            e = (NCH * b + q) * TAPS + k
                            src = om[:, bass.ds(512 * q, 512)]
                            pe.wait_ge(s_tap, 2 * (e + 1))
                            pe.wait_ge(s_mask, PRIME + e)
                            pe.matmul(m_ps[:], selk[:, 2 * DG, :], src, start=True, stop=True).then_inc(s_mp, 1)
                            for g in range(DG):
                                pe.wait_ge(s_yp, PRIME + DG * e + g)
                                pe.wait_ge(s_xd, PRIME + DG * e + g)
                                pe.matmul(y_ps[:], selk[:, 2 * g, :], src, start=True, stop=True)
                                pe.matmul(x_ps[:], selk[:, 2 * g + 1, :], src, start=True, stop=True).then_inc(s_pos, 1)
                                pe.wait_ge(s_val, PRIME + e)
                                for n in range(PAIRS):
                                    m = PAIRS * (DG * e + g) + n
                                    pe.wait_ge(s_s, PRIME + m + 1)
                                    pe.matmul(v_ps[g * CG:(g + 1) * CG, :], xt[:, n, g * CG:(g + 1) * CG], samp[n % 2][:],
                                              start=(n == 0), stop=(n == PAIRS - 1)).then_inc(s_mm, 1)
                            pe.wait_ge(s_val, PRIME + e + 1)
                            pe.wait_ge(s_acc, PRIME + e)
                            pe.matmul(c_ps[:], wck[:], val[:], start=True, stop=True).then_inc(s_conv, 1)

KX, KY = H, W // 2
ROWS2 = H // 2
CT = 4
KQ = KY // CT


def constants_l1():
    w, ky, h, kx = np.arange(W), np.arange(KY), np.arange(H), np.arange(KX)
    a = 2 * np.pi * np.outer(w, ky) / W
    fw = np.zeros((2, W, 2, 2, KY))
    for i in range(2):
        fw[i, :, i, 0], fw[i, :, i, 1] = np.cos(a), -np.sin(a)
    b = 2 * np.pi * np.outer(h, kx) / H
    fh = np.zeros((H, 2, 2, KX))
    fh[:, 0, 0], fh[:, 1, 0], fh[:, 0, 1], fh[:, 1, 1] = np.cos(b), np.sin(b), -np.sin(b), np.cos(b)
    fh /= PIX
    c = b.T
    ih = np.zeros((KX, 2, H, 2))
    ih[:, 0, :, 0], ih[:, 1, :, 0], ih[:, 0, :, 1], ih[:, 1, :, 1] = np.cos(c), -np.sin(c), np.sin(c), np.cos(c)
    iw = np.zeros((2, 2, KY, 2, W))
    for n in range(KY):
        k = CT * (n % KQ) + n // KQ
        d = 2 * np.pi * k * w / W
        for i in range(2):
            iw[i, 0, n, i] = np.cos(d) * (1 if k == 0 else 2)
            iw[i, 1, n, i] = -np.sin(d) * (0 if k == 0 else 2)
    f = lambda m: np.ascontiguousarray(m.reshape(128, 128).astype(np.float32))
    same = (np.arange(C)[:, None] // 4 == np.arange(C) // 4)
    return {"c_fw": f(fw), "c_fh": f(fh), "c_ih": f(ih), "c_iw": f(iw)}


def build_l1(nc, x1, wspec, c_fw, c_fh, c_ih, c_iw, c_group, c_ident, out, B=8):
    f1 = nc.dram_tensor("f1_scratch", [B, H, 2, KY, C], F32, kind="Internal").ap()
    ysp = nc.dram_tensor("y_scratch", [B, KX, 2, KY, C], F32, kind="Internal").ap()
    gsp = nc.dram_tensor("g_scratch", [B, H, 2, KY, C], F32, kind="Internal").ap()
    with ExitStack() as keep:
        norm = keep.enter_context(nc.sbuf_tensor("norm", [128, 2, B], F32))
        forward_columns(nc, x1, f1, c_fw, c_group, c_ident, norm, B)
        with nc.sbuf_tensor("spec", [128, KX, KY, 2, B], F32) as spec:
            forward_rows(nc, f1, c_fh, norm, spec, B)
            mix_modes(nc, spec, wspec, ysp, B)
    inverse_rows(nc, ysp, gsp, c_ih, B)
    inverse_columns(nc, gsp, x1, out, c_iw, B)


def forward_columns(nc, x1, f1, c_fw, c_group, c_ident, norm, B):
    with ExitStack() as ctx:
        sb = lambda n, s: ctx.enter_context(nc.sbuf_tensor(n, s, F32))
        ps = lambda n: ctx.enter_context(nc.psum_tensor(n, [128, 512], F32))
        sem = lambda n: ctx.enter_context(nc.semaphore(n))
        fw, group, ident = sb("fw", [128, 128]), sb("group1", [128, 128]), sb("ident1", [128, 128])
        xin = [sb(f"xin{i}", [128, PIX]) for i in range(2)]
        xt = [sb(f"xt{i}", [128, 512]) for i in range(2)]
        fo = [sb(f"fo{i}", [128, ROWS2, C]) for i in range(2)]
        stats, mv, gs = sb("stats1", [128, NCH, 6]), sb("mv1", [128, 2]), sb("gs1", [128, 6])
        t_ps = [ps(f"t_ps{i}") for i in range(2)]
        f_ps = [ps(f"f_ps{i}") for i in range(2)]
        g_ps = ps("g_ps")
        s_const, s_x, s_st = sem("fc_const"), [sem(f"fc_x{i}") for i in range(2)], [sem(f"fc_stored{i}") for i in range(2)]
        s_v, s_pg, s_rt, s_nm = sem("fc_stat_step"), sem("fc_group"), sem("fc_root"), sem("fc_norm")
        s_fx = sem("fc_stat_small")
        s_pass_v, s_pass_s = sem("fc_passed_vector"), sem("fc_passed_sync")
        s_tp, s_xt, s_f, s_fo = sem("fc_turned"), sem("fc_turned_copied"), sem("fc_transformed"), sem("fc_copied")
        block = ctx.enter_context(nc.Block())

        @block.sync
        def _(sp):
            for s in (s_fo, s_f, *s_st, s_xt):
                sp.sem_inc(s, PRIME)
            sp.dma_start(fw[:], c_fw).then_inc(s_const, 16)
            sp.dma_start(group[:], c_group).then_inc(s_const, 16)
            sp.dma_start(ident[:], c_ident).then_inc(s_const, 16)
            with sp.Fori(0, B // 2) as h:
                for i in range(2):
                    b = 2 * h + i
                    sp.wait_ge(s_fo, PRIME + NCH * (b + 1))
                    sp.dma_start(f1[bass.ds(b, 1), :, :, :, :].rearrange("a (m t) r k c -> (t r k) (a m) c", t=2),
                                   fo[i][:]).then_inc(s_st[i], 16)
            for i in range(2):
                sp.wait_ge(s_st[i], PRIME + 16 * (B // 2))

        @block.gpsimd
        def _(pool):
            with pool.Fori(0, B // 2) as h:
                for i in range(2):
                    b = 2 * h + i
                    pool.wait_ge(s_fo, PRIME + NCH * (b - 1))
                    pool.sem_inc(s_pass_s, 1)
                    pool.dma_start(xin[i][:], x1[bass.ds(b, 1), :, :].rearrange("a c p -> c (a p)")).then_inc(s_x[i], 16)

        @block.scalar
        def _(act):
            with act.Fori(0, B // 2) as h:
                for i in range(2):
                    b = 2 * h + i
                    for q in range(NCH):
                        n = NCH * b + q
                        act.wait_ge(s_tp, n + 1)
                        if q >= 2:
                            act.wait_ge(s_f, PRIME + n - 1)
                        else:
                            act.wait_ge(s_f, PRIME + NCH * b)
                        act.activation(xt[q % 2][:], t_ps[q % 2][:], ACT.Identity).then_inc(s_xt, 1)
                    act.wait_ge(s_v, 5 * b + 5)
                    act.activation(gs[:, 4:5], gs[:, 3:4], ACT.Sqrt).then_inc(s_rt, 1)

        @block.vector
        def _(dve):
            def copy_out(i, h, b, q):
                n = NCH * b + q
                dve.wait_ge(s_f, PRIME + n + 1)
                if q == 0:
                    dve.wait_ge(s_st[i], PRIME + 16 * h)
                dve.tensor_copy(fo[i][:, 4 * q:4 * q + 4, :], f_ps[q % 2][:].rearrange("p (m c) -> p m c", c=C)).then_inc(s_fo, 1)

            with dve.Fori(0, B // 2) as h:
                for i in range(2):
                    b = 2 * h + i
                    v = 5 * b
                    dve.wait_ge(s_x[i], 16 * (h + 1))
                    for q in range(NCH):
                        ins = dve.bn_stats(stats[:, q, :], xin[i][:, 512 * q:512 * (q + 1)])
                    ins.then_inc(s_v, 1)
                    dve.wait_ge(s_v, v + 1)
                    dve.sem_inc(s_pass_v, 1)
                    dve.bn_aggr(mv[:], stats[:].rearrange("p a b -> p (a b)")).then_inc(s_v, 1)
                    dve.wait_ge(s_pg, 2 * b + 1)
                    dve.tensor_copy(gs[:, 0:1], g_ps[:, 0:1]).then_inc(s_v, 1)
                    dve.wait_ge(s_v, v + 3)
                    dve.tensor_tensor(gs[:, 1:2], mv[:, 0:1], gs[:, 0:1], ALU.subtract).then_inc(s_fx, 1)
                    dve.wait_ge(s_fx, 3 * b + 1)
                    dve.tensor_tensor(gs[:, 1:2], gs[:, 1:2], gs[:, 1:2], ALU.mult).then_inc(s_fx, 1)
                    dve.wait_ge(s_fx, 3 * b + 2)
                    dve.tensor_tensor(gs[:, 2:3], gs[:, 1:2], mv[:, 1:2], ALU.add).then_inc(s_v, 1)
                    dve.wait_ge(s_pg, 2 * b + 2)
                    dve.tensor_scalar(gs[:, 3:4], g_ps[:, 1:2], 1e-5, None, ALU.add).then_inc(s_v, 1)
                    dve.tensor_copy(norm[:, 1, bass.ds(b, 1)], gs[:, 0:1]).then_inc(s_fx, 1)
                    for q in range(NCH):
                        copy_out(i, h, b, q)
                    dve.wait_ge(s_rt, b + 1)
                    dve.wait_ge(s_fx, 3 * b + 3)
                    dve.reciprocal(norm[:, 0, bass.ds(b, 1)], gs[:, 4:5]).then_inc(s_nm, 1)


        @block.tensor
        def _(pe):
            def turn(i, b, q):
                if q >= 2:
                    pe.wait_ge(s_xt, PRIME + NCH * b + q - 1)
                for m in range(4):
                    ins = pe.transpose(t_ps[q % 2][:, m * 128:(m + 1) * 128],
                                       xin[i][:, (4 * q + m) * 128:(4 * q + m + 1) * 128], ident[:])
                ins.then_inc(s_tp, 1)

            pe.wait_ge(s_const, 48)
            with pe.Fori(0, B // 2) as h:
                for i in range(2):
                    b = 2 * h + i
                    pe.wait_ge(s_x[i], 16 * (h + 1))
                    pe.wait_ge(s_xt, PRIME + NCH * b)
                    turn(i, b, 0)
                    pe.wait_ge(s_v, 5 * b + 2)
                    pe.matmul(g_ps[:, 0:1], group[:], mv[:, 0:1], start=True, stop=True).then_inc(s_pg, 1)
                    turn(i, b, 1)
                    pe.wait_ge(s_v, 5 * b + 4)
                    pe.matmul(g_ps[:, 1:2], group[:], gs[:, 2:3], start=True, stop=True).then_inc(s_pg, 1)
                    for q in range(NCH):
                        n = NCH * b + q
                        pe.wait_ge(s_xt, PRIME + n + 1)
                        if q >= 2:
                            pe.wait_ge(s_fo, PRIME + n - 1)
                        else:
                            pe.wait_ge(s_fo, PRIME + NCH * b)
                        pe.matmul(f_ps[q % 2][:], fw[:], xt[q % 2][:], start=True, stop=True).then_inc(s_f, 1)
                        if q + 2 < NCH:
                            turn(i, b, q + 2)


def forward_rows(nc, f1, c_fh, norm, spec, B):
    G = KY // 4
    with ExitStack() as ctx:
        sb = lambda n, s: ctx.enter_context(nc.sbuf_tensor(n, s, F32))
        sem = lambda n: ctx.enter_context(nc.semaphore(n))
        fh = sb("fh", [128, 128])
        fin = [sb(f"fin{i}", [128, KY, C]) for i in range(2)]
        ps = [ctx.enter_context(nc.psum_tensor(f"r_ps{i}", [128, 512], F32)) for i in range(4)]
        s_const, s_f = sem("fr_const"), [sem(f"fr_in{i}") for i in range(2)]
        s_r, s_a, s_d, s_dc = sem("fr_transformed"), sem("fr_by_scalar"), sem("fr_by_vector"), sem("fr_dc")
        block = ctx.enter_context(nc.Block())

        def place(b, g):
            return spec[:, :, 4 * g:4 * g + 4, :, bass.ds(b, 1)].rearrange("p x y r a -> p y r (x a)")

        @block.sync
        def _(sp):
            for s in (s_r, s_a, s_d):
                sp.sem_inc(s, PRIME)
            sp.dma_start(fh[:], c_fh).then_inc(s_const, 16)
            with sp.Fori(0, B // 2) as h:
                for i in range(2):
                    sp.wait_ge(s_r, PRIME + G * (2 * h + i - 1))
                    sp.dma_start(fin[i][:], f1[bass.ds(2 * h + i, 1), :, :, :, :].rearrange("a h r k c -> (a h r) k c")).then_inc(s_f[i], 16)

        @block.tensor
        def _(pe):
            pe.wait_ge(s_const, 16)
            with pe.Fori(0, B // 2) as h:
                for i in range(2):
                    b = 2 * h + i
                    pe.wait_ge(s_f[i], 16 * (h + 1))
                    for g in range(G):
                        done, n = (s_a, G // 2 * b + g // 2) if g % 2 == 0 else (s_d, G // 2 * b + g // 2)
                        if g >= 4:
                            pe.wait_ge(done, PRIME + n - 1)
                        else:
                            pe.wait_ge(done, PRIME + G // 2 * b)
                        for y in range(4):
                            ins = pe.matmul(ps[g % 4][:, 128 * y:128 * y + 128], fin[i][:, 4 * g + y, :], fh[:], start=True, stop=True)
                        ins.then_inc(s_r, 1)

        @block.scalar
        def _(act):
            with act.Fori(0, B // 2) as h:
                for i in range(2):
                    b = 2 * h + i
                    for g in range(0, G, 2):
                        act.wait_ge(s_r, PRIME + G * b + g + 1)
                        act.activation(place(b, g), ps[g % 4][:].rearrange("p (y r x) -> p y r x", y=4, r=2), ACT.Identity,
                                       scale=norm[:, 0, bass.ds(b, 1)]).then_inc(s_a, 1)

        @block.vector
        def _(dve):
            with dve.Fori(0, B // 2) as h:
                for i in range(2):
                    b = 2 * h + i
                    for g in range(1, G, 2):
                        dve.wait_ge(s_r, PRIME + G * b + g + 1)
                        dve.tensor_scalar(place(b, g), ps[g % 4][:].rearrange("p (y r x) -> p y r x", y=4, r=2),
                                          norm[:, 0, bass.ds(b, 1)], None, ALU.mult).then_inc(s_d, 1)
            dve.tensor_tensor(norm[:, 1, :], norm[:, 1, :], norm[:, 0, :], ALU.mult).then_inc(s_dc, 1)
            dve.wait_ge(s_dc, 1)
            dve.wait_ge(s_a, PRIME + G // 2 * B)
            dve.tensor_tensor(spec[:, 0, 0, 0, :], spec[:, 0, 0, 0, :], norm[:, 1, :], ALU.subtract).then_inc(s_dc, 1)


def mix_modes(nc, spec, wspec, ysp, B):
    P2 = 2 * B
    with ExitStack() as ctx:
        sb = lambda n, s: ctx.enter_context(nc.sbuf_tensor(n, s, F32))
        sem = lambda n: ctx.enter_context(nc.semaphore(n))
        wt = [sb(f"wt{i}", [128, 2, KY, C]) for i in range(2)]
        xs = [sb(f"xs{i}", [128, KY, 3 * B]) for i in range(2)]
        ys = [sb(f"ys{i}", [128, KQ, C]) for i in range(2)]
        ps = [ctx.enter_context(nc.psum_tensor(f"m_ps{i}", [128, 512], F32)) for i in range(4)]
        s_w = [[sem(f"mm_weights{i}{r}") for r in range(2)] for i in range(2)]
        s_zero, s_xs, s_mm, s_y = sem("mm_zeroed"), sem("mm_operand"), sem("mm_mixed"), sem("mm_copied")
        s_st = [sem(f"mm_stored{i}") for i in range(2)]
        block = ctx.enter_context(nc.Block())

        @block.sync
        def _(sp):
            for s in (s_mm, *s_st, s_y):
                sp.sem_inc(s, PRIME)
            with sp.Fori(0, KX // 2) as h:
                for i in range(2):
                    k = 2 * h + i
                    sp.wait_ge(s_mm, PRIME + 2 * (k - 1))
                    for r in range(2):
                        sp.dma_start(wt[i][:, r, :, :], wspec[bass.ds(k, 1), r, :, :, :].rearrange("a i y o -> i (a y) o")).then_inc(s_w[i][r], 16)

        @block.scalar
        def _(act):
            with act.Fori(0, KX // 2) as h:
                for i in range(2):
                    k = 2 * h + i
                    act.wait_ge(s_y, PRIME + 2 * (k + 1))
                    for j in range(CT):
                        act.dma_start(ysp[:, bass.ds(k, 1), :, KQ * j:KQ * (j + 1), :].rearrange("b a r q o -> (a r) b (q o)"),
                                      ys[i][32 * j:32 * j + P2, :, :].rearrange("p q o -> p (q o)")).then_inc(s_st[i], 16)
            for i in range(2):
                act.wait_ge(s_st[i], PRIME + 16 * CT * (KX // 2))

        @block.vector
        def _(dve):
            for p in ps:
                ins = dve.memset(p[:], 0.0)
            ins.then_inc(s_zero, 1)
            dve.wait_ge(s_zero, 1)

            def operand(i, h):
                k = 2 * h + i
                src = spec[:, bass.ds(k, 1), :, :, :].rearrange("p a y r b -> p (a y) (r b)")
                dve.wait_ge(s_mm, PRIME + 2 * (k - 1))
                dve.tensor_copy(xs[i][:, :, B:3 * B], src).then_inc(s_xs, 1)
                dve.tensor_scalar(xs[i][:, :, 0:B], src[:, :, B:2 * B], -1.0, None, ALU.mult).then_inc(s_xs, 1)

            with dve.Fori(0, KX // 2) as h:
                for i in range(2):
                    operand(i, h)
                    k = 2 * h + i
                    for f in range(2):
                        dve.wait_ge(s_mm, PRIME + 2 * k + f + 1)
                        if f == 0:
                            dve.wait_ge(s_st[i], PRIME + 16 * CT * h)
                        dve.tensor_copy(ys[i][:, 4 * f:4 * f + 4, :], ps[2 * i + f][:].rearrange("p (q o) -> p q o", o=C)).then_inc(s_y, 1)

        @block.tensor
        def _(pe):
            pe.wait_ge(s_zero, 1)
            with pe.Fori(0, KX // 2) as h:
                for i in range(2):
                    k = 2 * h + i
                    pe.wait_ge(s_xs, 2 * (k + 1))
                    for r in range(2):
                        pe.wait_ge(s_w[i][r], 16 * (h + 1))
                    pe.wait_ge(s_y, PRIME + 2 * (k - 1))
                    for f in range(2):
                        for q in range(4 * f, 4 * f + 4):
                            for r in range(2):
                                for j in range(CT):
                                    y = CT * q + j
                                    ins = pe.matmul(ps[2 * i + f][32 * j:32 * j + P2, (q % 4) * C:(q % 4 + 1) * C],
                                                    xs[i][:, y, (1 - r) * B:(3 - r) * B], wt[i][:, r, y, :],
                                                    start=(r == 0), stop=(r == 1))
                        ins.then_inc(s_mm, 1)


def inverse_rows(nc, ysp, gsp, c_ih, B):
    with ExitStack() as ctx:
        sb = lambda n, s: ctx.enter_context(nc.sbuf_tensor(n, s, F32))
        sem = lambda n: ctx.enter_context(nc.semaphore(n))
        ih = sb("ih", [128, 128])
        yin = [sb(f"yin{i}", [128, KY * C]) for i in range(2)]
        go = [sb(f"go{i}", [128, KY * C]) for i in range(2)]
        ps = [ctx.enter_context(nc.psum_tensor(f"i_ps{i}", [128, 512], F32)) for i in range(4)]
        s_const, s_in, s_st = sem("ir_const"), [sem(f"ir_in{i}") for i in range(2)], [sem(f"ir_stored{i}") for i in range(2)]
        s_mm, s_a, s_d = sem("ir_transformed"), sem("ir_by_scalar"), sem("ir_by_vector")
        block = ctx.enter_context(nc.Block())

        @block.sync
        def _(sp):
            for s in (s_mm, *s_st, s_a, s_d):
                sp.sem_inc(s, PRIME)
            sp.dma_start(ih[:], c_ih).then_inc(s_const, 16)
            with sp.Fori(0, B // 2) as h:
                for i in range(2):
                    b = 2 * h + i
                    sp.wait_ge(s_a, PRIME + NCH // 2 * (b + 1))
                    sp.wait_ge(s_d, PRIME + NCH // 2 * (b + 1))
                    sp.dma_start(gsp[bass.ds(b, 1), :, :, :, :].rearrange("a h r k c -> (a h r) (k c)"), go[i][:]).then_inc(s_st[i], 16)
            for i in range(2):
                sp.wait_ge(s_st[i], PRIME + 16 * (B // 2))

        def copier(eng, odd, done, copy):
            with eng.Fori(0, B // 2) as h:
                for i in range(2):
                    eng.wait_ge(s_st[i], PRIME + 16 * h)
                    for q in range(odd, NCH, 2):
                        eng.wait_ge(s_mm, PRIME + NCH * (2 * h + i) + q + 1)
                        copy(go[i][:, 512 * q:512 * (q + 1)], ps[q % 4][:]).then_inc(done, 1)

        @block.gpsimd
        def _(pool):
            with pool.Fori(0, B // 2) as h:
                for i in range(2):
                    pool.wait_ge(s_mm, PRIME + NCH * (2 * h + i - 1))
                    pool.dma_start(yin[i][:], ysp[bass.ds(2 * h + i, 1), :, :, :, :].rearrange("a x r k c -> (a x r) (k c)")).then_inc(s_in[i], 16)

        @block.scalar
        def _(act):
            copier(act, 0, s_a, lambda o, p: act.activation(o, p, ACT.Identity))

        @block.vector
        def _(dve):
            copier(dve, 1, s_d, lambda o, p: dve.tensor_copy(o, p))

        @block.tensor
        def _(pe):
            pe.wait_ge(s_const, 16)
            with pe.Fori(0, B // 2) as h:
                for i in range(2):
                    b = 2 * h + i
                    pe.wait_ge(s_in[i], 16 * (h + 1))
                    for q in range(NCH):
                        done = (s_a, s_d)[q % 2]
                        n = NCH // 2 * b + q // 2
                        pe.wait_ge(done, PRIME + (n - 1 if q >= 4 else NCH // 2 * b))
                        pe.matmul(ps[q % 4][:], ih[:], yin[i][:, 512 * q:512 * (q + 1)], start=True, stop=True).then_inc(s_mm, 1)


def inverse_columns(nc, gsp, x1, out, c_iw, B):
    with ExitStack() as ctx:
        sb = lambda n, s: ctx.enter_context(nc.sbuf_tensor(n, s, F32))
        sem = lambda n: ctx.enter_context(nc.semaphore(n))
        iw = sb("iw", [128, 128])
        gin = [sb(f"gin{i}", [128, ROWS2, C]) for i in range(2)]
        xr = [sb(f"xr{i}", [128, PIX]) for i in range(2)]
        ps = [ctx.enter_context(nc.psum_tensor(f"o_ps{i}", [128, 512], F32)) for i in range(4)]
        s_const, s_in, s_x, s_st = sem("ic_const"), [sem(f"ic_in{i}") for i in range(2)], [sem(f"ic_x{i}") for i in range(2)], [sem(f"ic_stored{i}") for i in range(2)]
        s_mm, s_o = sem("ic_transformed"), sem("ic_added")
        block = ctx.enter_context(nc.Block())

        @block.sync
        def _(sp):
            for s in (s_mm, *s_st, s_o):
                sp.sem_inc(s, PRIME)
            sp.dma_start(iw[:], c_iw).then_inc(s_const, 16)
            with sp.Fori(0, B // 2) as h:
                for i in range(2):
                    b = 2 * h + i
                    sp.wait_ge(s_o, PRIME + NCH * (b + 1))
                    sp.dma_start(out[bass.ds(b, 1), :, :].rearrange("a c p -> c (a p)"), xr[i][:]).then_inc(s_st[i], 16)
            for i in range(2):
                sp.wait_ge(s_st[i], PRIME + 16 * (B // 2))

        @block.scalar
        def _(act):
            with act.Fori(0, B // 2) as h:
                for i in range(2):
                    b = 2 * h + i
                    act.wait_ge(s_mm, PRIME + NCH * (b - 1))
                    for t in range(2):
                        act.dma_start(gin[i][64 * t:64 * t + 64], gsp[bass.ds(b, 1), :, :, :, :].rearrange("a (m t) r k c -> t (r k) (a m) c", t=2)[t]).then_inc(s_in[i], 16)
                    act.wait_ge(s_st[i], PRIME + 16 * h)
                    act.dma_start(xr[i][:], x1[bass.ds(b, 1), :, :].rearrange("a c p -> c (a p)")).then_inc(s_x[i], 16)

        @block.vector
        def _(dve):
            with dve.Fori(0, B // 2) as h:
                for i in range(2):
                    b = 2 * h + i
                    dve.wait_ge(s_x[i], 16 * (h + 1))
                    for q in range(NCH):
                        dve.wait_ge(s_mm, PRIME + NCH * b + q + 1)
                        dve.tensor_tensor(xr[i][:, 512 * q:512 * (q + 1)], ps[q % 4][:], xr[i][:, 512 * q:512 * (q + 1)], ALU.add).then_inc(s_o, 1)

        @block.tensor
        def _(pe):
            pe.wait_ge(s_const, 16)
            with pe.Fori(0, B // 2) as h:
                for i in range(2):
                    b = 2 * h + i
                    pe.wait_ge(s_in[i], 32 * (h + 1))
                    for q in range(NCH):
                        pe.wait_ge(s_o, PRIME + (NCH * b + q - 3 if q >= 4 else NCH * b))
                        for m in range(4):
                            ins = pe.matmul(ps[q % 4][:, 128 * m:128 * m + 128], gin[i][:, 4 * q + m, :], iw[:], start=True, stop=True)
                        ins.then_inc(s_mm, 1)


def build(nc, B, x, woff, boff, wconv, wspec, c_sel, c_patt, c_gsel, c_gpos, c_grow, c_group, c_ident,
          c_fw, c_fh, c_ih, c_iw, out):
    x1 = nc.dram_tensor("x1_scratch", [B, C, PIX], F32, kind="Internal").ap()
    with nc.sbuf_tensor("fint", [1, 1], I32) as fint:
        build_l0(nc, x, woff, boff, wconv, c_sel, c_patt, c_group, c_ident, x1, fint, B)
        build_general(nc, fint, x, woff, boff, wconv, c_gsel, c_gpos, c_grow, c_group, c_ident, x1, B)
    build_l1(nc, x1, wspec, c_fw, c_fh, c_ih, c_iw, c_group, c_ident, out, B)


def kernel(x, L0_conv_offset_w, L0_conv_offset_b, L0_conv_weight,
           L1_conv_w1_real, L1_conv_w1_imag, L1_conv_w2_real, L1_conv_w2_imag):
    import concourse.bacc as bacc
    from concourse.bass_utils import run_bass_kernel_spmd

    B = x.shape[0]
    wspec = np.empty((KX, 2, C, KY, C), np.float32)
    for half, parts in enumerate(((L1_conv_w1_real, L1_conv_w1_imag), (L1_conv_w2_real, L1_conv_w2_imag))):
        for r, w in enumerate(parts):
            wspec[half * KX // 2:(half + 1) * KX // 2, r] = np.asarray(w).transpose(2, 0, 3, 1)
    arrays = {
        "x": np.ascontiguousarray(np.asarray(x).reshape(B, C, PIX)),
        "woff": np.ascontiguousarray(np.asarray(L0_conv_offset_w).transpose(1, 2, 3, 0).reshape(CG, TAPS, OMC)),
        "boff": np.ascontiguousarray(np.asarray(L0_conv_offset_b).reshape(OMC, 1)),
        "wconv": np.ascontiguousarray(np.asarray(L0_conv_weight).transpose(1, 2, 3, 0).reshape(C, TAPS, C)),
        "wspec": wspec,
        **constants_l0(), **constants_general(), **constants_l1(),
    }
    nc = bacc.Bacc("TRN2", target_bir_lowering=False, num_devices=1)
    aps = {n: nc.dram_tensor(n, a.shape, mybir.dt.from_np(a.dtype), kind="ExternalInput").ap() for n, a in arrays.items()}
    out = nc.dram_tensor("out", (B, C, PIX), F32, kind="ExternalOutput").ap()
    build(nc, B=B, out=out, **aps)
    r = run_bass_kernel_spmd(nc, [arrays], core_ids=[0])
    return r.results[0]["out"].reshape(B, C, H, W)
```

```python
import concourse.bass as bass
from concourse import mybir
import numpy as np
from contextlib import ExitStack

F32, F16, I32 = mybir.dt.float32, mybir.dt.float16, mybir.dt.int32
ALU = mybir.AluOpType
ACT = mybir.ActivationFunctionType
AX = mybir.AxisListType

C, H, W = 128, 64, 64
PIX = H * W
TAPS = 9
DG = 2
CG = C // DG
OMC = DG * 3 * TAPS
NMASK = DG * TAPS
REACH = 2.0
TR = 4
TILES = (H + 4) // TR
BANDS = H // TR
PR = TR + 4
PC = 16
SW = W + 4
TW = TR * W
COLTILES = [(0, 16, 0), (16, 12, 12), (28, 12, 24), (40, 12, 36), (52, 16, 48)]
OMR = H + 8
LO = 64
PATT = OMC
XR, XCOLS = H + 8, W + 4
PIECES = [(0, 0, 5), (0, 5, 9), (1, 0, 9), (2, 0, 9), (3, 0, 9), (4, 0, 5), (4, 5, 9)]
NP_ = len(PIECES)
PRIME = 64
NCH = PIX // 512


U = DG * TAPS
UROWS = 6 * PR
OMP = 64


def col_base(pcol):
    return next(px for at, n, px in COLTILES if at <= pcol + 2 < at + n)


def constants_l0():
    colsel = np.zeros((128, U, 128), np.float16)
    rowsel = np.zeros((128, 3, 2, UROWS), np.float16)
    spread = np.zeros((128, 6, 128), np.float16)
    r, c = np.arange(128) // PC, np.arange(128) % PC
    for g in range(DG):
        for k in range(TAPS):
            dy, dx, u = 2 * (k // 3) - 2, 2 * (k % 3) - 2, g * TAPS + k
            at = (3 * g + k % 3) * PR
            for base in (0, LO):
                colsel[base + NMASK + 2 * u + 1, 2 * k + g] = 1
                rowsel[base + NMASK + 2 * u, k // 3, 0, at:at + PR] = 1
                rowsel[base + u, k // 3, 1, at:at + PR] = 2
                spread[base + at + r, 3 * g + k % 3, np.arange(128)] = 1
            colsel[PATT + 2 + k % 3, 2 * k + g] = 1
            colsel[PATT + 5, 2 * k + g] = -c
            rowsel[PATT + (1 if dy == 0 else 0), k // 3, 0, at:at + PR] = 1
            rowsel[PATT + 5, k // 3, 0, at:at + PR] = 2 - np.arange(PR)
    patt = np.zeros((6, OMR, W), np.float16)
    pr, pc = np.arange(OMR)[:, None], np.arange(W)
    patt[0], patt[1] = pr % TR, (pr + 2) % TR
    for n, dx in enumerate((-2, 0, 2)):
        patt[2 + n] = [p + dx - col_base(p + dx) for p in pc]
    patt[5] = 1
    same = (np.arange(C)[:, None] // 4 == np.arange(C) // 4)
    return {"c_colsel": colsel, "c_rowsel": rowsel, "c_spread": spread, "c_patt": patt.reshape(6, OMR * W),
            "c_group": (same / 4).astype(np.float32), "c_ident": np.eye(128, dtype=np.float32)}


def build_l0(nc, x, woff, boff, wconv, c_colsel, c_rowsel, c_spread, c_patt, c_group, c_ident, x1, fint, B):
    with ExitStack() as ctx:
        def sb(name, shape, dt=F32):
            return ctx.enter_context(nc.sbuf_tensor(name, shape, dt))

        def ps(name):
            return ctx.enter_context(nc.psum_tensor(name, [128, 512], F32))

        def sem(name):
            return ctx.enter_context(nc.semaphore(name))

        xraw = sb("xraw", [128, PIX])
        xpad = [sb(f"xpad{i}", [128, XR, XCOLS]) for i in range(2)]
        om = [sb(f"om{i}", [128, OMR * W], F16) for i in range(2)]
        colsel, rowsel, spread = sb("colsel", [128, U, 128], F16), sb("rowsel", [128, 3, 2, UROWS], F16), sb("spread", [128, 6, 128], F16)
        wof, bof = sb("wof", [128, TAPS, OMP]), sb("bof", [128, 1])
        wcv = sb("wcv", [128, TAPS, 128])
        group, ident = sb("group", [128, 128]), sb("ident", [128, 128])
        strip = [sb(f"strip{i}", [128, 5, PR, PC]) for i in range(2)]
        patch = [sb(f"patch{i}", [128, 5, 128]) for i in range(2)]
        dist = [sb(f"dist{i}", [128, 512]) for i in range(2)]
        hat = [sb(f"hat{i}", [128, 512]) for i in range(2)]
        rdist, rhat, mhat = sb("rdist", [UROWS, TW]), sb("rhat", [UROWS, TW]), sb("mhat", [UROWS, TW])
        rows16 = [sb(f"rows16{i}", [128, TW], F16) for i in range(3)]
        samp = [sb(f"samp{i}", [128, DG, TAPS * TR, SW]) for i in range(2)]
        val = [sb(f"val{i}", [128, TAPS * TR, SW]) for i in range(2)]
        window = [sb(f"window{i}", [128, 12, XCOLS]) for i in range(2)]
        om32 = sb("om32", [128, 256])
        band = [sb(f"band{i}", [128, TW]) for i in range(2)]
        stats, mv, gs, power = sb("stats", [128, NCH, 6]), sb("mv", [128, 2]), sb("gs", [128, 8]), sb("power", [128, 1])
        fmax, fcol, fone = sb("fmax", [128, B * NCH]), sb("fcol", [128, 1]), sb("fone", [1, 2])

        val_ps = [ps(f"val_ps{i}") for i in range(2)]
        dist_ps, spread_ps = ps("dist_ps"), [ps(f"spread_ps{i}") for i in range(2)]
        rows_ps, conv_ps, off_ps = ps("rows_ps"), ps("conv_ps"), ps("off_ps")
        patch_ps = rows_ps

        s_const, s_zero, s_pad, s_om0, s_patt = sem("const_loaded"), sem("buffers_zeroed"), sem("first_image_padded"), sem("maps_zeroed"), sem("patterns_loaded")
        s_xh, s_x, s_norm = sem("half_x_loaded"), sem("x_loaded"), sem("x_normalized")
        s_v, s_fx = sem("stat_step"), sem("stat_small_step")
        s_pg, s_rt, s_pow = sem("group_mean_ready"), sem("root_ready"), sem("power_set")
        s_off, s_om, s_sig, s_cl = sem("offset_conv_done"), sem("maps_biased"), sem("masks_ready"), sem("maps_clamped")
        s_fm, s_hi, s_lo = sem("offset_bound"), sem("maps_high"), sem("maps_low")
        s_strip, s_pt, s_patch = sem("strip_ready"), sem("patch_turned"), sem("patch_ready")
        s_bc, s_dist, s_hat, s_samp = sem("positions_spread"), sem("distances_ready"), sem("hats_ready"), sem("sampling_ready")
        s_rp, s_rd, s_rh = sem("rows_in_psum"), sem("row_distances_ready"), sem("row_hats_ready")
        s_mh, s_mhi, s_mlo, s_spread = sem("masked_rows_ready"), sem("masked_rows_high"), sem("masked_rows_low"), sem("rows_spread")
        s_win = [sem(f"window_loaded{i}") for i in range(2)]
        s_smm, s_val = sem("values_sampled"), sem("values_ready")
        s_half, s_conv, s_band = sem("conv_half_done"), sem("conv_done"), sem("band_ready")
        s_bx, s_st = [sem(f"band_loaded{i}") for i in range(2)], [sem(f"band_stored{i}") for i in range(2)]
        s_fl, s_flp = sem("flag_step"), sem("flag_turned")
        s_pass_v, s_pass_p = sem("passed_vector"), sem("passed_pool")

        NCONST = 6
        NZERO = 7
        PAIRS = (TILES - 3) // 2

        CONVOLVES = {"start": 0, "second": 0, "two": 0, "odd": 1, "even": 1, "zero": 1, "one": 1, "end": 1, "last end": 1}
        SAMPLES_AT = {8: 0, 10: 1, 12: 2, 14: 3, 16: 4}
        VALUES_AT = {8: 0, 10: 1, 13: 2, 15: 3, 17: 4}
        SAMPLES_LATE = {0: 5, 2: 6}
        VALUES_LATE = {1: 5, 2: 6}
        OFFSETS_ODD, OFFSETS_EVEN = (8, 10, 14, 16, 17), (1, 5, 7, 9)
        CONV_AT = {2: (0,), 3: (1, 2), 4: (3,), 5: (4,), 6: (5,), 8: (6,), 10: (7,), 12: (8,)}

        def window_of(b, c):
            if isinstance(b, int) and b == 0:
                return c % 2, c // 2 + 1
            return (1, NCH // 2 + b) if isinstance(c, int) else (0, NCH // 2 + (NCH - 1) * (b - 1) + c + 1)

        def tap_of(b, i, q, s, kind, j):
            if kind == "last end" or kind == "end" and j >= 3:
                return None
            if j >= 3:
                return j - 3, b, i, q, s
            if kind == "start":
                return None
            if kind in ("zero", "end"):
                return j + 6, b - 1, TILES - 1, 1 - q, 1 - s
            return j + 6, b, i - 1, q, 1 - s

        def bands_before(b, i, kind):
            return BANDS * b + {"zero": -2, "one": -1, "end": -2, "last end": -1, "two": 0}.get(kind, i - 3)

        def image_tiles(eng, b, q, tile, more=True):
            tile(b, 2, q, q, "two", more=more)
            with eng.Fori(0, PAIRS) as h:
                tile(b, 2 * h + 3, q, 1 - q, "odd", h, more)
                tile(b, 2 * h + 4, q, q, "even", h, more)
            tile(b + 1, 0, 1 - q, 1 - q, "zero" if more else "end")
            tile(b + 1, 1, 1 - q, q, "one" if more else "last end")

        def all_tiles(eng, tile):
            tile(0, 0, 0, 0, "start")
            tile(0, 1, 0, 1, "second")
            with eng.Fori(0, B // 2 - 1) as p:
                for q in range(2):
                    image_tiles(eng, 2 * p + q, q, tile)
            image_tiles(eng, B - 2, 0, tile)
            image_tiles(eng, B - 1, 1, tile, more=False)

        block = ctx.enter_context(nc.Block())

        @block.sync
        def _(sp):
            for s in (s_norm, s_om, s_hi, s_lo, s_cl, s_pt, s_patch, s_bc, s_dist, s_hat, s_samp, s_rp, s_rd, s_rh, s_mh, s_mhi, s_mlo, s_spread,
                      s_smm, s_val, s_half, s_conv, s_band, s_strip, s_off, *s_st):
                sp.sem_inc(s, PRIME)
            sp.dma_start(xraw[:, 0:PIX // 2], x[0, :, 0:PIX // 2]).then_inc(s_xh, 16)
            sp.dma_start(xraw[:, PIX // 2:], x[0, :, PIX // 2:]).then_inc(s_x, 16)
            for dst, src in ((colsel, c_colsel), (rowsel, c_rowsel), (spread, c_spread)):
                sp.dma_start(dst[:], src).then_inc(s_const, 16)
            sp.dma_start(group[:], c_group).then_inc(s_const, 16)
            sp.dma_start(ident[:], c_ident).then_inc(s_const, 16)
            sp.dma_start(wcv[:], wconv).then_inc(s_const, 16)
            sp.wait_ge(s_om0, 4)
            for i in range(2):
                sp.dma_start(om[i][PATT:PATT + 6, :], c_patt).then_inc(s_patt, 16)
            for base in (0, LO):
                sp.dma_start(bof[base:base + NMASK, :], boff[2 * NMASK:OMC, :]).then_inc(s_patt, 16)
                sp.dma_start(bof[base + NMASK:base + OMC, :], boff[0:2 * NMASK, :]).then_inc(s_patt, 16)
            sp.dma_start(wof[0:CG, :, NMASK:NMASK + 27], woff[:, :, 0:27]).then_inc(s_patt, 16)
            sp.dma_start(wof[CG:C, :, NMASK + 27:OMC], woff[:, :, 27:36]).then_inc(s_patt, 16)
            sp.dma_start(wof[CG:C, :, 0:NMASK], woff[:, :, 36:54]).then_inc(s_patt, 16)

            def load_band(b, r, i, use):
                sp.wait_ge(s_st[i], PRIME + 16 * use)
                sp.dma_start(band[i][:], x[bass.ds(b, 1), :, bass.ds(TW * r, TW)].rearrange("a c p -> c (a p)")).then_inc(s_bx[i], 16)

            def store_band(b, r, i):
                sp.wait_ge(s_band, PRIME + BANDS * b + r + 1)
                sp.dma_start(x1[bass.ds(b, 1), :, bass.ds(TW * r, TW)].rearrange("a c p -> c (a p)"), band[i][:]).then_inc(s_st[i], 16)

            def bands(b):
                load_band(b, 0, 0, BANDS // 2 * b)
                with sp.Fori(0, BANDS // 2 - 1) as h:
                    load_band(b, 2 * h + 1, 1, BANDS // 2 * b + h)
                    store_band(b, 2 * h, 0)
                    load_band(b, 2 * h + 2, 0, BANDS // 2 * b + h + 1)
                    store_band(b, 2 * h + 1, 1)
                load_band(b, 15, 1, BANDS // 2 * b + 7)
                store_band(b, 14, 0)
                store_band(b, 15, 1)

            with sp.Fori(0, B - 1) as b:
                sp.wait_ge(s_norm, PRIME + NCH * (b + 1))
                sp.dma_start(xraw[:], x[bass.ds(b + 1, 1), :, :].rearrange("a c p -> c (a p)")).then_inc(s_x, 16)
                bands(b)
            bands(B - 1)
            for i in range(2):
                sp.wait_ge(s_st[i], PRIME + 16 * B * BANDS // 2)

        @block.gpsimd
        def _(pool):
            for i in range(2):
                pool.memset(om[i][:], 0.0).then_inc(s_om0, 1)
            pool.memset(wof[:], 0.0).then_inc(s_om0, 1)
            pool.memset(bof[:], 0.0).then_inc(s_om0, 1)
            pool.memset(fmax[:], 0.0).then_inc(s_zero, 1)
            for rows in rows16:
                pool.memset(rows[:], 0.0).then_inc(s_zero, 1)
            pool.memset(xpad[0][:], 0.0).then_inc(s_pad, 1)

            def tile(b, i, q, s, kind, h=None, more=True):
                if kind in ("end", "last end"):
                    return
                t = TILES * b + i
                if kind in ("start", "zero"):
                    pool.wait_ge(s_norm, PRIME + NCH * (b + 1))
                if kind == "zero":
                    load_window(b, q, NCH - 1)
                pool.wait_ge(s_pt, PRIME + 2 * (t - 1))
                if kind != "start":
                    pool.sem_inc(s_pass_p, 1)
                for j, (_, _, px) in enumerate(COLTILES):
                    src = xpad[q][:, 0:PR, 2 + px:2 + px + PC] if kind in ("start", "zero") \
                        else xpad[q][:, bass.ds(TR * i, PR), 2 + px:2 + px + PC]
                    ins = pool.tensor_copy(strip[s][:, j], src)
                ins.then_inc(s_strip, 1)
                if kind == "two" and more:
                    root(b + 1)
                if kind == "odd" and more:
                    pool.wait_ge(s_norm, PRIME + NCH * (b + 1) + h + 2)
                    load_window(b + 1, 1 - q, h)

            def load_window(b, q, c):
                first = isinstance(b, int) and b == 0
                pool.wait_ge(s_off, PRIME + NCH * b + c - (1 if first else 0))
                pool.sem_inc(s_pass_p, 1)
                rows = slice(8 * c + 2, 8 * c + 14) if isinstance(c, int) else bass.ds(8 * c + 2, 12)
                w, _ = window_of(b, c)
                pool.dma_start(window[w][:], xpad[q][:, rows, :]).then_inc(s_win[w], 16)

            def root(b):
                pool.wait_ge(s_pow, 1)
                pool.wait_ge(s_v, 6 * b + 5)
                pool.tensor_tensor(gs[:, 5:6], gs[:, 3:4], power[:], ALU.pow).then_inc(s_rt, 1)

            pool.memset(power[:], -0.5).then_inc(s_pow, 1)
            root(0)
            pool.memset(xpad[1][:], 0.0).then_inc(s_zero, 1)
            for c in range(NCH):
                pool.wait_ge(s_norm, PRIME + min(c + 2, NCH))
                load_window(0, 0, c)
            all_tiles(pool, tile)

        @block.scalar
        def _(act):
            def normalize(b, q, c):
                rows = slice(4 + 8 * c, 12 + 8 * c) if isinstance(c, int) else bass.ds(4 + 8 * c, 8)
                cols = slice(512 * c, 512 * (c + 1)) if isinstance(c, int) else bass.ds(512 * c, 512)
                act.activation(xpad[q][:, rows, 2:2 + W], xraw[:, cols].rearrange("p (r c) -> p r c", c=W),
                               ACT.Identity, bias=gs[:, 6:7], scale=gs[:, 5:6]).then_inc(s_norm, 1)

            def maps_bias(n):
                act.wait_ge(s_off, PRIME + n + 1)
                act.wait_ge(s_lo, PRIME + 2 * n)
                act.activation(om32[:], off_ps[:, 0:256], ACT.Identity, bias=bof[:, 0:1]).then_inc(s_om, 1)

            def maps_mask(n):
                act.wait_ge(s_om, PRIME + n + 1)
                for base in (0, LO):
                    act.activation(om32[base:base + NMASK, :], om32[base:base + NMASK, :], ACT.Sigmoid).then_inc(s_sig, 1)

            def maps_high(b, q, c):
                act.wait_ge(s_cl, PRIME + NCH * b + c + 1)
                at = (4 + 8 * c) * W
                for base in (0, LO):
                    cols = slice(at + 4 * base, at + 4 * base + 256) if isinstance(c, int) else bass.ds(at + 4 * base, 256)
                    act.activation(om[q][base:base + OMC, cols], om32[base:base + OMC, :], ACT.Identity).then_inc(s_hi, 1)

            def values(t, s, m):
                j, k0, k1 = PIECES[m]
                at, n, _ = COLTILES[j]
                rows = slice(k0 * TR, k1 * TR)
                act.wait_ge(s_smm, PRIME + NP_ * t + m + 1)
                act.activation(val[s][:, rows, at:at + n],
                               val_ps[(m + s) % 2][:, 0:(k1 - k0) * TR * n].rearrange("p (r c) -> p r c", c=n),
                               ACT.Identity).then_inc(s_val, 1)

            def tile(b, i, q, s, kind, h=None, more=True):
                t = TILES * b + i
                whole = kind not in ("end", "last end")
                for v in range(2 * TAPS):
                    j, second = divmod(v, 2)
                    n = TAPS * t + j - 3
                    tap = tap_of(b, i, q, s, kind, j)
                    if not second and tap:
                        r = (s + j + 1) % 2
                        act.wait_ge(s_bc, PRIME + n + 1)
                        act.wait_ge(s_hat, PRIME + n - 1)
                        act.activation(dist[r][:], dist_ps[:], ACT.Abs).then_inc(s_dist, 1)
                    if whole and v % 6 == 1:
                        act.wait_ge(s_rp, PRIME + 3 * t + j // 3 + 1)
                        act.wait_ge(s_rh, PRIME + 3 * t + j // 3)
                        act.activation(rdist[:], rows_ps[0:UROWS, 0:TW], ACT.Abs).then_inc(s_rd, 1)
                    if whole and v % 6 == 4:
                        act.wait_ge(s_mh, PRIME + 3 * t + j // 3 + 1)
                        act.wait_ge(s_spread, PRIME + TAPS * (t - 1) + j // 3 * 3 + 3)
                        act.activation(rows16[j // 3][0:UROWS, :], mhat[:], ACT.Identity).then_inc(s_mhi, 1)
                    if v in VALUES_LATE and kind not in ("start", "second"):
                        values(t - 2, s, VALUES_LATE[v])
                    if v in VALUES_AT and kind not in ("start", "last end"):
                        if VALUES_AT[v] == 0:
                            act.wait_ge(s_half, PRIME + bands_before(b, i, kind) + CONVOLVES[kind])
                        values(t - 1, 1 - s, VALUES_AT[v])
                    if whole and v == 5:
                        act.wait_ge(s_pt, PRIME + 2 * t + 1)
                        act.wait_ge(s_smm, PRIME + NP_ * (t - 1))
                        act.activation(patch[s][:, 0:4, :], patch_ps[:].rearrange("p (j c) -> p j c", c=128), ACT.Identity).then_inc(s_patch, 1)
                    if whole and v == 11:
                        act.wait_ge(s_pt, PRIME + 2 * t + 2)
                        act.activation(patch[s][:, 4, :], patch_ps[:, 0:128], ACT.Identity).then_inc(s_patch, 1)
                    if more and kind == "two" and v == 17:
                        act.wait_ge(s_v, 6 * (b + 1) + 6)
                        normalize(b + 1, 1 - q, 0)
                    if more and kind == "odd" and v == 1:
                        normalize(b + 1, 1 - q, h + 1)
                    if more and kind == "even":
                        if v == 11:
                            maps_bias(NCH * (b + 1) + h)
                        if v == 12:
                            maps_mask(NCH * (b + 1) + h)
                        if v == 14:
                            maps_high(b + 1, 1 - q, h)
                    if kind == "zero":
                        if v == 14:
                            maps_bias(NCH * b + NCH - 1)
                        if v == 15:
                            maps_mask(NCH * b + NCH - 1)
                        if v == 17:
                            maps_high(b, q, NCH - 1)

            act.wait_ge(s_const, 16 * NCONST)
            act.wait_ge(s_patt, 16 * 9)
            act.wait_ge(s_pad, 1)
            act.wait_ge(s_v, 6)
            for c in range(NCH):
                normalize(0, 0, c)
            for c in range(NCH):
                maps_bias(c)
                maps_mask(c)
                maps_high(0, 0, c)
            act.wait_ge(s_zero, NZERO)
            all_tiles(act, tile)

        @block.vector
        def _(dve):
            def statistics(b, step):
                v = 6 * b
                first = isinstance(b, int) and b == 0
                if step == 0 and first:
                    dve.wait_ge(s_xh, 16)
                if step == (NCH // 2 if first else 0):
                    dve.wait_ge(s_x, 16 * (b + 1))
                if step < NCH:
                    ins = dve.bn_stats(stats[:, step, :], xraw[:, 512 * step:512 * (step + 1)])
                    if step == NCH - 1:
                        ins.then_inc(s_v, 1)
                if step == 8:
                    dve.wait_ge(s_v, v + 1)
                    dve.sem_inc(s_pass_v, 1)
                    dve.bn_aggr(mv[:], stats[:].rearrange("p a b -> p (a b)")).then_inc(s_v, 1)
                if step == 9:
                    dve.wait_ge(s_pg, 2 * b + 1)
                    dve.tensor_copy(gs[:, 0:1], off_ps[:, 0:1]).then_inc(s_v, 1)
                    dve.wait_ge(s_v, v + 3)
                    dve.tensor_tensor(gs[:, 1:2], mv[:, 0:1], gs[:, 0:1], ALU.subtract).then_inc(s_fx, 1)
                    dve.wait_ge(s_fx, 3 * b + 1)
                    dve.tensor_tensor(gs[:, 1:2], gs[:, 1:2], gs[:, 1:2], ALU.mult).then_inc(s_fx, 1)
                    dve.wait_ge(s_fx, 3 * b + 2)
                    dve.tensor_tensor(gs[:, 2:3], gs[:, 1:2], mv[:, 1:2], ALU.add).then_inc(s_v, 1)
                if step == 10:
                    dve.wait_ge(s_pg, 2 * b + 2)
                    dve.tensor_scalar(gs[:, 3:4], off_ps[:, 1:2], 1e-5, None, ALU.add).then_inc(s_v, 1)
                    dve.tensor_scalar(gs[:, 7:8], gs[:, 0:1], -1.0, None, ALU.mult).then_inc(s_fx, 1)
                if step == 11:
                    dve.wait_ge(s_rt, b + 1)
                    dve.wait_ge(s_fx, 3 * b + 3)
                    dve.tensor_tensor(gs[:, 6:7], gs[:, 7:8], gs[:, 5:6], ALU.mult).then_inc(s_v, 1)

            def maps_clamp(n):
                dve.wait_ge(s_sig, 2 * (n + 1))
                dve.tensor_reduce(fmax[:, bass.ds(n, 1)], om32[:], AX.X, ALU.max, apply_absolute_value=True).then_inc(s_fm, 1)
                dve.wait_ge(s_fm, n + 1)
                dve.tensor_scalar(om32[:], om32[:], 256.0, -256.0, ALU.min, ALU.max).then_inc(s_cl, 1)

            def maps_low(b, q, c):
                at = (4 + 8 * c) * W
                dve.wait_ge(s_hi, PRIME + 2 * (NCH * b + c + 1))
                for base in (0, LO):
                    cols = slice(at + 4 * base, at + 4 * base + 256) if isinstance(c, int) else bass.ds(at + 4 * base, 256)
                    dve.tensor_tensor(om[q][LO - base:LO - base + OMC, cols], om32[base:base + OMC, :], om[q][base:base + OMC, cols],
                                      ALU.subtract).then_inc(s_lo, 1)

            def sampling(n, k, s, r):
                dx = 2 * (k % 3) - 2
                dve.wait_ge(s_spread, PRIME + n + 1)
                dve.wait_ge(s_hat, PRIME + n + 1)
                dve.tensor_tensor(samp[s][:, :, k * TR:(k + 1) * TR, 2 + dx:2 + dx + W],
                                  spread_ps[r][:].rearrange("p (g r c) -> p g r c", g=DG, c=W),
                                  hat[r][:].rearrange("p (g r c) -> p g r c", g=DG, c=W),
                                  ALU.mult).then_inc(s_samp, 1)

            def tile(b, i, q, s, kind, h=None, more=True):
                t = TILES * b + i
                whole = kind not in ("end", "last end")
                for v in range(2 * TAPS):
                    j, second = divmod(v, 2)
                    n = TAPS * t + j - 3
                    tap = tap_of(b, i, q, s, kind, j)
                    r = (s + j + 1) % 2
                    if not second and (tap_of(b, i, q, s, kind, j - 1) if j else kind not in ("start", "last end")):
                        k = (j - 4) % TAPS
                        if k == 0:
                            dve.wait_ge(s_smm, PRIME + NP_ * (t - 1))
                        sampling(n - 1, k, s if j > 3 else 1 - s, 1 - r)
                    if not second and tap:
                        dve.wait_ge(s_dist, PRIME + n + 1)
                        dve.wait_ge(s_samp, PRIME + n - 1)
                        dve.tensor_scalar(hat[r][:], dist[r][:], 1.0, -1.0, ALU.min, ALU.add).then_inc(s_hat, 1)
                    w = 3 * t + j // 3
                    if whole and v % 6 == 1:
                        dve.wait_ge(s_rd, PRIME + w + 1)
                        dve.wait_ge(s_mh, PRIME + w)
                        dve.tensor_scalar(rhat[:], rdist[:], 1.0, -1.0, ALU.min, ALU.add).then_inc(s_rh, 1)
                    if whole and v % 6 == 3:
                        dve.wait_ge(s_rh, PRIME + w + 1)
                        dve.wait_ge(s_mlo, PRIME + w)
                        dve.tensor_tensor(mhat[:], rows_ps[0:UROWS, TW:2 * TW], rhat[:], ALU.mult).then_inc(s_mh, 1)
                    if whole and v % 6 == 5:
                        dve.wait_ge(s_mhi, PRIME + w + 1)
                        dve.tensor_tensor(rows16[j // 3][LO:LO + UROWS, :], mhat[:], rows16[j // 3][0:UROWS, :], ALU.subtract).then_inc(s_mlo, 1)
                    if CONVOLVES[kind] and v == 12:
                        i2 = {"even": 1, "one": 1, "last end": 1}.get(kind, 0)
                        use = BANDS // 2 * b + {"odd": h, "even": h, "zero": -1, "one": -1, "end": -1, "last end": -1}[kind]
                        dve.wait_ge(s_conv, PRIME + bands_before(b, i, kind) + 1)
                        dve.wait_ge(s_bx[i2], 16 * (use + 1))
                        dve.tensor_tensor(band[i2][:], conv_ps[:, 0:TW], band[i2][:], ALU.add).then_inc(s_band, 1)
                    if more and kind == "two" and v < 12:
                        statistics(b + 1, v)
                    if more and kind == "even" and v == 12:
                        maps_clamp(NCH * (b + 1) + h)
                    if more and kind == "even" and v == 16:
                        maps_low(b + 1, 1 - q, h)
                    if kind == "zero" and v == 16:
                        maps_clamp(NCH * b + NCH - 1)
                    if kind == "zero" and v == 17:
                        maps_low(b, q, NCH - 1)

            dve.memset(samp[0][:], 0.0).then_inc(s_zero, 1)
            dve.memset(samp[1][:], 0.0).then_inc(s_zero, 1)
            dve.wait_ge(s_const, 16 * NCONST)
            for step in range(12):
                statistics(0, step)
            dve.wait_ge(s_zero, NZERO)
            for c in range(NCH):
                maps_clamp(c)
                maps_low(0, 0, c)
            all_tiles(dve, tile)
            dve.wait_ge(s_fm, NCH * B)
            dve.tensor_reduce(fcol[:], fmax[:], AX.X, ALU.max).then_inc(s_fl, 1)
            dve.wait_ge(s_flp, 1)
            dve.tensor_reduce(fone[:, 0:1], off_ps[0:1, 0:128], AX.X, ALU.max).then_inc(s_fl, 1)
            dve.wait_ge(s_fl, 2)
            dve.tensor_scalar(fone[:, 1:2], fone[:, 0:1], REACH, None, ALU.is_ge).then_inc(s_fl, 1)
            dve.wait_ge(s_fl, 3)
            dve.tensor_copy(fint[:], fone[:, 1:2]).then_inc(s_fl, 1)
            dve.wait_ge(s_fl, 4)

        @block.tensor
        def _(pe):
            def sample(t, s, m):
                j, k0, k1 = PIECES[m]
                at, n, _ = COLTILES[j]
                if m == 0:
                    pe.wait_ge(s_samp, PRIME + TAPS * (t + 1))
                    pe.wait_ge(s_patch, PRIME + 2 * (t + 1))
                pe.wait_ge(s_val, PRIME + NP_ * t + m - 1)
                for g in range(DG):
                    ins = pe.matmul(val_ps[(m + s) % 2][g * CG:(g + 1) * CG, 0:(k1 - k0) * TR * n],
                                    patch[s][:, j, g * CG:(g + 1) * CG],
                                    samp[s][:, g, k0 * TR:k1 * TR, at:at + n], start=True, stop=True)
                ins.then_inc(s_smm, 1)

            def conv(t, s, n, k):
                dx = 2 * (k % 3) - 2
                out = conv_ps[:, 0:TW].rearrange("p (r c) -> p r c", c=W)
                cols = slice(2 + dx, 2 + dx + W)
                if k == 0:
                    pe.wait_ge(s_val, PRIME + NP_ * t)
                    pe.wait_ge(s_band, PRIME + n)
                if k == 3:
                    pe.wait_ge(s_val, PRIME + NP_ * (t + 1))
                if k < 3:
                    ins = pe.matmul(out, wcv[:, k, :], val[s][:, k * TR:(k + 1) * TR, cols], start=(k == 0), stop=False)
                elif k < 6:
                    pe.matmul(out[:, 0:2, :], wcv[:, k, :], val[s][:, k * TR + 2:(k + 1) * TR, cols], start=False, stop=False)
                    ins = pe.matmul(out[:, 2:4, :], wcv[:, k, :], val[1 - s][:, k * TR:k * TR + 2, cols], start=False, stop=False)
                else:
                    ins = pe.matmul(out, wcv[:, k, :], val[1 - s][:, k * TR:(k + 1) * TR, cols], start=False, stop=(k == 8))
                if k == 5:
                    ins.then_inc(s_half, 1)
                if k == 8:
                    ins.then_inc(s_conv, 1)

            def offsets(b, q, c, k):
                dy, dx = 2 * (k // 3) - 2, 2 * (k % 3) - 2
                w, use = window_of(b, c)
                if k == 0:
                    pe.wait_ge(s_om, PRIME + NCH * b + c)
                    pe.wait_ge(s_win[w], 16 * use)
                win = window[w]
                for half in range(2):
                    at = 2 + dy + 4 * half
                    ins = pe.matmul(off_ps[OMP * half:OMP * (half + 1), 0:256], wof[:, k, :], win[:, at:at + 4, 2 + dx:2 + dx + W],
                                    start=(k == 0), stop=(k == TAPS - 1))
                if k == TAPS - 1:
                    ins.then_inc(s_off, 1)

            def group_mean(b):
                pe.wait_ge(s_v, 6 * b + 2)
                pe.matmul(off_ps[:, 0:1], group[:], mv[:, 0:1], start=True, stop=True).then_inc(s_pg, 1)

            def group_variance(b):
                pe.wait_ge(s_v, 6 * b + 4)
                pe.matmul(off_ps[:, 1:2], group[:], gs[:, 2:3], start=True, stop=True).then_inc(s_pg, 1)

            def turn(s, j):
                dst = patch_ps[:, (j % 4) * 128:(j % 4 + 1) * 128]
                return pe.transpose(dst, strip[s][:, j].rearrange("p r c -> p (r c)"), ident[:])

            def tile(b, i, q, s, kind, h=None, more=True):
                t = TILES * b + i
                if kind in ("start", "second", "zero"):
                    pe.wait_ge(s_lo, PRIME + 2 * (NCH * (b + 1) - 1))
                if kind == "two":
                    pe.wait_ge(s_lo, PRIME + 2 * NCH * (b + 1))
                whole = kind not in ("end", "last end")
                for v in range(2 * TAPS):
                    j, second = divmod(v, 2)
                    n = TAPS * t + j - 3
                    tap = tap_of(b, i, q, s, kind, j)
                    if tap and not second:
                        k, _, i_, q_, s_ = tap
                        at = W * (TR * i_ + 2 - (2 * (k // 3) - 2))
                        pe.wait_ge(s_dist, PRIME + n)
                        for g in range(DG):
                            ins = pe.matmul(dist_ps[:, TW * g:TW * (g + 1)], colsel[:, 2 * k + g, :], om[q_][:, bass.ds(at, TW)],
                                            start=True, stop=True)
                        ins.then_inc(s_bc, 1)
                    if tap and second:
                        k = tap[0]
                        if k % 3 == 0:
                            pe.wait_ge(s_mlo, PRIME + 3 * t + j // 3)
                        r = (s + j + 1) % 2
                        pe.wait_ge(s_samp, PRIME + n - 1)
                        for g in range(DG):
                            ins = pe.matmul(spread_ps[r][:, TW * g:TW * (g + 1)], spread[0:LO + UROWS, 3 * g + k % 3, :],
                                            rows16[k // 3][0:LO + UROWS, :], start=True, stop=True)
                        ins.then_inc(s_spread, 1)
                    if whole and v % 6 == 0:
                        w = v // 6
                        pe.wait_ge(s_mh, PRIME + 3 * t + w)
                        if w > 0:
                            pe.wait_ge(s_patch, PRIME + 2 * t + w)
                        at = W * (TR * i + 2 - (2 * w - 2))
                        for y in range(2):
                            ins = pe.matmul(rows_ps[0:UROWS, TW * y:TW * (y + 1)], rowsel[:, w, y, :], om[q][:, bass.ds(at, TW)],
                                            start=True, stop=True)
                        ins.then_inc(s_rp, 1)
                    if whole and v == 4:
                        pe.wait_ge(s_mh, PRIME + 3 * t + 1)
                        pe.wait_ge(s_strip, PRIME + t + 1)
                        for j in range(4):
                            ins = turn(s, j)
                        ins.then_inc(s_pt, 1)
                    if whole and v == 11:
                        pe.wait_ge(s_mh, PRIME + 3 * t + 2)
                        turn(s, 4).then_inc(s_pt, 1)
                    if CONVOLVES[kind] and v in CONV_AT:
                        for k in CONV_AT[v]:
                            conv(t - 2, 1 - s, bands_before(b, i, kind), k)
                    if kind not in ("start", "second") and v in SAMPLES_LATE:
                        sample(t - 2, s, SAMPLES_LATE[v])
                    if kind not in ("start", "last end") and v in SAMPLES_AT:
                        sample(t - 1, 1 - s, SAMPLES_AT[v])
                    if more and kind == "two" and v == 10:
                        group_mean(b + 1)
                    if more and kind == "two" and v == 12:
                        group_variance(b + 1)
                    if more and kind == "odd" and v in OFFSETS_ODD:
                        offsets(b + 1, 1 - q, h, OFFSETS_ODD.index(v))
                    if more and kind == "even" and v in OFFSETS_EVEN:
                        offsets(b + 1, 1 - q, h, 5 + OFFSETS_EVEN.index(v))
                    if kind == "zero" and 5 <= v < 14:
                        offsets(b, q, NCH - 1, v - 5)

            pe.wait_ge(s_const, 16 * NCONST)
            pe.wait_ge(s_patt, 16 * 9)
            group_mean(0)
            group_variance(0)
            pe.wait_ge(s_v, 5)
            for c in range(NCH):
                for k in range(TAPS):
                    offsets(0, 0, c, k)
            all_tiles(pe, tile)
            pe.wait_ge(s_fl, 1)
            pe.transpose(off_ps[0:1, 0:128], fcol[:], ident[:]).then_inc(s_flp, 1)

GK = 128


def constants_general():
    sel = np.zeros((GK, TAPS, 2 * DG + 1, 128), np.float32)
    col = np.arange(128) % W
    for k in range(TAPS):
        dy, dx = 2 * (k // 3) - 2, 2 * (k % 3) - 2
        for g in range(DG):
            row = NMASK + (g * TAPS + k) * 2
            sel[row, k, 2 * g] = sel[PATT, k, 2 * g] = 1
            sel[PATT + 2, k, 2 * g] = dy
            sel[row + 1, k, 2 * g + 1] = sel[PATT + 1, k, 2 * g + 1] = 1
            sel[PATT + 2, k, 2 * g + 1] = dx - col
            sel[g * TAPS + k, k, 2 * DG, g * CG:(g + 1) * CG] = 2
    pos = np.zeros((3, H, W), np.float32)
    pos[0], pos[1], pos[2] = np.arange(H)[:, None], np.arange(W), 1
    rows = -(2 * np.arange(H // 2) + (np.arange(128) // W)[:, None]).astype(np.float32)
    return {"c_gsel": sel, "c_gpos": pos.reshape(3, PIX), "c_grow": rows}


def build_general(nc, fint, x, woff, boff, wconv, c_gsel, c_gpos, c_grow, c_group, c_ident, x1, B):
    PAIRS = H // 2
    with ExitStack() as ctx:
        sb = lambda n, s, d=F32: ctx.enter_context(nc.sbuf_tensor(n, s, d))
        ps = lambda n: ctx.enter_context(nc.psum_tensor(n, [128, 512], F32))
        sem = lambda n: ctx.enter_context(nc.semaphore(n))
        xraw, xn, xt = sb("g_xraw", [128, PIX]), sb("g_xn", [128, PIX]), sb("g_xt", [128, PAIRS, C])
        xpad = sb("g_xpad", [128, XR, XCOLS])
        om = sb("g_om", [GK, PIX])
        sel, selk = sb("g_sel", [GK, TAPS, 2 * DG + 1, 128]), sb("g_selk", [GK, 2 * DG + 1, 128])
        wof, bof = sb("g_wof", [128, TAPS, OMC]), sb("g_bof", [OMC, 1])
        wcv, wck = sb("g_wcv", [128, TAPS, 128]), sb("g_wck", [128, 128])
        group, ident, rows = sb("g_group", [128, 128]), sb("g_ident", [128, 128]), sb("g_rows", [128, PAIRS])
        stats, mv, gs = sb("g_stats", [128, NCH, 6]), sb("g_mv", [128, 2]), sb("g_gs", [128, 8])
        ypos, xdist, xhat = sb("g_ypos", [128, 512]), sb("g_xdist", [128, 512]), sb("g_xhat", [128, 512])
        ydist, yhat, samp = ([sb(f"g_{n}{i}", [128, 512]) for i in range(2)] for n in ("ydist", "yhat", "samp"))
        mask, val = sb("g_mask", [128, 512]), sb("g_val", [128, 512])
        y_ps, x_ps, m_ps, v_ps, c_ps, t_ps = (ps(f"g_{n}_ps") for n in "yxmvct")

        s_const, s_zero, s_patt = sem("g_const_loaded"), sem("g_zeroed"), sem("g_patterns_loaded")
        s_x, s_st, s_pass_v = sem("g_x_loaded"), sem("g_x1_stored"), sem("g_passed_vector")
        s_v, s_pg, s_rt, s_xpad, s_xn = sem("g_stat_step"), sem("g_group_ready"), sem("g_root_ready"), sem("g_padded"), sem("g_normalized")
        s_tp, s_xt = sem("g_turned"), sem("g_turned_copied")
        s_off, s_om, s_sig, s_cl = sem("g_offset_conv_done"), sem("g_maps_biased"), sem("g_masks_ready"), sem("g_maps_clamped")
        s_tap, s_pos, s_yp, s_xd, s_xh = sem("g_tap_operands"), sem("g_positions_spread"), sem("g_rows_copied"), sem("g_column_distance"), sem("g_column_hat")
        s_yd, s_yh, s_s, s_mm = sem("g_row_distance"), sem("g_row_hat"), sem("g_sampling_ready"), sem("g_sampled")
        s_mp, s_mask, s_val, s_conv, s_acc = sem("g_mask_spread"), sem("g_mask_ready"), sem("g_values_ready"), sem("g_conv_done"), sem("g_added")
        block = ctx.enter_context(nc.Block())

        @block.sync
        def _(sp):
            flag = sp.value_load(fint[0:1, 0:1], min_val=0, max_val=1)
            with sp.If(flag == 1):
                for s in (s_st, s_conv, s_val, s_yd, s_xh, s_yh, s_s, s_mm, s_pos, s_mp, s_acc, s_xn, s_xt, s_om, s_mask, s_yp, s_xd):
                    sp.sem_inc(s, PRIME)
                for dst, src in ((sel, c_gsel), (group, c_group), (ident, c_ident), (rows, c_grow), (wcv, wconv)):
                    sp.dma_start(dst[:], src).then_inc(s_const, 16)
                sp.dma_start(bof[0:NMASK, :], boff[2 * NMASK:OMC, :]).then_inc(s_const, 16)
                sp.dma_start(bof[NMASK:OMC, :], boff[0:2 * NMASK, :]).then_inc(s_const, 16)
                sp.wait_ge(s_zero, 3)
                sp.dma_start(om[PATT:PATT + 3, :], c_gpos).then_inc(s_patt, 16)
                sp.dma_start(wof[0:CG, :, NMASK:NMASK + 27], woff[:, :, 0:27]).then_inc(s_patt, 16)
                sp.dma_start(wof[CG:C, :, NMASK + 27:OMC], woff[:, :, 27:36]).then_inc(s_patt, 16)
                sp.dma_start(wof[CG:C, :, 0:NMASK], woff[:, :, 36:54]).then_inc(s_patt, 16)
                with sp.Fori(0, B) as b:
                    sp.wait_ge(s_st, PRIME + 16 * b)
                    sp.dma_start(xraw[:], x[bass.ds(b, 1), :, :].rearrange("a c p -> c (a p)")).then_inc(s_x, 16)
                    sp.wait_ge(s_acc, PRIME + NCH * TAPS * (b + 1))
                    sp.dma_start(x1[bass.ds(b, 1), :, :].rearrange("a c p -> c (a p)"), xraw[:]).then_inc(s_st, 16)
                sp.wait_ge(s_st, PRIME + 16 * B)

        @block.gpsimd
        def _(pool):
            flag = pool.value_load(fint[0:1, 0:1], min_val=0, max_val=1)
            with pool.If(flag == 1):
                pool.memset(wof[:], 0.0).then_inc(s_zero, 1)
                pool.memset(om[:], 0.0).then_inc(s_zero, 1)
                pool.memset(xpad[:], 0.0).then_inc(s_zero, 1)

        @block.scalar
        def _(act):
            flag = act.value_load(fint[0:1, 0:1], min_val=0, max_val=1)
            with act.If(flag == 1):
                act.wait_ge(s_const, 16 * 7)
                act.wait_ge(s_zero, 3)
                with act.Fori(0, B) as b:
                    act.wait_ge(s_v, 9 * b + 6)
                    act.activation(gs[:, 4:5], gs[:, 3:4], ACT.Sqrt).then_inc(s_rt, 1)
                    act.wait_ge(s_v, 9 * b + 9)
                    act.wait_ge(s_conv, PRIME + NCH * TAPS * b)
                    for q in range(NCH):
                        act.activation(xpad[:, 4 + 8 * q:12 + 8 * q, 2:2 + W],
                                       xraw[:, 512 * q:512 * (q + 1)].rearrange("p (r c) -> p r c", c=W),
                                       ACT.Identity, bias=gs[:, 6:7], scale=gs[:, 5:6]).then_inc(s_xpad, 1)
                        act.activation(xn[:, 512 * q:512 * (q + 1)], xraw[:, 512 * q:512 * (q + 1)],
                                       ACT.Identity, bias=gs[:, 6:7], scale=gs[:, 5:6]).then_inc(s_xn, 1)
                    for q in range(NCH):
                        act.wait_ge(s_tp, NCH * b + q + 1)
                        act.activation(xt[:, 4 * q:4 * q + 4, :], t_ps[:].rearrange("p (m c) -> p m c", c=C), ACT.Identity).then_inc(s_xt, 1)
                    for q in range(NCH):
                        n = NCH * b + q
                        act.wait_ge(s_off, n + 1)
                        part = om[0:OMC, 512 * q:512 * (q + 1)]
                        act.activation(part, t_ps[0:OMC, :], ACT.Identity, bias=bof[:, 0:1]).then_inc(s_om, 1)
                        act.wait_ge(s_om, PRIME + n + 1)
                        part = om[0:NMASK, 512 * q:512 * (q + 1)]
                        act.activation(part, part, ACT.Sigmoid).then_inc(s_sig, 1)
                    with act.Fori(0, NCH) as q:
                        with act.Fori(0, TAPS) as k:
                            e = (NCH * b + q) * TAPS + k
                            act.wait_ge(s_mp, PRIME + e + 1)
                            act.wait_ge(s_val, PRIME + e)
                            act.activation(mask[:], m_ps[:], ACT.Identity).then_inc(s_mask, 1)
                            for g in range(DG):
                                act.wait_ge(s_pos, PRIME + DG * e + g + 1)
                                act.wait_ge(s_yd, PRIME + PAIRS * (DG * e + g))
                                act.wait_ge(s_xh, PRIME + DG * e + g)
                                act.activation(ypos[:], y_ps[:], ACT.Identity).then_inc(s_yp, 1)
                                act.activation(xdist[:], x_ps[:], ACT.Abs).then_inc(s_xd, 1)
                                act.wait_ge(s_yp, PRIME + DG * e + g + 1)
                                for n in range(PAIRS):
                                    m = PAIRS * (DG * e + g) + n
                                    act.wait_ge(s_yh, PRIME + (m - 1 if n >= 2 else PAIRS * (DG * e + g)))
                                    act.activation(ydist[n % 2][:], ypos[:], ACT.Abs, bias=rows[:, n:n + 1]).then_inc(s_yd, 1)

        @block.vector
        def _(dve):
            flag = dve.value_load(fint[0:1, 0:1], min_val=0, max_val=1)
            with dve.If(flag == 1):
                dve.wait_ge(s_const, 16 * 7)
                dve.wait_ge(s_zero, 3)
                with dve.Fori(0, B) as b:
                    v = 9 * b
                    dve.wait_ge(s_x, 16 * (b + 1))
                    for q in range(NCH):
                        ins = dve.bn_stats(stats[:, q, :], xraw[:, 512 * q:512 * (q + 1)])
                    ins.then_inc(s_v, 1)
                    dve.wait_ge(s_v, v + 1)
                    dve.sem_inc(s_pass_v, 1)
                    dve.bn_aggr(mv[:], stats[:].rearrange("p a b -> p (a b)")).then_inc(s_v, 1)
                    dve.wait_ge(s_pg, 2 * b + 1)
                    dve.tensor_copy(gs[:, 0:1], t_ps[:, 0:1]).then_inc(s_v, 1)
                    dve.wait_ge(s_v, v + 3)
                    dve.tensor_tensor(gs[:, 1:2], mv[:, 0:1], gs[:, 0:1], ALU.subtract).then_inc(s_v, 1)
                    dve.wait_ge(s_v, v + 4)
                    dve.scalar_tensor_tensor(gs[:, 2:3], gs[:, 1:2], gs[:, 1:2], mv[:, 1:2], ALU.mult, ALU.add).then_inc(s_v, 1)
                    dve.wait_ge(s_pg, 2 * b + 2)
                    dve.tensor_scalar(gs[:, 3:4], t_ps[:, 1:2], 1e-5, None, ALU.add).then_inc(s_v, 1)
                    dve.wait_ge(s_rt, b + 1)
                    dve.wait_ge(s_xn, PRIME + NCH * b)
                    dve.reciprocal(gs[:, 5:6], gs[:, 4:5]).then_inc(s_v, 1)
                    dve.tensor_scalar(gs[:, 7:8], gs[:, 0:1], -1.0, None, ALU.mult).then_inc(s_v, 1)
                    dve.wait_ge(s_v, v + 8)
                    dve.tensor_tensor(gs[:, 6:7], gs[:, 7:8], gs[:, 5:6], ALU.mult).then_inc(s_v, 1)
                    for q in range(NCH):
                        n = NCH * b + q
                        dve.wait_ge(s_sig, n + 1)
                        part = om[0:OMC, 512 * q:512 * (q + 1)]
                        dve.tensor_scalar(part, part, 256.0, -256.0, ALU.min, ALU.max).then_inc(s_cl, 1)
                    with dve.Fori(0, NCH) as q:
                        with dve.Fori(0, TAPS) as k:
                            e = (NCH * b + q) * TAPS + k
                            dve.wait_ge(s_conv, PRIME + e)
                            dve.wait_ge(s_pos, PRIME + DG * e)
                            dve.wait_ge(s_mp, PRIME + e)
                            dve.tensor_copy(selk[:], sel[:, bass.ds(k, 1), :, :].rearrange("p a s q -> p (a s) q")).then_inc(s_tap, 1)
                            dve.tensor_copy(wck[:], wcv[:, bass.ds(k, 1), :].rearrange("p a o -> p (a o)")).then_inc(s_tap, 1)
                            for g in range(DG):
                                dve.wait_ge(s_xd, PRIME + DG * e + g + 1)
                                dve.wait_ge(s_s, PRIME + PAIRS * (DG * e + g))
                                dve.tensor_scalar(xhat[:], xdist[:], 1.0, -1.0, ALU.min, ALU.add).then_inc(s_xh, 1)
                                dve.wait_ge(s_xh, PRIME + DG * e + g + 1)
                                for n in range(PAIRS):
                                    m = PAIRS * (DG * e + g) + n
                                    dve.wait_ge(s_yd, PRIME + m + 1)
                                    dve.wait_ge(s_s, PRIME + (m - 1 if n >= 2 else PAIRS * (DG * e + g)))
                                    dve.tensor_scalar(yhat[n % 2][:], ydist[n % 2][:], 1.0, -1.0, ALU.min, ALU.add).then_inc(s_yh, 1)
                                    dve.wait_ge(s_yh, PRIME + m + 1)
                                    dve.wait_ge(s_mm, PRIME + (m - 1 if n >= 2 else PAIRS * (DG * e + g)))
                                    dve.tensor_tensor(samp[n % 2][:], xhat[:], yhat[n % 2][:], ALU.mult).then_inc(s_s, 1)
                            dve.wait_ge(s_mm, PRIME + PAIRS * DG * (e + 1))
                            dve.wait_ge(s_mask, PRIME + e + 1)
                            dve.tensor_tensor(val[:], v_ps[:], mask[:], ALU.mult).then_inc(s_val, 1)
                            dve.wait_ge(s_conv, PRIME + e + 1)
                            dve.wait_ge(s_acc, PRIME + e)
                            dst = xraw[:, bass.ds(512 * q, 512)]
                            dve.tensor_tensor(dst, c_ps[:], dst, ALU.add).then_inc(s_acc, 1)

        @block.tensor
        def _(pe):
            flag = pe.value_load(fint[0:1, 0:1], min_val=0, max_val=1)
            with pe.If(flag == 1):
                pe.wait_ge(s_const, 16 * 7)
                pe.wait_ge(s_patt, 16 * 4)
                with pe.Fori(0, B) as b:
                    pe.wait_ge(s_v, 9 * b + 2)
                    pe.matmul(t_ps[:, 0:1], group[:], mv[:, 0:1], start=True, stop=True).then_inc(s_pg, 1)
                    pe.wait_ge(s_v, 9 * b + 5)
                    pe.matmul(t_ps[:, 1:2], group[:], gs[:, 2:3], start=True, stop=True).then_inc(s_pg, 1)
                    pe.wait_ge(s_v, 9 * b + 6)
                    for q in range(NCH):
                        pe.wait_ge(s_xn, PRIME + NCH * b + q + 1)
                        pe.wait_ge(s_xt, PRIME + NCH * b + q)
                        for m in range(4):
                            ins = pe.transpose(t_ps[:, 128 * m:128 * m + 128], xn[:, 512 * q + 128 * m:512 * q + 128 * m + 128], ident[:])
                        ins.then_inc(s_tp, 1)
                    pe.wait_ge(s_xpad, NCH * (b + 1))
                    pe.wait_ge(s_xt, PRIME + NCH * (b + 1))
                    for q in range(NCH):
                        pe.wait_ge(s_om, PRIME + NCH * b + q)
                        for k in range(TAPS):
                            dy, dx = 2 * (k // 3) - 2, 2 * (k % 3) - 2
                            ins = pe.matmul(t_ps[0:OMC, :], wof[:, k, :],
                                            xpad[:, 8 * q + dy + 4:8 * q + dy + 12, 2 + dx:2 + dx + W],
                                            start=(k == 0), stop=(k == TAPS - 1))
                        ins.then_inc(s_off, 1)
                    with pe.Fori(0, NCH) as q:
                        with pe.Fori(0, TAPS) as k:
                            pe.wait_ge(s_cl, NCH * (b + 1))
                            e = (NCH * b + q) * TAPS + k
                            src = om[:, bass.ds(512 * q, 512)]
                            pe.wait_ge(s_tap, 2 * (e + 1))
                            pe.wait_ge(s_mask, PRIME + e)
                            pe.matmul(m_ps[:], selk[:, 2 * DG, :], src, start=True, stop=True).then_inc(s_mp, 1)
                            for g in range(DG):
                                pe.wait_ge(s_yp, PRIME + DG * e + g)
                                pe.wait_ge(s_xd, PRIME + DG * e + g)
                                pe.matmul(y_ps[:], selk[:, 2 * g, :], src, start=True, stop=True)
                                pe.matmul(x_ps[:], selk[:, 2 * g + 1, :], src, start=True, stop=True).then_inc(s_pos, 1)
                                pe.wait_ge(s_val, PRIME + e)
                                for n in range(PAIRS):
                                    m = PAIRS * (DG * e + g) + n
                                    pe.wait_ge(s_s, PRIME + m + 1)
                                    pe.matmul(v_ps[g * CG:(g + 1) * CG, :], xt[:, n, g * CG:(g + 1) * CG], samp[n % 2][:],
                                              start=(n == 0), stop=(n == PAIRS - 1)).then_inc(s_mm, 1)
                            pe.wait_ge(s_val, PRIME + e + 1)
                            pe.wait_ge(s_acc, PRIME + e)
                            pe.matmul(c_ps[:], wck[:], val[:], start=True, stop=True).then_inc(s_conv, 1)

KX, KY = H, W // 2
CT = 4
KQ = KY // CT


def constants_l1():
    w, ky, h, kx = np.arange(W), np.arange(KY), np.arange(H), np.arange(KX)
    a = 2 * np.pi * np.outer(w, ky) / W
    fw = np.zeros((2, W, 2, 2, KY))
    for i in range(2):
        fw[i, :, i, 0], fw[i, :, i, 1] = np.cos(a), -np.sin(a)
    b = 2 * np.pi * np.outer(h, kx) / H
    fh = np.zeros((H, 2, 2, KX))
    fh[:, 0, 0], fh[:, 1, 0], fh[:, 0, 1], fh[:, 1, 1] = np.cos(b), np.sin(b), -np.sin(b), np.cos(b)
    fh /= PIX
    c = b.T
    ih = np.zeros((KX, 2, H, 2))
    ih[:, 0, :, 0], ih[:, 1, :, 0], ih[:, 0, :, 1], ih[:, 1, :, 1] = np.cos(c), -np.sin(c), np.sin(c), np.cos(c)
    iw = np.zeros((2, 2, KY, 2, W))
    for n in range(KY):
        k = CT * (n % KQ) + n // KQ
        d = 2 * np.pi * k * w / W
        for i in range(2):
            iw[i, 0, n, i] = np.cos(d) * (1 if k == 0 else 2)
            iw[i, 1, n, i] = -np.sin(d) * (0 if k == 0 else 2)
    f = lambda m: np.ascontiguousarray(m.reshape(128, 128).astype(np.float32))
    return {"c_fw": f(fw), "c_fh": f(fh), "c_ih": f(ih), "c_iw": f(iw)}


def build_l1(nc, x1, wspec, c_fw, c_fh, c_ih, c_iw, c_group, c_ident, out, B=8):
    ysp = nc.dram_tensor("y_scratch", [B, KX, 2, KY, C], F32, kind="Internal").ap()
    with nc.sbuf_tensor("spec", [128, KX, KY, 2, B], F32) as spec, nc.sbuf_tensor("scales", [128, 3 * B], F32) as scales:
        forward(nc, x1, c_fw, c_fh, c_group, c_ident, spec, scales, B)
        mix_modes(nc, spec, scales, wspec, ysp, B)
    inverse(nc, ysp, x1, out, c_ih, c_iw, c_ident, B)


def forward(nc, x1, c_fw, c_fh, c_group, c_ident, spec, scales, B):
    with ExitStack() as ctx:
        sb = lambda n, s: ctx.enter_context(nc.sbuf_tensor(n, s, F32))
        ps = lambda n: ctx.enter_context(nc.psum_tensor(n, [128, 512], F32))
        sem = lambda n: ctx.enter_context(nc.semaphore(n))
        fw, fh, group, ident = (sb(n, [128, 128]) for n in ("fw", "fh", "group1", "ident1"))
        xin = [sb(f"xin{i}", [128, PIX]) for i in range(2)]
        xt = [sb(f"xt{i}", [128, 512]) for i in range(2)]
        cols = [sb(f"cols{i}", [128, H * 2, KY]) for i in range(2)]
        ct = [sb(f"ct{i}", [128, 512]) for i in range(2)]
        stats, mv, mva = sb("stats1", [128, NCH, 6]), sb("mv1", [128, 2]), sb("mva", [128, 2, B])
        gm = sb("gm", [128, 5, B])
        xt_ps, ct_ps, g_ps = ps("xt_ps"), ps("ct_ps"), ps("g_ps")
        w_ps, h_ps = [ps(f"w_ps{i}") for i in range(2)], [ps(f"h_ps{i}") for i in range(2)]
        s_const, s_x = sem("fw_const"), [sem(f"fw_x{i}") for i in range(2)]
        s_xp, s_xt, s_w, s_wc = sem("fw_image_turned"), sem("fw_image_copied"), sem("fw_columns"), sem("fw_columns_copied")
        s_cp, s_ct, s_h, s_hc = sem("fw_spectra_turned"), sem("fw_spectra_copied"), sem("fw_rows"), sem("fw_rows_copied")
        s_bn, s_ag, s_mv, s_pg, s_fin, s_rt = sem("fw_measured"), sem("fw_aggregated"), sem("fw_statistics"), sem("fw_group"), sem("fw_final_step"), sem("fw_root")
        s_pass_v = sem("fw_passed_vector")
        block = ctx.enter_context(nc.Block())

        def images(eng, step):
            step(0, 0, True, False)
            with eng.Fori(0, B // 2 - 1) as h:
                step(2 * h + 1, 1, True, True)
                step(2 * h + 2, 0, True, True)
            step(B - 1, 1, True, True)
            step(B, 0, False, True)

        @block.sync
        def _(sp):
            for s in (s_xp, s_xt, s_w, s_wc, s_cp, s_ct, s_h, s_hc, s_bn, s_mv):
                sp.sem_inc(s, PRIME)
            sp.dma_start(xin[0][:], x1[0, :, :]).then_inc(s_x[0], 16)
            for dst, src in ((ident, c_ident), (fw, c_fw), (fh, c_fh), (group, c_group)):
                sp.dma_start(dst[:], src).then_inc(s_const, 16)
            sp.dma_start(xin[1][:], x1[1, :, :]).then_inc(s_x[1], 16)
            with sp.Fori(1, B // 2) as h:
                for i in range(2):
                    b = 2 * h + i
                    sp.wait_ge(s_wc, PRIME + NCH * (b - 1))
                    sp.dma_start(xin[i][:], x1[bass.ds(b, 1), :, :].rearrange("a c p -> c (a p)")).then_inc(s_x[i], 16)

        @block.scalar
        def _(act):
            def step(b, i, first, second):
                for q in range(NCH):
                    if first:
                        act.wait_ge(s_xp, PRIME + NCH * b + q + 1)
                        act.wait_ge(s_w, PRIME + NCH * b + q - 1)
                        act.activation(xt[q % 2][:], xt_ps[:], ACT.Identity).then_inc(s_xt, 1)
                    if second:
                        act.wait_ge(s_cp, PRIME + NCH * (b - 1) + q + 1)
                        act.wait_ge(s_h, PRIME + NCH * (b - 1) + q - 1)
                        act.activation(ct[q % 2][:], ct_ps[:], ACT.Identity).then_inc(s_ct, 1)

            images(act, step)
            act.wait_ge(s_fin, 5)
            act.activation(gm[:, 4, :], gm[:, 3, :], ACT.Sqrt).then_inc(s_rt, 1)

        @block.vector
        def _(dve):
            def step(b, i, first, second):
                for q in range(NCH):
                    if first:
                        if q == 0:
                            dve.wait_ge(s_x[i], 16 * (b // 2 + 1) if isinstance(b, int) else 8 * (b - i) + 16)
                            dve.wait_ge(s_ag, b) if isinstance(b, int) and b > 0 else None
                        ins = dve.bn_stats(stats[:, q, :], xin[i][:, 512 * q:512 * (q + 1)])
                        ins.then_inc(s_bn, 1)
                        dve.wait_ge(s_w, PRIME + NCH * b + q + 1)
                        if q == 0:
                            dve.wait_ge(s_cp, PRIME + NCH * (b - 1))
                        dve.tensor_copy(cols[i][:, 16 * q:16 * q + 16, :], w_ps[q % 2][:].rearrange("p (a k) -> p a k", k=KY)).then_inc(s_wc, 1)
                    if second:
                        dve.wait_ge(s_h, PRIME + NCH * (b - 1) + q + 1)
                        dve.tensor_copy(spec[:, :, 4 * q:4 * q + 4, :, bass.ds(b - 1, 1)].rearrange("p x y r a -> p y r (x a)"),
                                        h_ps[q % 2][:].rearrange("p (y r x) -> p y r x", y=4, r=2)).then_inc(s_hc, 1)
                if first:
                    dve.wait_ge(s_bn, PRIME + NCH * (b + 1))
                    dve.sem_inc(s_pass_v, 1)
                    dve.bn_aggr(mv[:], stats[:].rearrange("p a b -> p (a b)")).then_inc(s_ag, 1)
                    dve.wait_ge(s_ag, b + 1)
                    dve.tensor_copy(mva[:, :, bass.ds(b, 1)], mv[:].rearrange("p (s a) -> p s a", a=1)).then_inc(s_mv, 1)
                    dve.wait_ge(s_mv, PRIME + b + 1)

            images(dve, step)
            dve.wait_ge(s_pg, 1)
            dve.tensor_copy(gm[:, 0, :], g_ps[:, 0:B]).then_inc(s_fin, 1)
            dve.wait_ge(s_fin, 1)
            dve.tensor_tensor(gm[:, 1, :], mva[:, 0, :], gm[:, 0, :], ALU.subtract).then_inc(s_fin, 1)
            dve.wait_ge(s_fin, 2)
            dve.tensor_tensor(gm[:, 1, :], gm[:, 1, :], gm[:, 1, :], ALU.mult).then_inc(s_fin, 1)
            dve.wait_ge(s_fin, 3)
            dve.tensor_tensor(gm[:, 2, :], gm[:, 1, :], mva[:, 1, :], ALU.add).then_inc(s_fin, 1)
            dve.wait_ge(s_pg, 2)
            dve.tensor_scalar(gm[:, 3, :], g_ps[:, B:2 * B], 1e-5, None, ALU.add).then_inc(s_fin, 1)
            dve.wait_ge(s_rt, 1)
            dve.reciprocal(scales[:, B:2 * B], gm[:, 4, :]).then_inc(s_fin, 1)
            dve.wait_ge(s_fin, 6)
            dve.tensor_copy(scales[:, 2 * B:3 * B], scales[:, B:2 * B]).then_inc(s_fin, 1)
            dve.tensor_scalar(scales[:, 0:B], scales[:, B:2 * B], -1.0, None, ALU.mult).then_inc(s_fin, 1)
            dve.wait_ge(s_hc, PRIME + NCH * B)
            dve.tensor_tensor(spec[:, 0, 0, 0, :], spec[:, 0, 0, 0, :], gm[:, 0, :], ALU.subtract).then_inc(s_fin, 1)
            dve.wait_ge(s_fin, 9)

        @block.tensor
        def _(pe):
            def turn_image(b, i, q):
                pe.wait_ge(s_xt, PRIME + NCH * b + q)
                for m in range(4):
                    ins = pe.transpose(xt_ps[:, m * 128:(m + 1) * 128], xin[i][:, (4 * q + m) * 128:(4 * q + m + 1) * 128], ident[:])
                ins.then_inc(s_xp, 1)

            def turn_spectra(b, i, q):
                pe.wait_ge(s_ct, PRIME + NCH * b + q)
                for y in range(4):
                    ins = pe.transpose(ct_ps[:, y * 128:(y + 1) * 128], cols[i][:, :, 4 * q + y], ident[:])
                ins.then_inc(s_cp, 1)

            def step(b, i, first, second):
                if first:
                    pe.wait_ge(s_x[i], 16 * (b // 2 + 1) if isinstance(b, int) else 8 * (b - i) + 16)
                    turn_image(b, i, 0)
                if second:
                    pe.wait_ge(s_wc, PRIME + NCH * b)
                    turn_spectra(b - 1, 1 - i, 0)
                for q in range(NCH):
                    if first:
                        if q + 1 < NCH:
                            turn_image(b, i, q + 1)
                        pe.wait_ge(s_xt, PRIME + NCH * b + q + 1)
                        pe.wait_ge(s_wc, PRIME + NCH * b + q - 1)
                        for m in range(4):
                            ins = pe.matmul(w_ps[q % 2][:, 128 * m:128 * m + 128], xt[q % 2][:, 128 * m:128 * m + 128], fw[:], start=True, stop=True)
                        ins.then_inc(s_w, 1)
                    if second:
                        if q + 1 < NCH:
                            turn_spectra(b - 1, 1 - i, q + 1)
                        pe.wait_ge(s_ct, PRIME + NCH * (b - 1) + q + 1)
                        pe.wait_ge(s_hc, PRIME + NCH * (b - 1) + q - 1)
                        for y in range(4):
                            ins = pe.matmul(h_ps[q % 2][:, 128 * y:128 * y + 128], ct[q % 2][:, 128 * y:128 * y + 128], fh[:], start=True, stop=True)
                        ins.then_inc(s_h, 1)

            pe.wait_ge(s_const, 64)
            images(pe, step)
            pe.wait_ge(s_mv, PRIME + B)
            pe.matmul(g_ps[:, 0:B], group[:], mva[:, 0, :], start=True, stop=True).then_inc(s_pg, 1)
            pe.wait_ge(s_fin, 4)
            pe.matmul(g_ps[:, B:2 * B], group[:], gm[:, 2, :], start=True, stop=True).then_inc(s_pg, 1)


def mix_modes(nc, spec, scales, wspec, ysp, B):
    with ExitStack() as ctx:
        sb = lambda n, s: ctx.enter_context(nc.sbuf_tensor(n, s, F32))
        sem = lambda n: ctx.enter_context(nc.semaphore(n))
        wt = [sb(f"wt{i}", [128, 2, KY, C]) for i in range(2)]
        xs = [sb(f"xs{i}", [128, KY, 3 * B]) for i in range(2)]
        ys = [sb(f"ys{i}", [128, KQ, C]) for i in range(2)]
        ps = [ctx.enter_context(nc.psum_tensor(f"m_ps{i}", [128, 512], F32)) for i in range(4)]
        s_w = [[sem(f"mm_weights{i}{r}") for r in range(2)] for i in range(2)]
        s_zero, s_xs, s_mm, s_y = sem("mm_zeroed"), sem("mm_operand"), sem("mm_mixed"), sem("mm_copied")
        s_st = [sem(f"mm_stored{i}") for i in range(2)]
        block = ctx.enter_context(nc.Block())

        @block.sync
        def _(sp):
            for s in (s_mm, *s_st, s_y):
                sp.sem_inc(s, PRIME)
            with sp.Fori(0, KX // 2) as h:
                for i in range(2):
                    k = 2 * h + i
                    sp.wait_ge(s_mm, PRIME + 2 * (k - 1))
                    for r in range(2):
                        sp.dma_start(wt[i][:, r, :, :], wspec[bass.ds(k, 1), r, :, :, :].rearrange("a i y o -> i (a y) o")).then_inc(s_w[i][r], 16)

        @block.scalar
        def _(act):
            with act.Fori(0, KX // 2) as h:
                for i in range(2):
                    k = 2 * h + i
                    act.wait_ge(s_y, PRIME + 2 * (k + 1))
                    for j in range(CT):
                        act.dma_start(ysp[:, bass.ds(k, 1), :, KQ * j:KQ * (j + 1), :].rearrange("b a r q o -> (a r) b (q o)"),
                                      ys[i][32 * j:32 * j + 2 * B, :, :].rearrange("p q o -> p (q o)")).then_inc(s_st[i], 16)
            for i in range(2):
                act.wait_ge(s_st[i], PRIME + 16 * CT * (KX // 2))

        @block.vector
        def _(dve):
            for p in ps:
                ins = dve.memset(p[:], 0.0)
            ins.then_inc(s_zero, 1)
            dve.wait_ge(s_zero, 1)

            def operand(i, h):
                k = 2 * h + i
                src = spec[:, bass.ds(k, 1), :, :, :].rearrange("p a y r b -> p (a y) (r b)")
                dve.wait_ge(s_mm, PRIME + 2 * (k - 1))
                dve.tensor_tensor(xs[i][:, :, B:3 * B], src, scales[:, None, B:3 * B].to_broadcast([128, KY, 2 * B]), ALU.mult).then_inc(s_xs, 1)
                dve.tensor_tensor(xs[i][:, :, 0:B], src[:, :, B:2 * B], scales[:, None, 0:B].to_broadcast([128, KY, B]), ALU.mult).then_inc(s_xs, 1)

            with dve.Fori(0, KX // 2) as h:
                for i in range(2):
                    operand(i, h)
                    k = 2 * h + i
                    for f in range(2):
                        dve.wait_ge(s_mm, PRIME + 2 * k + f + 1)
                        if f == 0:
                            dve.wait_ge(s_st[i], PRIME + 16 * CT * h)
                        dve.tensor_copy(ys[i][:, 4 * f:4 * f + 4, :], ps[2 * i + f][:].rearrange("p (q o) -> p q o", o=C)).then_inc(s_y, 1)

        @block.tensor
        def _(pe):
            pe.wait_ge(s_zero, 1)
            with pe.Fori(0, KX // 2) as h:
                for i in range(2):
                    k = 2 * h + i
                    pe.wait_ge(s_xs, 2 * (k + 1))
                    for r in range(2):
                        pe.wait_ge(s_w[i][r], 16 * (h + 1))
                    pe.wait_ge(s_y, PRIME + 2 * (k - 1))
                    for f in range(2):
                        for q in range(4 * f, 4 * f + 4):
                            for r in range(2):
                                for j in range(CT):
                                    y = CT * q + j
                                    ins = pe.matmul(ps[2 * i + f][32 * j:32 * j + 2 * B, (q % 4) * C:(q % 4 + 1) * C],
                                                    xs[i][:, y, (1 - r) * B:(3 - r) * B], wt[i][:, r, y, :],
                                                    start=(r == 0), stop=(r == 1))
                        ins.then_inc(s_mm, 1)


def inverse(nc, ysp, x1, out, c_ih, c_iw, c_ident, B):
    with ExitStack() as ctx:
        sb = lambda n, s: ctx.enter_context(nc.sbuf_tensor(n, s, F32))
        ps = lambda n: ctx.enter_context(nc.psum_tensor(n, [128, 512], F32))
        sem = lambda n: ctx.enter_context(nc.semaphore(n))
        ih, iw, ident = (sb(n, [128, 128]) for n in ("ih", "iw", "ident2"))
        yin = [sb(f"yin{i}", [128, KY, C]) for i in range(2)]
        rows = [sb(f"rows{i}", [128, H * 2, KY]) for i in range(2)]
        rt = [sb(f"rt{i}", [128, 512]) for i in range(2)]
        xr = [sb(f"xr{i}", [128, PIX]) for i in range(2)]
        z_ps, t_ps = [ps(f"z_ps{i}") for i in range(2)], [ps(f"rt_ps{i}") for i in range(2)]
        o_ps = [ps(f"o_ps{i}") for i in range(2)]
        s_const, s_in, s_x = sem("in_const"), [sem(f"in_y{i}") for i in range(2)], [sem(f"in_x{i}") for i in range(2)]
        s_st = [sem(f"in_stored{i}") for i in range(2)]
        s_z, s_zc, s_tp, s_tc, s_o, s_oc = sem("in_rows"), sem("in_rows_copied"), sem("in_turned"), sem("in_turned_copied"), sem("in_columns"), sem("in_added")
        block = ctx.enter_context(nc.Block())

        def images(eng, step):
            step(0, 0, True, False)
            with eng.Fori(0, B // 2 - 1) as h:
                step(2 * h + 1, 1, True, True)
                step(2 * h + 2, 0, True, True)
            step(B - 1, 1, True, True)
            step(B, 0, False, True)

        @block.sync
        def _(sp):
            for s in (s_z, s_zc, s_tp, s_tc, s_o, s_oc, *s_st):
                sp.sem_inc(s, PRIME)
            for dst, src in ((ih, c_ih), (iw, c_iw), (ident, c_ident)):
                sp.dma_start(dst[:], src).then_inc(s_const, 16)
            sp.dma_start(yin[0][:], ysp[0, :, :, :, :].rearrange("x r k c -> (x r) k c")).then_inc(s_in[0], 16)

            def load(b, i):
                sp.wait_ge(s_z, PRIME + NCH * (b - 1))
                sp.dma_start(yin[i][:], ysp[bass.ds(b, 1), :, :, :, :].rearrange("a x r k c -> (a x r) k c")).then_inc(s_in[i], 16)

            def store(b, i):
                sp.wait_ge(s_oc, PRIME + NCH * (b + 1))
                sp.dma_start(out[bass.ds(b, 1), :, :].rearrange("a c p -> c (a p)"), xr[i][:]).then_inc(s_st[i], 16)

            load(1, 1)
            with sp.Fori(1, B // 2) as h:
                for i in range(2):
                    load(2 * h + i, i)
                    store(2 * h + i - 2, i)
            for i in range(2):
                store(B - 2 + i, i)
            for i in range(2):
                sp.wait_ge(s_st[i], PRIME + 16 * (B // 2))

        @block.scalar
        def _(act):
            def step(b, i, first, second):
                for q in range(NCH):
                    if first:
                        act.wait_ge(s_z, PRIME + NCH * b + q + 1)
                        if q == 0:
                            act.wait_ge(s_tp, PRIME + NCH * (b - 1))
                        act.activation(rows[i][:, :, 4 * q:4 * q + 4].rearrange("p a y -> p y a"),
                                       z_ps[q % 2][:].rearrange("p (y a) -> p y a", y=4), ACT.Identity).then_inc(s_zc, 1)

            images(act, step)

        @block.gpsimd
        def _(pool):
            pool.wait_ge(s_in[0], 16)
            with pool.Fori(0, B // 2) as h:
                for i in range(2):
                    b = 2 * h + i
                    pool.wait_ge(s_st[i], PRIME + 16 * h)
                    pool.dma_start(xr[i][:], x1[bass.ds(b, 1), :, :].rearrange("a c p -> c (a p)")).then_inc(s_x[i], 16)

        @block.vector
        def _(dve):
            def step(b, i, first, second):
                for q in range(NCH):
                    if second:
                        n = NCH * (b - 1) + q
                        dve.wait_ge(s_tp, PRIME + n + 1)
                        dve.wait_ge(s_o, PRIME + n - 1)
                        dve.tensor_copy(rt[q % 2][:], t_ps[q % 2][:]).then_inc(s_tc, 1)
                        if q > 0:
                            add(b - 1, 1 - i, q - 1)
                if second:
                    add(b - 1, 1 - i, NCH - 1)

            def add(b, i, q):
                if q == 0:
                    dve.wait_ge(s_x[i], 16 * (b // 2 + 1) if isinstance(b, int) else 8 * (b - i) + 16)
                dve.wait_ge(s_o, PRIME + NCH * b + q + 1)
                part = xr[i][:, 512 * q:512 * (q + 1)]
                dve.tensor_tensor(part, o_ps[q % 2][:], part, ALU.add).then_inc(s_oc, 1)

            images(dve, step)

        @block.tensor
        def _(pe):
            def turn(b, i, q):
                pe.wait_ge(s_tc, PRIME + NCH * b + q - 1)
                for m in range(4):
                    src = rows[i][:, 4 * (4 * q + m):4 * (4 * q + m) + 4, :].rearrange("p a k -> p (a k)")
                    ins = pe.transpose(t_ps[q % 2][:, m * 128:(m + 1) * 128], src, ident[:])
                ins.then_inc(s_tp, 1)

            def step(b, i, first, second):
                if first:
                    pe.wait_ge(s_in[i], 16 * (b // 2 + 1) if isinstance(b, int) else 8 * (b - i) + 16)
                if second:
                    pe.wait_ge(s_zc, PRIME + NCH * b)
                    turn(b - 1, 1 - i, 0)
                for q in range(NCH):
                    if second and q + 1 < NCH:
                        turn(b - 1, 1 - i, q + 1)
                    if first:
                        pe.wait_ge(s_zc, PRIME + NCH * b + q - 1)
                        for y in range(4):
                            ins = pe.matmul(z_ps[q % 2][:, 128 * y:128 * y + 128], yin[i][:, 4 * q + y, :], ih[:], start=True, stop=True)
                        ins.then_inc(s_z, 1)
                    if second:
                        pe.wait_ge(s_tc, PRIME + NCH * (b - 1) + q + 1)
                        pe.wait_ge(s_oc, PRIME + NCH * (b - 1) + q - 1)
                        for m in range(4):
                            ins = pe.matmul(o_ps[q % 2][:, 128 * m:128 * m + 128], rt[q % 2][:, 128 * m:128 * m + 128], iw[:], start=True, stop=True)
                        ins.then_inc(s_o, 1)

            pe.wait_ge(s_const, 48)
            images(pe, step)


def build(nc, B, x, woff, boff, wconv, wspec, c_colsel, c_rowsel, c_spread, c_patt, c_gsel, c_gpos, c_grow, c_group, c_ident,
          c_fw, c_fh, c_ih, c_iw, out):
    x1 = nc.dram_tensor("x1_scratch", [B, C, PIX], F32, kind="Internal").ap()
    with nc.sbuf_tensor("fint", [1, 1], I32) as fint:
        build_l0(nc, x, woff, boff, wconv, c_colsel, c_rowsel, c_spread, c_patt, c_group, c_ident, x1, fint, B)
        build_general(nc, fint, x, woff, boff, wconv, c_gsel, c_gpos, c_grow, c_group, c_ident, x1, B)
    build_l1(nc, x1, wspec, c_fw, c_fh, c_ih, c_iw, c_group, c_ident, out, B)


def kernel(x, L0_conv_offset_w, L0_conv_offset_b, L0_conv_weight,
           L1_conv_w1_real, L1_conv_w1_imag, L1_conv_w2_real, L1_conv_w2_imag):
    import concourse.bacc as bacc
    from concourse.bass_utils import run_bass_kernel_spmd

    B = x.shape[0]
    wspec = np.empty((KX, 2, C, KY, C), np.float32)
    for half, parts in enumerate(((L1_conv_w1_real, L1_conv_w1_imag), (L1_conv_w2_real, L1_conv_w2_imag))):
        for r, w in enumerate(parts):
            wspec[half * KX // 2:(half + 1) * KX // 2, r] = np.asarray(w).transpose(2, 0, 3, 1)
    arrays = {
        "x": np.ascontiguousarray(np.asarray(x).reshape(B, C, PIX)),
        "woff": np.ascontiguousarray(np.asarray(L0_conv_offset_w).transpose(1, 2, 3, 0).reshape(CG, TAPS, OMC)),
        "boff": np.ascontiguousarray(np.asarray(L0_conv_offset_b).reshape(OMC, 1)),
        "wconv": np.ascontiguousarray(np.asarray(L0_conv_weight).transpose(1, 2, 3, 0).reshape(C, TAPS, C)),
        "wspec": wspec,
        **constants_l0(), **constants_general(), **constants_l1(),
    }
    nc = bacc.Bacc("TRN2", target_bir_lowering=False, num_devices=1)
    aps = {n: nc.dram_tensor(n, a.shape, mybir.dt.from_np(a.dtype), kind="ExternalInput").ap() for n, a in arrays.items()}
    out = nc.dram_tensor("out", (B, C, PIX), F32, kind="ExternalOutput").ap()
    build(nc, B=B, out=out, **aps)
    r = run_bass_kernel_spmd(nc, [arrays], core_ids=[0])
    return r.results[0]["out"].reshape(B, C, H, W)
```
